# Optimizing a Trainium2 kernel written in Bass

```python
import numpy as np
import jax
import jax.numpy as jnp

def _softmax(x, axis=-1):
    return jax.nn.softmax(x, axis=axis)

def _gelu(x):
    return jax.nn.gelu(x, approximate=True)

def _silu(x):
    return jax.nn.silu(x)

def _sigmoid(x):
    return jax.nn.sigmoid(x)

def _layernorm(x, axis=-1, eps=1e-05):
    m = jnp.mean(x, axis=axis, keepdims=True)
    v = jnp.var(x, axis=axis, keepdims=True)
    return (x - m) / jnp.sqrt(v + eps)

def _scatter_add(tgt, idx, src, axis=0):
    return tgt.at[idx].add(src)

def _segment_sum(src, seg, n):
    return jax.ops.segment_sum(src, seg, n)
kernel_name = 'mk_seq_preln_d1_jaxref_r4_954d26'

def setup_inputs(seed: int=0):
    np.random.seed(seed)
    _w = jnp.asarray

    def _L0_attn_setup():
        import jax, jax.numpy as jnp
        import numpy as np
        D = 256
        HS = 128
        NKV = 2

        def apply_rope(x):
            d = x.shape[-1]
            T = x.shape[-2]
            positions = jnp.arange(0, d, 2, dtype=jnp.float32)
            theta = 10000.0 ** (-2.0 * positions / d)
            angles = jnp.arange(T, dtype=jnp.float32)[:, None] * theta[None, :]
            cos, sin = (jnp.cos(angles), jnp.sin(angles))
            xr = x.reshape(x.shape[:-1] + (d // 2, 2))
            out = jnp.stack([xr[..., 0] * cos - xr[..., 1] * sin, xr[..., 1] * cos + xr[..., 0] * sin], axis=-1)
            return out.reshape(x.shape)
        key = jax.random.key(seed)
        k1, k2, k3, k4, k5 = jax.random.split(key, 5)
        B, T = (4, 512)
        x = jax.random.normal(k1, (B, T, D), dtype=jnp.float32)
        s = 1.0 / np.sqrt(D)
        Wq = jax.random.normal(k2, (NKV, HS, D), dtype=jnp.float32) * s
        Wk = jax.random.normal(k3, (HS, D), dtype=jnp.float32) * s
        Wv = jax.random.normal(k4, (HS, D), dtype=jnp.float32) * s
        Wo = jax.random.normal(k5, (D, NKV * HS), dtype=jnp.float32) * (1.0 / np.sqrt(NKV * HS))
        return {'x': x, 'Wq': Wq, 'Wk': Wk, 'Wv': Wv, 'Wo': Wo}
    _L0_attn_in = _L0_attn_setup()

    def _L0_ffn_setup():
        import jax, jax.numpy as jnp
        import numpy as np
        B, S, DIM = (4, 1024, 256)
        BASE_COUPLING = 0.1
        NUM_CYCLES = 3

        def _gelu(x):
            return jax.nn.gelu(x, approximate=False)

        def _coupling_net(h, w1, b1, w2, b2, w3, b3, w4, b4):
            h = _gelu(h @ w1 + b1)
            h = _gelu(h @ w2 + b2)
            h = _gelu(h @ w3 + b3)
            return jax.nn.sigmoid(h @ w4 + b4)

        def _global_net(h, w1, b1, w2, b2, w3, b3):
            h = _gelu(h @ w1 + b1)
            h = _gelu(h @ w2 + b2)
            return jax.nn.sigmoid(h @ w3 + b3)

        def _twist(x):
            o_r, o_i, p_r, p_i = jnp.split(x, 4, axis=-1)
            return jnp.concatenate([p_r, -p_i, -o_r, o_i], axis=-1)
        key = jax.random.key(seed)
        ks = jax.random.split(key, 9)
        d = DIM

        def w(k, fan_in, fan_out):
            return jax.random.normal(k, (fan_in, fan_out), dtype=jnp.float32) / np.sqrt(fan_in).astype(np.float32)
        inp = {'x': jax.random.normal(ks[0], (B, S, d), dtype=jnp.float32)}
        cn_dims = [(d, d), (d, d // 2), (d // 2, d // 4), (d // 4, 1)]
        for i, (a, b) in enumerate(cn_dims):
            inp[f'cn_w{i + 1}'] = w(ks[1 + i], a, b)
            inp[f'cn_b{i + 1}'] = jnp.zeros((b,), dtype=jnp.float32)
        gc_dims = [(d, d // 2), (d // 2, d // 4), (d // 4, 1)]
        for i, (a, b) in enumerate(gc_dims):
            inp[f'gc_w{i + 1}'] = w(ks[5 + i], a, b)
            inp[f'gc_b{i + 1}'] = jnp.zeros((b,), dtype=jnp.float32)
        inp['adaptive_range'] = jnp.full((1,), 0.2, dtype=jnp.float32)
        return inp
    _L0_ffn_in = _L0_ffn_setup()
    _d = {'L0_attn_x': _L0_attn_in['x'], 'L0_attn_Wq': _L0_attn_in['Wq'], 'L0_attn_Wk': _L0_attn_in['Wk'], 'L0_attn_Wv': _L0_attn_in['Wv'], 'L0_attn_Wo': _L0_attn_in['Wo'], 'L0_ffn_cn_w1': _L0_ffn_in['cn_w1'], 'L0_ffn_cn_b1': _L0_ffn_in['cn_b1'], 'L0_ffn_cn_w2': _L0_ffn_in['cn_w2'], 'L0_ffn_cn_b2': _L0_ffn_in['cn_b2'], 'L0_ffn_cn_w3': _L0_ffn_in['cn_w3'], 'L0_ffn_cn_b3': _L0_ffn_in['cn_b3'], 'L0_ffn_cn_w4': _L0_ffn_in['cn_w4'], 'L0_ffn_cn_b4': _L0_ffn_in['cn_b4'], 'L0_ffn_gc_w1': _L0_ffn_in['gc_w1'], 'L0_ffn_gc_b1': _L0_ffn_in['gc_b1'], 'L0_ffn_gc_w2': _L0_ffn_in['gc_w2'], 'L0_ffn_gc_b2': _L0_ffn_in['gc_b2'], 'L0_ffn_gc_w3': _L0_ffn_in['gc_w3'], 'L0_ffn_gc_b3': _L0_ffn_in['gc_b3'], 'L0_ffn_adaptive_range': _L0_ffn_in['adaptive_range']}
    _x0 = _d['L0_attn_x']
    _d['L0_attn_x'] = jax.random.normal(jax.random.fold_in(jax.random.key(seed), 1), (8, 1024, 256), dtype=_x0.dtype)
    del _x0
    return _d

def reference(L0_attn_x, L0_attn_Wq, L0_attn_Wk, L0_attn_Wv, L0_attn_Wo, L0_ffn_cn_w1, L0_ffn_cn_b1, L0_ffn_cn_w2, L0_ffn_cn_b2, L0_ffn_cn_w3, L0_ffn_cn_b3, L0_ffn_cn_w4, L0_ffn_cn_b4, L0_ffn_gc_w1, L0_ffn_gc_b1, L0_ffn_gc_w2, L0_ffn_gc_b2, L0_ffn_gc_w3, L0_ffn_gc_b3, L0_ffn_adaptive_range):

    def _L0_attn_ref(x, Wq, Wk, Wv, Wo):
        import jax, jax.numpy as jnp
        import numpy as np
        D = 256
        HS = 128
        NKV = 2

        def apply_rope(x):
            d = x.shape[-1]
            T = x.shape[-2]
            positions = jnp.arange(0, d, 2, dtype=jnp.float32)
            theta = 10000.0 ** (-2.0 * positions / d)
            angles = jnp.arange(T, dtype=jnp.float32)[:, None] * theta[None, :]
            cos, sin = (jnp.cos(angles), jnp.sin(angles))
            xr = x.reshape(x.shape[:-1] + (d // 2, 2))
            out = jnp.stack([xr[..., 0] * cos - xr[..., 1] * sin, xr[..., 1] * cos + xr[..., 0] * sin], axis=-1)
            return out.reshape(x.shape)
        B, T, _ = x.shape
        k = apply_rope(x @ Wk.T)
        v = x @ Wv.T
        q = jnp.einsum('btd,hkd->bhtk', x, Wq)
        q = apply_rope(q)
        scale = HS ** (-0.5)
        scores = jnp.einsum('bhtk,bsk->bhts', q, k) * scale
        causal = jnp.tril(jnp.ones((T, T), dtype=bool))
        scores = jnp.where(causal, scores, -jnp.inf)
        w = jax.nn.softmax(scores, axis=-1)
        out = jnp.einsum('bhts,bsk->bhtk', w, v)
        out = out.transpose(0, 2, 1, 3).reshape(B, T, NKV * HS)
        return out @ Wo.T

    def _L0_ffn_ref(x, cn_w1, cn_b1, cn_w2, cn_b2, cn_w3, cn_b3, cn_w4, cn_b4, gc_w1, gc_b1, gc_w2, gc_b2, gc_w3, gc_b3, adaptive_range):
        import jax, jax.numpy as jnp
        import numpy as np
        B, S, DIM = (4, 1024, 256)
        BASE_COUPLING = 0.1
        NUM_CYCLES = 3

        def _gelu(x):
            return jax.nn.gelu(x, approximate=False)

        def _coupling_net(h, w1, b1, w2, b2, w3, b3, w4, b4):
            h = _gelu(h @ w1 + b1)
            h = _gelu(h @ w2 + b2)
            h = _gelu(h @ w3 + b3)
            return jax.nn.sigmoid(h @ w4 + b4)

        def _global_net(h, w1, b1, w2, b2, w3, b3):
            h = _gelu(h @ w1 + b1)
            h = _gelu(h @ w2 + b2)
            return jax.nn.sigmoid(h @ w3 + b3)

        def _twist(x):
            o_r, o_i, p_r, p_i = jnp.split(x, 4, axis=-1)
            return jnp.concatenate([p_r, -p_i, -o_r, o_i], axis=-1)
        global_context = x.mean(axis=1, keepdims=True)
        gf = _global_net(global_context, gc_w1, gc_b1, gc_w2, gc_b2, gc_w3, gc_b3)
        out = x
        for _ in range(NUM_CYCLES):
            tf = _coupling_net(out, cn_w1, cn_b1, cn_w2, cn_b2, cn_w3, cn_b3, cn_w4, cn_b4)
            combined = 0.7 * gf + 0.3 * tf
            coupling = BASE_COUPLING + adaptive_range * (combined - 0.5) * 2.0
            out = out + coupling * _twist(out)
        return out
    x = L0_attn_x
    x = x + _L0_attn_ref(_layernorm(x, axis=-1), L0_attn_Wq, L0_attn_Wk, L0_attn_Wv, L0_attn_Wo)
    x = x + _L0_ffn_ref(_layernorm(x, axis=-1), L0_ffn_cn_w1, L0_ffn_cn_b1, L0_ffn_cn_w2, L0_ffn_cn_b2, L0_ffn_cn_w3, L0_ffn_cn_b3, L0_ffn_cn_w4, L0_ffn_cn_b4, L0_ffn_gc_w1, L0_ffn_gc_b1, L0_ffn_gc_w2, L0_ffn_gc_b2, L0_ffn_gc_w3, L0_ffn_gc_b3, L0_ffn_adaptive_range)
    return x

_drawn_inputs = setup_inputs


def setup_inputs(seed=0):
    import zlib

    import numpy as np

    out = dict(_drawn_inputs(seed))
    spreads = {'L0_ffn_cn_b1': (0.0, 2.0),
     'L0_ffn_cn_b2': (0.0, 2.0),
     'L0_ffn_cn_b3': (0.0, 2.0),
     'L0_ffn_gc_b1': (0.0, 0.8),
     'L0_ffn_gc_b2': (0.0, 0.8)}
    factors = {'L0_ffn_cn_w1': 7.431,
     'L0_ffn_cn_w2': 7.684,
     'L0_ffn_cn_w3': 6.147,
     'L0_ffn_cn_w4': 6.976,
     'L0_ffn_gc_w1': 8.0,
     'L0_ffn_gc_w2': 8.0,
     'L0_ffn_gc_w3': 6.497}
    for name, (base, spread) in spreads.items():
        noise = np.random.default_rng([zlib.crc32(name.encode()), seed]).standard_normal(out[name].shape)
        drawn = base * np.exp(spread * noise) if base else spread * noise
        out[name] = jnp.asarray(drawn.astype(out[name].dtype))
    for name, factor in factors.items():
        out[name] = (out[name] * factor).astype(out[name].dtype)
    return out
```

```python
from contextlib import ExitStack

import concourse.bass as bass
from concourse import mybir

F32 = mybir.dt.float32
F32R = mybir.dt.float32r
BF16 = mybir.dt.bfloat16
ALU = mybir.AluOpType
ACT = mybir.ActivationFunctionType
AX_X = mybir.AxisListType.X

P = 128
B, T, D = 8, 1024, 256
HS, NH = 128, 2
TILES = T // P
G = 4
GROUPS = TILES // G
DC = D // P
EPS = 1e-5
MASKED = -1e30
HALF = HS // 2

UNITS = [(g, h) for g in range(GROUPS) for h in range(NH)]
STEPS = [G * (g + 1) for g, h in UNITS]
FIRST_STEP = [sum(STEPS[:u]) for u in range(len(UNITS))]
BATCH_STEPS = sum(STEPS)
BATCH_SCORES = len(UNITS) * G


def at_least(engine, semaphore, value):
    if isinstance(value, int) and value <= 0:
        return
    engine.wait_ge(semaphore, value)


def spread(*parts):
    keyed = [((n + 0.5) / len(part), which, n, step)
             for which, part in enumerate(parts) for n, step in enumerate(part)]
    return [step for _, _, _, step in sorted(keyed, key=lambda x: x[:3])]


def front_steps(ahead, g):
    return ([("scale", ahead, g)] + [("turn_x", ahead, g, c) for c in range(DC)]
            + [("project", ahead, g, t) for t in range(G)]
            + [("turn_qk", ahead, g, c) for c in range(NH + 1)])


def batch_order(first, last):
    def scores(u):
        return [("scores", 0, u, k) for k in range(G)]

    def attend(ahead, u):
        return [("attend", ahead, u, j) for j in range(STEPS[u])] + [("close", ahead, u)]

    def output(ahead, g):
        return [("output", ahead, g, t) for t in range(G)]

    late = front_steps(0, 1)
    early = front_steps(1, 0)
    order = spread(scores(0), [] if first else attend(-1, 3), late[:5])
    order += spread(scores(1), attend(0, 0), [] if first else output(-1, 1), late[5:])
    order += [] if last else [("norm", 1, 0)]
    order += spread(scores(2), attend(0, 1), [] if last else early[:3])
    order += spread(scores(3), attend(0, 2), output(0, 0), [] if last else early[3:])
    return order + ([] if last else [("norm", 1, 1)])


PROLOGUE = [("norm", 0, 0)] + front_steps(0, 0) + [("norm", 0, 1)]
FIRST_BATCH = batch_order(True, False)
MIDDLE_BATCH = batch_order(False, False)
LAST_BATCH = batch_order(False, True)
EPILOGUE = ([("attend", -1, 3, j) for j in range(STEPS[3])] + [("close", -1, 3)]
            + [("output", -1, 1, t) for t in range(G)])


def walk(engine, do):
    do(PROLOGUE, 0, 0, 0)
    do(FIRST_BATCH, 0, 0, 0)
    with engine.Fori(0, (B - 2) // 2) as pair:
        do(MIDDLE_BATCH, pair * 2 + 1, pair, 1)
        do(MIDDLE_BATCH, pair * 2 + 2, pair + 1, 0)
    do(LAST_BATCH, B - 1, (B - 1) // 2, (B - 1) % 2)
    do(EPILOGUE, B, B // 2, B % 2)


def attention_phase(nc, x, wqkv, wo, cos_t, sin_t, x2):
    x_view = x.rearrange("b (i p) f -> b p i f", p=P)
    x2_view = x2.rearrange("b (i p) f -> b p i f", p=P)
    with ExitStack() as ctx:
        def sb(name, shape, dt=F32):
            return ctx.enter_context(nc.sbuf_tensor(name, shape, dt))

        def psum(name, shape):
            return ctx.enter_context(nc.psum_tensor(name, shape, F32))

        def sem(name):
            return ctx.enter_context(nc.semaphore(name))

        ident = sb("ident", [P, P])
        ident_b = sb("ident_b", [P, P], BF16)
        mask_b = sb("mask_b", [P, P], BF16)
        minus_half = sb("minus_half", [P, 1])
        wqkv_f = sb("wqkv_f", [P, DC, 4 * HS])
        wqkv_hi = sb("wqkv_hi", [P, DC, 4 * HS], F32R)
        wqkv_lo = sb("wqkv_lo", [P, DC, 4 * HS], F32R)
        wo_f = sb("wo_f", [P, NH, D])
        wo_hi = sb("wo_hi", [P, NH, D], F32R)
        wo_lo = sb("wo_lo", [P, NH, D], F32R)
        cos_sb = sb("cos_sb", [P, TILES, HALF])
        sin_sb = sb("sin_sb", [P, TILES, HS])
        xt = [sb(f"xt{n}", [P, TILES, D]) for n in range(2)]
        stats = sb("stats", [P, G, 6])
        moments = [sb(f"moments{n}", [P, G, 2]) for n in range(GROUPS)]
        var_eps = [sb(f"var_eps{n}", [P, G]) for n in range(GROUPS)]
        rstd = [sb(f"rstd{n}", [P, G]) for n in range(GROUPS)]
        xn = [sb(f"xn{n}", [P, G, D]) for n in range(GROUPS)]
        xnT_hi = sb("xnT_hi", [P, DC, G * P], F32R)
        xnT_lo = sb("xnT_lo", [P, DC, G * P], F32R)
        qkv = [sb(f"qkv{t}", [P, 4 * HS]) for t in range(G)]
        rope_a = sb("rope_a", [P, 3 * HS])
        rope_b = sb("rope_b", [P, 3 * HS])
        rot = sb("rot", [P, G, 3 * HS])
        q_hi = [[sb(f"q_hi{g}{h}", [P, G * P], F32R) for h in range(NH)] for g in range(GROUPS)]
        q_lo = [[sb(f"q_lo{g}{h}", [P, G * P], F32R) for h in range(NH)] for g in range(GROUPS)]
        k_hi = [sb(f"k_hi{n}", [P, T], F32R) for n in range(2)]
        k_lo = [sb(f"k_lo{n}", [P, T], F32R) for n in range(2)]
        v_hi = [sb(f"v_hi{n}", [P, TILES, HS], F32R) for n in range(2)]
        v_lo = [sb(f"v_lo{n}", [P, TILES, HS], F32R) for n in range(2)]
        neg_max = sb("neg_max", [P, BATCH_SCORES])
        row_sum = [sb(f"row_sum{n}", [P, BATCH_SCORES]) for n in range(2)]
        inv_sum = sb("inv_sum", [P, NH * G])
        probs = [sb(f"probs{n}", [P, G, T]) for n in range(2)]
        PT_RING = 3
        pT_hi = [sb(f"pT_hi{n}", [P, G * P], F32R) for n in range(PT_RING)]
        pT_lo = [sb(f"pT_lo{n}", [P, G * P], F32R) for n in range(PT_RING)]
        oT_hi = [sb(f"oT_hi{h}", [P, G * P], F32R) for h in range(NH)]
        oT_lo = [sb(f"oT_lo{h}", [P, G * P], F32R) for h in range(NH)]
        x_plus = sb("x_plus", [P, D])

        scores_ps = [psum(f"scores_ps{n}", [P, T]) for n in range(2)]
        pT_ps = [psum(f"pT_ps{n}", [P, G * P]) for n in range(2)]
        oT_ps = psum("oT_ps", [P, G * P])
        front_ps = psum("front_ps", [P, G * P])

        x_loaded = [sem(f"x_loaded{n}") for n in range(2)]
        w_loaded = sem("w_loaded")
        x2_stored = [sem(f"x2_stored{n}") for n in range(2)]
        zeroed = sem("zeroed")
        consts_ready = sem("consts_ready")
        w_hi_ready = sem("w_hi_ready")
        w_ready = sem("w_ready")
        moments_ready = sem("moments_ready")
        var_ready = sem("var_ready")
        rstd_ready = sem("rstd_ready")
        xn_ready = sem("xn_ready")
        x_turned = sem("x_turned")
        xT_hi_ready = sem("xT_hi_ready")
        xT_ready = sem("xT_ready")
        projected = sem("projected")
        qkv_ready = sem("qkv_ready")
        v_hi_ready = sem("v_hi_ready")
        v_ready = sem("v_ready")
        rope_products = sem("rope_products")
        rot_ready = sem("rot_ready")
        qk_turned = sem("qk_turned")
        qk_hi_ready = sem("qk_hi_ready")
        qk_ready = sem("qk_ready")
        scores_done = sem("scores_done")
        max_ready = sem("max_ready")
        probs_ready = sem("probs_ready")
        p_turned = sem("p_turned")
        pT_hi_ready = sem("pT_hi_ready")
        pT_ready = sem("pT_ready")
        attended = sem("attended")
        oT_hi_ready = sem("oT_hi_ready")
        oT_ready = sem("oT_ready")
        inv_ready = sem("inv_ready")
        output_done = sem("output_done")
        x_plus_ready = sem("x_plus_ready")
        x2_ready = sem("x2_ready")

        block = ctx.enter_context(nc.Block())

        @block.sync
        def _(sp):
            sp.dma_start(xt[0][:], x_view[0]).then_inc(x_loaded[0], 16)
            for dst, src in ((wqkv_f, wqkv.rearrange("(c p) n -> p c n", p=P)),
                             (cos_sb, cos_t.rearrange("(i p) n -> p i n", p=P)),
                             (sin_sb, sin_t.rearrange("(i p) n -> p i n", p=P)),
                             (wo_f, wo.rearrange("(c p) n -> p c n", p=P))):
                sp.dma_start(dst[:], src).then_inc(w_loaded, 16)
            sp.dma_start(xt[1][:], x_view[1]).then_inc(x_loaded[1], 16)

            def do(order, b, half, parity):
                for kind, ahead, *rest in order:
                    if kind != "output" or rest[1] != G - 1:
                        continue
                    g, bb, n = rest[0], b + ahead, (parity + ahead) % 2
                    turn = half + (parity + ahead) // 2
                    sp.wait_ge(x2_ready, bb * TILES + G * (g + 1))
                    sp.dma_start(x2_view[bb, :, G * g:G * (g + 1), :],
                                 xt[n][:, G * g:G * (g + 1), :]).then_inc(x2_stored[n], 16)
                    if g == GROUPS - 1 and not (isinstance(bb, int) and bb + 2 >= B):
                        sp.wait_ge(x2_stored[n], turn * (16 * GROUPS) + 16 * GROUPS)
                        sp.dma_start(xt[n][:], x_view[bb + 2]).then_inc(x_loaded[n], 16)

            walk(sp, do)
            for n in range(2):
                sp.wait_ge(x2_stored[n], 16 * GROUPS * B // 2)

        @block.gpsimd
        def _(pool):
            pool.memset(ident[:], 0.0).then_inc(zeroed, 1)
            pool.memset(ident_b[:], 0.0).then_inc(zeroed, 1)
            pool.memset(mask_b[:], 0.0).then_inc(zeroed, 1)
            pool.memset(minus_half[:], -0.5).then_inc(zeroed, 1)
            pool.wait_ge(zeroed, 4)
            for m in (ident, ident_b):
                pool.affine_select(out=m[:], in_=m[:], compare_op=ALU.not_equal, fill=1.0, base=0,
                                   pattern=[[-1, P]], channel_multiplier=1).then_inc(consts_ready, 1)
            pool.affine_select(out=mask_b[:], in_=mask_b[:], compare_op=ALU.is_ge, fill=MASKED,
                               base=0, pattern=[[-1, P]],
                               channel_multiplier=1).then_inc(consts_ready, 1)
            pool.wait_ge(w_loaded, 64)

            def do(order, b, half, parity):
                for kind, ahead, *rest in order:
                    bb, n = b + ahead, (parity + ahead) % 2
                    if kind == "norm":
                        g, = rest
                        group = bb * GROUPS + g
                        pool.wait_ge(var_ready, group + 1)
                        pool.tensor_tensor(rstd[g][:], var_eps[g][:],
                                           minus_half[:].to_broadcast([P, G]),
                                           ALU.pow).then_inc(rstd_ready, 1)
                    if kind == "project":
                        g, t = rest
                        i = G * g + t
                        tile = bb * TILES + i
                        pool.wait_ge(qkv_ready, tile + 1)
                        v = qkv[t][:, 3 * HS:4 * HS]
                        at_least(pool, rot_ready, tile)
                        qk = qkv[t][:, 0:3 * HS].rearrange("p (c e d) -> p c e d", e=2, d=HALF)
                        cos = cos_sb[:, i, :].unsqueeze(1).broadcast_to([P, 2 * (NH + 1), HALF])
                        sin = sin_sb[:, i, :].unsqueeze(1).broadcast_to([P, NH + 1, HS])
                        pool.tensor_tensor(
                            rope_a[:].rearrange("p (c d) -> p c d", d=HALF),
                            qkv[t][:, 0:3 * HS].rearrange("p (c d) -> p c d", d=HALF),
                            cos, ALU.mult).then_inc(rope_products, 1)
                        pool.tensor_tensor(
                            rope_b[:].rearrange("p (c e d) -> p c e d", e=2, d=HALF),
                            qk[:, :, ::-1, :],
                            sin.rearrange("p c (e d) -> p c e d", e=2),
                            ALU.mult).then_inc(rope_products, 1)
                        pool.wait_ge(v_hi_ready, tile + 1)
                        pool.tensor_tensor(v_lo[n][:, i, :], v, v_hi[n][:, i, :].bitcast(F32),
                                           ALU.subtract).then_inc(v_ready, 1)
                        pool.wait_ge(rope_products, (tile + 1) * 2)
                        at_least(pool, qk_turned, (bb * GROUPS + g) * (NH + 1))
                        pool.tensor_tensor(rot[:, t, :], rope_a[:], rope_b[:],
                                           ALU.add).then_inc(rot_ready, 1)

            walk(pool, do)

        @block.scalar
        def _(act):
            def copy(out, in_):
                return nc.scalar.activation(out, in_, ACT.Copy)

            def do(order, b, half, parity):
                for kind, ahead, *rest in order:
                    bb, n = b + ahead, (parity + ahead) % 2
                    if kind == "turn_x":
                        g, c = rest
                        group = bb * GROUPS + g
                        act.wait_ge(x_turned, group * DC + c + 1)
                        at_least(act, projected, group * G)
                        copy(xnT_hi[:, c, :], front_ps[:]).then_inc(xT_hi_ready, 1)
                    if kind == "project":
                        g, t = rest
                        tile = bb * TILES + G * g + t
                        act.wait_ge(projected, tile + 1)
                        at_least(act, rot_ready, tile - G + 1)
                        at_least(act, v_ready, tile - G + 1)
                        copy(qkv[t][:], front_ps[:]).then_inc(qkv_ready, 1)
                    if kind == "turn_qk":
                        g, c = rest
                        group = bb * GROUPS + g
                        act.wait_ge(qk_turned, group * (NH + 1) + c + 1)
                        at_least(act, scores_done,
                                 (bb - 1) * BATCH_SCORES + NH * G * (g + 1))
                        out = q_hi[g][c][:] if c < NH else k_hi[n][:, g * G * P:(g + 1) * G * P]
                        copy(out, front_ps[:]).then_inc(qk_hi_ready, 1)
                    if kind == "scores":
                        u, k = rest
                        g, h = UNITS[u]
                        keys = (G * g + k + 1) * P
                        s = bb * BATCH_SCORES + u * G + k
                        act.wait_ge(max_ready, s + 1)
                        if k == 0:
                            before = (u - 2) % len(UNITS)
                            at_least(act, p_turned, (bb - (u < 2)) * BATCH_STEPS
                                     + FIRST_STEP[before] + STEPS[before])
                        nc.scalar.activation(probs[u % 2][:, k, 0:keys], scores_ps[k % 2][:, 0:keys],
                                             ACT.Exp, bias=neg_max[:, u * G + k:u * G + k + 1],
                                             accum_out=row_sum[n][:, u * G + k:u * G + k + 1]
                                             ).then_inc(probs_ready, 1)
                    if kind == "attend":
                        u, j = rest
                        m = bb * BATCH_STEPS + FIRST_STEP[u] + j
                        skip = max(0, j - G * UNITS[u][0]) * P
                        r = (FIRST_STEP[u] + j) % PT_RING
                        act.wait_ge(p_turned, m + 1)
                        at_least(act, attended, m - PT_RING + 1)
                        copy(pT_hi[r][:, skip:], pT_ps[m_parity(u, j)][:, skip:]).then_inc(pT_hi_ready, 1)
                    if kind == "close":
                        u, = rest
                        g, h = UNITS[u]
                        act.wait_ge(attended, bb * BATCH_STEPS + FIRST_STEP[u] + STEPS[u])
                        at_least(act, output_done, bb * TILES + G * g)
                        copy(oT_hi[h][:], oT_ps[:]).then_inc(oT_hi_ready, 1)

            walk(act, do)

        @block.vector
        def _(dve):
            dve.wait_ge(w_loaded, 64)
            for hi, f in ((wqkv_hi, wqkv_f), (wo_hi, wo_f)):
                dve.tensor_copy(hi[:], f[:]).then_inc(w_hi_ready, 1)
            dve.wait_ge(w_hi_ready, 2)
            for lo, f, hi in ((wqkv_lo, wqkv_f, wqkv_hi), (wo_lo, wo_f, wo_hi)):
                dve.tensor_tensor(lo[:], f[:], hi[:].bitcast(F32), ALU.subtract).then_inc(w_ready, 1)

            def low(out, whole, hi):
                return dve.tensor_tensor(out, whole, hi.bitcast(F32), ALU.subtract)

            def do(order, b, half, parity):
                for kind, ahead, *rest in order:
                    bb, n = b + ahead, (parity + ahead) % 2
                    if kind == "norm":
                        g, = rest
                        group = bb * GROUPS + g
                        turn = half + (parity + ahead) // 2
                        dve.wait_ge(x_loaded[n], turn * 16 + 16)
                        at_least(dve, moments_ready, group * G)
                        at_least(dve, xn_ready, (group - GROUPS + 1) * G)
                        for t in range(G):
                            dve.bn_stats(stats[:, t, :], xt[n][:, G * g + t, :])
                        dve.drain()
                        for t in range(G):
                            dve.bn_aggr(moments[g][:, t, :], stats[:, t, :]).then_inc(moments_ready, 1)
                        dve.wait_ge(moments_ready, (group + 1) * G)
                        dve.tensor_scalar(var_eps[g][:], moments[g][:, :, 1], EPS, None,
                                          ALU.add).then_inc(var_ready, 1)
                    if kind == "scale":
                        g, = rest
                        group = bb * GROUPS + g
                        dve.wait_ge(rstd_ready, group + 1)
                        at_least(dve, x_turned, (group - GROUPS + 1) * DC)
                        for t in range(G):
                            dve.tensor_scalar(xn[g][:, t, :], xt[n][:, G * g + t, :],
                                              moments[g][:, t, 0:1], rstd[g][:, t:t + 1],
                                              ALU.subtract, ALU.mult).then_inc(xn_ready, 1)
                    if kind == "turn_x":
                        g, c = rest
                        dve.wait_ge(xT_hi_ready, (bb * GROUPS + g) * DC + c + 1)
                        low(xnT_lo[:, c, :], front_ps[:], xnT_hi[:, c, :]).then_inc(xT_ready, 1)
                    if kind == "project":
                        g, t = rest
                        i = G * g + t
                        dve.wait_ge(qkv_ready, bb * TILES + i + 1)
                        dve.tensor_copy(v_hi[n][:, i, :], qkv[t][:, 3 * HS:]).then_inc(v_hi_ready, 1)
                    if kind == "turn_qk":
                        g, c = rest
                        dve.wait_ge(qk_hi_ready, (bb * GROUPS + g) * (NH + 1) + c + 1)
                        cols = slice(g * G * P, (g + 1) * G * P)
                        lo, hi = ((q_lo[g][c][:], q_hi[g][c][:]) if c < NH
                                  else (k_lo[n][:, cols], k_hi[n][:, cols]))
                        low(lo, front_ps[:], hi).then_inc(qk_ready, 1)
                    if kind == "scores":
                        u, k = rest
                        keys = (G * UNITS[u][0] + k + 1) * P
                        dve.wait_ge(scores_done, bb * BATCH_SCORES + u * G + k + 1)
                        dve.tensor_reduce(neg_max[:, u * G + k:u * G + k + 1],
                                          scores_ps[k % 2][:, 0:keys], AX_X, ALU.max,
                                          negate=True).then_inc(max_ready, 1)
                    if kind == "attend":
                        u, j = rest
                        m = bb * BATCH_STEPS + FIRST_STEP[u] + j
                        skip = max(0, j - G * UNITS[u][0]) * P
                        r = (FIRST_STEP[u] + j) % PT_RING
                        dve.wait_ge(pT_hi_ready, m + 1)
                        low(pT_lo[r][:, skip:], pT_ps[m_parity(u, j)][:, skip:],
                            pT_hi[r][:, skip:]).then_inc(pT_ready, 1)
                    if kind == "close":
                        u, = rest
                        h = UNITS[u][1]
                        dve.wait_ge(oT_hi_ready, bb * len(UNITS) + u + 1)
                        low(oT_lo[h][:], oT_ps[:], oT_hi[h][:]).then_inc(oT_ready, 1)
                    if kind == "output":
                        g, t = rest
                        i = G * g + t
                        tile = bb * TILES + i
                        if t == 0:
                            dve.wait_ge(probs_ready, bb * BATCH_SCORES + NH * G * (g + 1))
                            at_least(dve, x2_ready, tile)
                            dve.reciprocal(inv_sum[:], row_sum[n][:, NH * G * g:NH * G * (g + 1)]
                                           ).then_inc(inv_ready, 1)
                            dve.wait_ge(inv_ready, bb * GROUPS + g + 1)
                        dve.wait_ge(output_done, tile + 1)
                        at_least(dve, x2_ready, tile)
                        dve.scalar_tensor_tensor(out=x_plus[:], in0=front_ps[:, 0:D],
                                                 scalar=inv_sum[:, t:t + 1], in1=xt[n][:, i, :],
                                                 op0=ALU.mult, op1=ALU.add).then_inc(x_plus_ready, 1)
                        dve.wait_ge(x_plus_ready, tile + 1)
                        dve.scalar_tensor_tensor(out=xt[n][:, i, :], in0=front_ps[:, D:2 * D],
                                                 scalar=inv_sum[:, G + t:G + t + 1], in1=x_plus[:],
                                                 op0=ALU.mult, op1=ALU.add).then_inc(x2_ready, 1)

            walk(dve, do)

        @block.tensor
        def _(pe):
            def split_product(out, stationary, moving, first=True, last=True):
                nc.tensor.matmul(out, stationary[0], moving[0], start=first, stop=False)
                nc.tensor.matmul(out, stationary[0], moving[1], start=False, stop=False)
                return nc.tensor.matmul(out, stationary[1], moving[0], start=False, stop=last)

            pe.wait_ge(consts_ready, 3)
            pe.wait_ge(w_ready, 2)
            front_reader = [None]

            def take_front():
                if front_reader[0] is not None:
                    pe.wait_ge(*front_reader[0])

            def do(order, b, half, parity):
                if order is MIDDLE_BATCH:
                    front_reader[0] = (qk_ready, (b * GROUPS + 1) * (NH + 1))
                for kind, ahead, *rest in order:
                    bb, n = b + ahead, (parity + ahead) % 2
                    if kind == "turn_x":
                        g, c = rest
                        group = bb * GROUPS + g
                        pe.wait_ge(xn_ready, (group + 1) * G)
                        take_front()
                        for t in range(G):
                            mm = nc.tensor.transpose(front_ps[:, t * P:(t + 1) * P],
                                                     xn[g][:, t, c * P:(c + 1) * P], ident[:])
                        mm.then_inc(x_turned, 1)
                        front_reader[0] = (xT_ready, group * DC + c + 1)
                    if kind == "project":
                        g, t = rest
                        tile = bb * TILES + G * g + t
                        pe.wait_ge(xT_ready, (bb * GROUPS + g + 1) * DC)
                        take_front()
                        for c in range(DC):
                            cols = slice(t * P, (t + 1) * P)
                            mm = split_product(front_ps[:], (xnT_hi[:, c, cols], xnT_lo[:, c, cols]),
                                               (wqkv_hi[:, c, :], wqkv_lo[:, c, :]),
                                               c == 0, c == DC - 1)
                        mm.then_inc(projected, 1)
                        front_reader[0] = (qkv_ready, tile + 1)
                    if kind == "turn_qk":
                        g, c = rest
                        group = bb * GROUPS + g
                        pe.wait_ge(rot_ready, (group + 1) * G)
                        take_front()
                        for t in range(G):
                            mm = nc.tensor.transpose(front_ps[:, t * P:(t + 1) * P],
                                                     rot[:, t, c * HS:(c + 1) * HS], ident[:])
                        mm.then_inc(qk_turned, 1)
                        front_reader[0] = (qk_ready, group * (NH + 1) + c + 1)
                    if kind == "scores":
                        u, k = rest
                        g, h = UNITS[u]
                        keys = (G * g + k + 1) * P
                        s = bb * BATCH_SCORES + u * G + k
                        pe.wait_ge(qk_ready, (bb * GROUPS + g + 1) * (NH + 1))
                        at_least(pe, probs_ready, s - 1)
                        tile = slice(k * P, (k + 1) * P)
                        ps = scores_ps[k % 2]
                        for at in range(0, keys, G * P):
                            cols = slice(at, min(at + G * P, keys))
                            mm = split_product(ps[:, cols], (q_hi[g][h][:, tile], q_lo[g][h][:, tile]),
                                               (k_hi[n][:, cols], k_lo[n][:, cols]),
                                               last=cols.stop < keys)
                        mm = nc.tensor.matmul(ps[:, keys - P:keys], ident_b[:], mask_b[:],
                                              start=False, stop=True)
                        mm.then_inc(scores_done, 1)
                    if kind == "attend":
                        u, j = rest
                        turn_p(bb, u, j)
                        if j > 0:
                            attend(bb, n, u, j - 1)
                    if kind == "close":
                        attend(bb, n, rest[0], STEPS[rest[0]] - 1)
                    if kind == "output":
                        g, t = rest
                        pe.wait_ge(oT_ready, bb * len(UNITS) + NH * (g + 1))
                        take_front()
                        for h in range(NH):
                            cols = slice(t * P, (t + 1) * P)
                            mm = split_product(front_ps[:, h * D:(h + 1) * D],
                                               (oT_hi[h][:, cols], oT_lo[h][:, cols]),
                                               (wo_hi[:, h, :], wo_lo[:, h, :]))
                        mm.then_inc(output_done, 1)
                        front_reader[0] = (x2_ready, bb * TILES + G * g + t + 1)

            def turn_p(bb, u, j):
                m = bb * BATCH_STEPS + FIRST_STEP[u] + j
                g = UNITS[u][0]
                pe.wait_ge(probs_ready, bb * BATCH_SCORES + (u + 1) * G)
                at_least(pe, pT_ready, m - 1)
                for k in range(max(0, j - G * g), G):
                    mm = nc.tensor.transpose(pT_ps[m_parity(u, j)][:, k * P:(k + 1) * P],
                                             probs[u % 2][:, k, j * P:(j + 1) * P], ident[:])
                mm.then_inc(p_turned, 1)

            def attend(bb, n, u, j):
                m = bb * BATCH_STEPS + FIRST_STEP[u] + j
                skip = max(0, j - G * UNITS[u][0]) * P
                r = (FIRST_STEP[u] + j) % PT_RING
                pe.wait_ge(pT_ready, m + 1)
                if j == 0:
                    at_least(pe, oT_ready, bb * len(UNITS) + u)
                    pe.wait_ge(v_ready, bb * TILES + STEPS[u])
                split_product(oT_ps[:, skip:], (v_hi[n][:, j, :], v_lo[n][:, j, :]),
                              (pT_hi[r][:, skip:], pT_lo[r][:, skip:]),
                              j == 0, j == STEPS[u] - 1).then_inc(attended, 1)

            walk(pe, do)


def m_parity(u, j):
    return (FIRST_STEP[u] + j) % 2


FFN_CYCLES = 3
H2, H3 = D // 2, D // 4
BLOCK = D // 4
NGROUPS = B * GROUPS
STAGES = 1 + FFN_CYCLES
SLOTS = 4

PERIOD = [
    ("spread", 2), ("spread", 1), ("gelu1", 0), ("turn", 0), ("turn", 1), ("mix", 2), ("h2", 0),
    ("mix", 1), ("stats",), ("product", 0), ("gelu1", 2), ("global", 0), ("h3", 0), ("h2", 2),
    ("gelu1", 1), ("product", 1), ("global", 1), ("dot", 0), ("h2", 1), ("h3", 2), ("product", 2),
    ("global", 2), ("squash", 0), ("dot", 2), ("h3", 1), ("squash", 2), ("final", 0), ("final", 1),
    ("product", 3), ("dot", 1), ("final", 2), ("squash", 1), ("final", 3), ("scale",),
]


def period_steps(n):
    for kind, *rest in PERIOD:
        if kind in ("turn", "product", "global"):
            ahead = 0
        elif kind in ("stats", "scale"):
            ahead = 1
        else:
            ahead = -FFN_CYCLES if kind == "final" else -1 - rest[0]
        if isinstance(n, int) and not 0 <= n + ahead < NGROUPS:
            continue
        yield kind, ahead, rest


def walk_periods(engine, do):
    for n in range(-1, SLOTS):
        do(n, n // SLOTS, n % SLOTS)
    with engine.Fori(1, NGROUPS // SLOTS - 1) as turn:
        for r in range(SLOTS):
            do(turn * SLOTS + r, turn, r)
    for n in range(NGROUPS - SLOTS, NGROUPS + FFN_CYCLES):
        do(n, n // SLOTS, n % SLOTS)


def batch_of(turn, r, ahead):
    return (turn + (r + ahead) // SLOTS) * (SLOTS // GROUPS) + (r + ahead) % SLOTS // GROUPS


def ffn_phase(nc, x2, w, out):
    x2_view = x2.rearrange("b (i p) f -> b p i f", p=P)
    out_view = out.rearrange("b (g i p) f -> (b g) p i f", p=P, g=GROUPS)
    with ExitStack() as ctx:
        def sb(name, shape, dt=F32):
            return ctx.enter_context(nc.sbuf_tensor(name, shape, dt))

        def psum(name, shape):
            return ctx.enter_context(nc.psum_tensor(name, shape, F32))

        def sem(name):
            return ctx.enter_context(nc.semaphore(name))

        def cycle_sems(name):
            return [sem(f"{name}{c}") for c in range(FFN_CYCLES)]

        ident = sb("f_ident", [P, P])
        minus_half = sb("f_minus_half", [P, 1])
        sign = sb("sign", [P, 2])
        ones = sb("ones", [1, P])
        ones_r = sb("ones_r", [1, P], F32R)
        w1_f = sb("w1_f", [P, DC, D])
        w1_hi = [sb(f"w1_hi{n}", [P, DC, D], F32R) for n in range(2)]
        w1_lo = [sb(f"w1_lo{n}", [P, DC, D], F32R) for n in range(2)]
        w2_sb = sb("w2_sb", [P, DC, H2])
        w3_sb = sb("w3_sb", [P, H3])
        w4_sb = sb("w4_sb", [P, H3])
        b1_sb = sb("b1_sb", [P, DC])
        b2_sb = sb("b2_sb", [P, 1])
        b3_f = sb("b3_f", [1, H3])
        b3_hi = sb("b3_hi", [1, H3], F32R)
        b3_lo = sb("b3_lo", [1, H3], F32R)
        b4_f = sb("b4_f", [P, 1])
        b4_half = sb("b4_half", [P, 1])
        gw1_sb = sb("gw1_sb", [P, DC, H2])
        gw2_sb = sb("gw2_sb", [P, H3])
        gw3_sb = sb("gw3_sb", [H3, 1])
        gb1_sb = sb("gb1_sb", [P, 1])
        gb2_sb = sb("gb2_sb", [H3, 1])
        gb3_f = sb("gb3_f", [P, 1])
        gb3_half = sb("gb3_half", [P, 1])
        range_f = sb("range_f", [P, 1])
        range_token = sb("range_token", [P, 1])
        range_global = sb("range_global", [P, 1])

        x_all = sb("x_all", [P, B * TILES, D])
        stats = sb("f_stats", [P, G, 6])
        moments = [sb(f"f_moments{n}", [P, G, 2]) for n in range(SLOTS)]
        var_eps = [sb(f"f_var_eps{n}", [P, G]) for n in range(SLOTS)]
        rstd = [sb(f"f_rstd{n}", [P, G]) for n in range(SLOTS)]
        x0 = [sb(f"x0_{n}", [P, G, D]) for n in range(SLOTS)]
        x0T_hi = sb("x0T_hi", [P, DC, G * P], F32R)
        x0T_lo = sb("x0T_lo", [P, DC, G * P], F32R)
        x0_sum = [sb(f"x0_sum{n}", [P, DC]) for n in range(SLOTS)]
        made = [sb(f"made{n}", [P, 2 * DC, G * P]) for n in range(SLOTS)]
        part_a = sb("part_a", [P, DC, G * P])
        part_b = [None] + [sb(f"part_b{c}", [P, DC, G * P]) for c in range(1, FFN_CYCLES)]
        mixed_sb = [None] + [sb(f"mixed{c}", [P, DC, G * P]) for c in range(1, FFN_CYCLES)]
        h1 = [sb(f"h1_{c}", [P, DC, G * P]) for c in range(FFN_CYCLES)]
        h2 = [sb(f"h2_{c}", [P, G * P]) for c in range(FFN_CYCLES)]
        h3 = [sb(f"h3_{c}", [P, G, H3]) for c in range(FFN_CYCLES)]
        h3_w4 = [sb(f"h3_w4_{c}", [P, G, H3]) for c in range(FFN_CYCLES)]
        logit = [sb(f"logit{c}", [P, G]) for c in range(FFN_CYCLES)]
        token_tanh = [sb(f"token_tanh{c}", [P, G]) for c in range(FFN_CYCLES)]
        coupling = [sb(f"coupling{c}", [P, G]) for c in range(FFN_CYCLES)]
        scaled = [sb(f"scaled{c}", [P, 2, G]) for c in range(FFN_CYCLES)]
        state = [[sb(f"state{c}_{n}", [P, 2, G]) for n in range(2)] for c in range(FFN_CYCLES)]
        minus_b = sb("minus_b", [P, G])
        gh1 = sb("gh1", [P, 1])
        gh2 = sb("gh2", [H3, 1])
        global_tanh = sb("global_tanh", [P, 1])
        base_coupling = [sb(f"base_coupling{n}", [P, 1]) for n in range(2)]
        y_part = sb("y_part", [P, D])

        made_ps = [psum(f"made_ps{n}", [P, G * P]) for n in range(3)]
        cycle_ps = [psum(f"cycle_ps{c}", [P, G * P]) for c in range(FFN_CYCLES)]
        spread_a_ps = psum("spread_a_ps", [P, G * P])
        global_ps = psum("global_ps", [P, G * P])

        f_loaded = sem("f_loaded")
        x2_loaded = [sem(f"x2_loaded{n}") for n in range(2)]
        f_zeroed = sem("f_zeroed")
        f_consts = sem("f_consts")
        f_hi = sem("f_hi")
        moments_ready = sem("f_moments_ready")
        var_ready = sem("f_var_ready")
        rstd_ready = sem("f_rstd_ready")
        x0_ready = sem("x0_ready")
        x0_turned = sem("x0_turned")
        x0T_hi_ready = sem("x0T_hi_ready")
        x0T_ready = sem("x0T_ready")
        made_done = sem("made_done")
        made_ready = sem("made_ready")
        global_done = sem("global_done")
        global_act = sem("global_act")
        base_ready = sem("base_ready")
        spread_done = cycle_sems("spread_done")
        parts_ready = cycle_sems("parts_ready")
        mix_ready = cycle_sems("mix_ready")
        h1_ready = cycle_sems("h1_ready")
        h2_done = cycle_sems("h2_done")
        h2_ready = cycle_sems("h2_ready")
        h3_done = cycle_sems("h3_done")
        h3_ready = cycle_sems("h3_ready")
        h3_w4_ready = cycle_sems("h3_w4_ready")
        logit_ready = cycle_sems("logit_ready")
        tanh_ready = cycle_sems("tanh_ready")
        coupling_ready = cycle_sems("coupling_ready")
        scaled_ready = cycle_sems("scaled_ready")
        state_ready = cycle_sems("state_ready")
        minus_b_ready = sem("minus_b_ready")
        y_part_ready = sem("y_part_ready")
        y_ready = sem("y_ready")
        y_stored = sem("y_stored")

        block = ctx.enter_context(nc.Block())

        loads = [
            (w1_f, w["cn_w1"].rearrange("(c p) n -> p c n", p=P)),
            (w2_sb, w["cn_w2"].rearrange("(c p) n -> p c n", p=P)),
            (w3_sb, w["cn_w3"]),
            (w4_sb, w["cn_w4"].rearrange("k n -> n k").partition_broadcast(P)),
            (b1_sb, w["cn_b1"].rearrange("(c p) -> p c", p=P)),
            (b2_sb, w["cn_b2"].rearrange("(p a) -> p a", a=1)),
            (b3_f, w["cn_b3"].rearrange("(a n) -> a n", a=1)),
            (b4_f, w["cn_b4"].rearrange("(a n) -> a n", a=1).partition_broadcast(P)),
            (gw1_sb, w["gc_w1"].rearrange("(c p) n -> p c n", p=P)),
            (gw2_sb, w["gc_w2"]),
            (gw3_sb, w["gc_w3"]),
            (gb1_sb, w["gc_b1"].rearrange("(p a) -> p a", a=1)),
            (gb2_sb, w["gc_b2"].rearrange("(p a) -> p a", a=1)),
            (gb3_f, w["gc_b3"].rearrange("(a n) -> a n", a=1).partition_broadcast(P)),
            (range_f, w["adaptive_range"].rearrange("(a n) -> a n", a=1).partition_broadcast(P)),
        ]

        @block.sync
        def _(sp):
            sp.dma_start(x_all[:, 0:TILES, :], x2_view[0]).then_inc(x2_loaded[0], 16)
            with nc.allow_non_contiguous_dma(reason="small vectors"):
                for dst, src in loads:
                    sp.dma_start(dst[:], src).then_inc(f_loaded, 16)
            for b in range(1, B):
                at_least(sp, x2_loaded[b % 2], 16 * (b // 2))
                sp.dma_start(x_all[:, b * TILES:(b + 1) * TILES, :],
                             x2_view[b]).then_inc(x2_loaded[b % 2], 16)
            with sp.Fori(0, NGROUPS) as m:
                sp.wait_ge(y_ready, m * (2 * G) + 2 * G)
                sp.dma_start(out_view[m], x_all[:, bass.ds(m * G, G), :]).then_inc(y_stored, 16)
            sp.wait_ge(y_stored, 16 * NGROUPS)

        @block.gpsimd
        def _(pool):
            pool.memset(ident[:], 0.0).then_inc(f_zeroed, 1)
            pool.memset(minus_half[:], -0.5).then_inc(f_zeroed, 1)
            pool.memset(ones[:], 1.0).then_inc(f_zeroed, 1)
            pool.memset(sign[:, 0:1], -1.0).then_inc(f_zeroed, 1)
            pool.memset(sign[:, 1:2], 1.0).then_inc(f_zeroed, 1)
            pool.wait_ge(f_zeroed, 5)
            pool.affine_select(out=ident[:], in_=ident[:], compare_op=ALU.not_equal, fill=1.0,
                               base=0, pattern=[[-1, P]], channel_multiplier=1).then_inc(f_consts, 1)
            for s in range(2):
                pool.affine_select(out=sign[:, s:s + 1], in_=sign[:, s:s + 1], compare_op=ALU.is_gt,
                                   fill=1.0 - 2.0 * s, base=BLOCK, pattern=[[0, 1]],
                                   channel_multiplier=-1).then_inc(f_consts, 1)
            pool.wait_ge(f_loaded, 16 * len(loads))

            def do(n, turn, r):
                for kind, ahead, rest in period_steps(n):
                    m, slot = n + ahead, (r + ahead) % SLOTS
                    if kind == "stats":
                        pool.wait_ge(var_ready, m + 1)
                        pool.tensor_tensor(rstd[slot][:], var_eps[slot][:],
                                           minus_half[:].to_broadcast([P, G]),
                                           ALU.pow).then_inc(rstd_ready, 1)
                    if kind == "mix":
                        c, = rest
                        pool.wait_ge(parts_ready[c], (m + 1) * c)
                        at_least(pool, h1_ready[c], m * DC)
                        other = made[slot][:, 0:DC, :] if c == 1 else part_a[:]
                        pool.tensor_tensor(mixed_sb[c][:], part_b[c][:], other,
                                           ALU.add).then_inc(mix_ready[c], 1)
                    if kind == "dot":
                        c, = rest
                        pool.wait_ge(h3_ready[c], m + 1)
                        at_least(pool, logit_ready[c], m)
                        pool.tensor_tensor(h3_w4[c][:], h3[c][:],
                                           w4_sb[:].unsqueeze(1).broadcast_to([P, G, H3]),
                                           ALU.mult).then_inc(h3_w4_ready[c], 1)

            walk_periods(pool, do)

        @block.scalar
        def _(act):
            act.wait_ge(f_loaded, 16 * len(loads))
            act.wait_ge(f_hi, 13)

            def do(n, turn, r):
                for kind, ahead, rest in period_steps(n):
                    m, slot = n + ahead, (r + ahead) % SLOTS
                    if kind == "turn":
                        c, = rest
                        act.wait_ge(x0_turned, m * DC + c + 1)
                        at_least(act, made_done, m * (2 * DC))
                        nc.scalar.activation(x0T_hi[:, c, :], made_ps[c][:], ACT.Copy,
                                             accum_out=x0_sum[slot][:, c:c + 1]
                                             ).then_inc(x0T_hi_ready, 1)
                    if kind == "product":
                        e, = rest
                        act.wait_ge(made_done, m * (2 * DC) + e + 1)
                        at_least(act, mix_ready[FFN_CYCLES - 1], m - SLOTS + 1)
                        nc.scalar.activation(made[slot][:, e, :], made_ps[(DC + e) % 3][:],
                                             ACT.Copy).then_inc(made_ready, 1)
                    if kind == "global" and r % 2 == 1:
                        s, = rest
                        batch = batch_of(turn, r, 0)
                        act.wait_ge(global_done, batch * 3 + s + 1)
                        if s == 0:
                            nc.scalar.activation(gh1[:], global_ps[:, 0:1], ACT.Gelu,
                                                 bias=gb1_sb[:], scale=1.0 / T).then_inc(global_act, 1)
                        elif s == 1:
                            nc.scalar.activation(gh2[:], global_ps[0:H3, 1:2], ACT.Gelu,
                                                 bias=gb2_sb[:]).then_inc(global_act, 1)
                        else:
                            at_least(act, base_ready, batch)
                            nc.scalar.activation(global_tanh[:], global_ps[:, 2:3], ACT.Tanh,
                                                 bias=gb3_half[:], scale=0.5).then_inc(global_act, 1)
                    if kind == "gelu1":
                        c, = rest
                        if c == 0:
                            act.wait_ge(made_ready, m * (2 * DC) + DC)
                        else:
                            act.wait_ge(mix_ready[c], m + 1)
                        at_least(act, h2_done[c], m)
                        for k in range(DC):
                            src = made[slot][:, k, :] if c == 0 else mixed_sb[c][:, k, :]
                            nc.scalar.activation(h1[c][:, k, :], src, ACT.Gelu,
                                                 bias=b1_sb[:, k:k + 1]).then_inc(h1_ready[c], 1)
                    if kind == "h2":
                        c, = rest
                        act.wait_ge(h2_done[c], m + 1)
                        at_least(act, h3_done[c], m)
                        nc.scalar.activation(h2[c][:], cycle_ps[c][:], ACT.Gelu,
                                             bias=b2_sb[:]).then_inc(h2_ready[c], 1)
                    if kind == "h3":
                        c, = rest
                        act.wait_ge(h3_done[c], m + 1)
                        at_least(act, h3_w4_ready[c], m)
                        nc.scalar.activation(h3[c][:].rearrange("p t k -> p (t k)"),
                                             cycle_ps[c][:, 0:G * H3],
                                             ACT.Gelu).then_inc(h3_ready[c], 1)
                    if kind == "squash":
                        c, = rest
                        act.wait_ge(logit_ready[c], m + 1)
                        at_least(act, coupling_ready[c], m)
                        nc.scalar.activation(token_tanh[c][:], logit[c][:], ACT.Tanh,
                                             bias=b4_half[:], scale=0.5).then_inc(tanh_ready[c], 1)

            walk_periods(act, do)

        @block.vector
        def _(dve):
            dve.wait_ge(f_loaded, 16 * len(loads))
            dve.wait_ge(f_consts, 3)
            dve.tensor_copy(w1_hi[0][:], w1_f[:]).then_inc(f_hi, 1)
            dve.tensor_copy(b3_hi[:], b3_f[:]).then_inc(f_hi, 1)
            dve.tensor_copy(ones_r[:], ones[:]).then_inc(f_hi, 1)
            dve.wait_ge(f_hi, 3)
            dve.tensor_tensor(w1_lo[0][:], w1_f[:], w1_hi[0][:].bitcast(F32),
                              ALU.subtract).then_inc(f_hi, 1)
            dve.tensor_tensor(b3_lo[:], b3_f[:], b3_hi[:].bitcast(F32),
                              ALU.subtract).then_inc(f_hi, 1)
            dve.wait_ge(f_hi, 5)
            for dst, src in ((w1_hi[1], w1_hi[0]), (w1_lo[1], w1_lo[0])):
                for k in range(DC):
                    dve.tensor_scalar(dst[:, k, :], src[:, DC - 1 - k, :].bitcast(F32),
                                      sign[:, k:k + 1], None, ALU.mult).then_inc(f_hi, 1)
            for dst, src, by in ((b4_half, b4_f, 0.5), (gb3_half, gb3_f, 0.5),
                                 (range_token, range_f, 0.3), (range_global, range_f, 0.7)):
                dve.tensor_scalar(dst[:], src[:], by, None, ALU.mult).then_inc(f_hi, 1)

            dve.wait_ge(f_hi, 13)

            def do(n, turn, r):
                for kind, ahead, rest in period_steps(n):
                    m, slot = n + ahead, (r + ahead) % SLOTS
                    if kind == "stats":
                        batch_parity = slot // 2
                        dve.wait_ge(x2_loaded[batch_parity], (turn + (r + ahead) // SLOTS) * 16 + 16)
                        at_least(dve, moments_ready, m * G)
                        for t in range(G):
                            dve.bn_stats(stats[:, t, :], x_tile(m, t))
                        dve.drain()
                        for t in range(G):
                            dve.bn_aggr(moments[slot][:, t, :], stats[:, t, :]).then_inc(moments_ready, 1)
                        dve.wait_ge(moments_ready, m * G + G)
                        dve.tensor_scalar(var_eps[slot][:], moments[slot][:, :, 1], EPS, None,
                                          ALU.add).then_inc(var_ready, 1)
                    if kind == "scale":
                        dve.wait_ge(rstd_ready, m + 1)
                        at_least(dve, x0_turned, (m - SLOTS + 1) * DC)
                        at_least(dve, y_ready, (m - SLOTS + 1) * (2 * G))
                        for t in range(G):
                            dve.tensor_scalar(x0[slot][:, t, :], x_tile(m, t),
                                              moments[slot][:, t, 0:1], rstd[slot][:, t:t + 1],
                                              ALU.subtract, ALU.mult).then_inc(x0_ready, 1)
                    if kind == "turn":
                        c, = rest
                        dve.wait_ge(x0T_hi_ready, m * DC + c + 1)
                        dve.tensor_tensor(x0T_lo[:, c, :], made_ps[c][:], x0T_hi[:, c, :].bitcast(F32),
                                          ALU.subtract).then_inc(x0T_ready, 1)
                    if kind == "global" and r % 2 == 1 and rest[0] == 2:
                        batch = batch_of(turn, r, 0)
                        dve.wait_ge(global_act, batch * 3 + 3)
                        dve.tensor_scalar(base_coupling[(r // 2) % 2][:], global_tanh[:],
                                          range_global[:], 0.1, ALU.mult,
                                          ALU.add).then_inc(base_ready, 1)
                    if kind == "mix":
                        c, = rest
                        dve.wait_ge(spread_done[c], m + 1)
                        at_least(dve, mix_ready[c], m)
                        if c == FFN_CYCLES - 1:
                            dve.tensor_tensor(part_a[:],
                                              spread_a_ps[:].unsqueeze(1).broadcast_to([P, DC, G * P]),
                                              made[slot][:, 0:DC, :], ALU.mult).then_inc(parts_ready[c], 1)
                        dve.tensor_tensor(part_b[c][:],
                                          cycle_ps[c][:].unsqueeze(1).broadcast_to([P, DC, G * P]),
                                          made[slot][:, DC:, :], ALU.mult).then_inc(parts_ready[c], 1)
                    if kind == "dot":
                        c, = rest
                        dve.wait_ge(h3_w4_ready[c], m + 1)
                        at_least(dve, tanh_ready[c], m)
                        dve.tensor_reduce(logit[c][:], h3_w4[c][:], AX_X, ALU.add).then_inc(logit_ready[c], 1)
                    if kind == "squash":
                        c, = rest
                        if c == 0:
                            dve.wait_ge(base_ready, batch_of(turn, r, ahead) + 1)
                        update_state(c, m, slot)
                    if kind == "final":
                        t, = rest
                        a_b = state[FFN_CYCLES - 1][slot % 2]
                        if t == 0:
                            dve.wait_ge(minus_b_ready, m + 1)
                        at_least(dve, y_ready, (m * G + t) * 2)
                        dve.scalar_tensor_tensor(out=y_part[:], in0=x0[slot][:, t, :],
                                                 scalar=a_b[:, 0, t:t + 1], in1=x_tile(m, t),
                                                 op0=ALU.mult, op1=ALU.add).then_inc(y_part_ready, 1)
                        dve.wait_ge(y_part_ready, m * G + t + 1)
                        y = x_tile(m, t).rearrange("p (k d) -> p k d", d=BLOCK)
                        y_in = y_part[:].rearrange("p (k d) -> p k d", d=BLOCK)
                        source = x0[slot][:, t, :].rearrange("p (k d) -> p k d", d=BLOCK)
                        dve.scalar_tensor_tensor(out=y[:, 0:4:3, :], in0=source[:, 2:0:-1, :],
                                                 scalar=a_b[:, 1, t:t + 1], in1=y_in[:, 0:4:3, :],
                                                 op0=ALU.mult, op1=ALU.add).then_inc(y_ready, 1)
                        dve.scalar_tensor_tensor(out=y[:, 1:3, :], in0=source[:, 3::-3, :],
                                                 scalar=minus_b[:, t:t + 1], in1=y_in[:, 1:3, :],
                                                 op0=ALU.mult, op1=ALU.add).then_inc(y_ready, 1)

            def x_tile(m, t):
                if isinstance(m, int):
                    return x_all[:, m * G + t, :]
                return x_all[:, bass.ds(m * G + t, 1), :].rearrange("p a f -> p (a f)")

            def update_state(c, m, slot):
                new = state[c][slot % 2]
                old = state[c - 1][slot % 2]
                dve.wait_ge(tanh_ready[c], m + 1)
                if c == 0:
                    at_least(dve, spread_done[1], m - 1)
                    at_least(dve, coupling_ready[0], m)
                    dve.tensor_scalar(new[:, 1, :], token_tanh[c][:], range_token[:],
                                      base_coupling[slot // 2][:], ALU.mult,
                                      ALU.add).then_inc(coupling_ready[0], 1)
                    return
                at_least(dve, state_ready[c], m * 2)
                dve.tensor_scalar(coupling[c][:], token_tanh[c][:], range_token[:],
                                  base_coupling[slot // 2][:], ALU.mult,
                                  ALU.add).then_inc(coupling_ready[c], 1)
                dve.wait_ge(coupling_ready[c], m + 1)
                if c == 1:
                    dve.wait_ge(coupling_ready[0], m + 1)
                    dve.tensor_tensor(scaled[c][:, 0, :], old[:, 1, :], coupling[c][:],
                                      ALU.mult).then_inc(scaled_ready[c], 1)
                    dve.wait_ge(scaled_ready[c], m + 1)
                    at_least(dve, spread_done[2], m - 1)
                    dve.tensor_tensor(new[:, 1, :], old[:, 1, :], coupling[c][:],
                                      ALU.add).then_inc(state_ready[c], 1)
                    dve.tensor_scalar(new[:, 0, :], scaled[c][:, 0, :], -1.0, 1.0, ALU.mult,
                                      ALU.add).then_inc(state_ready[c], 1)
                    return
                dve.wait_ge(state_ready[1], m * 2 + 2)
                dve.tensor_tensor(scaled[c][:], old[:],
                                  coupling[c][:].unsqueeze(1).broadcast_to([P, 2, G]),
                                  ALU.mult).then_inc(scaled_ready[c], 1)
                dve.wait_ge(scaled_ready[c], m + 1)
                at_least(dve, y_ready, m * (2 * G))
                dve.tensor_tensor(new[:, 0, :], old[:, 0, :], scaled[c][:, 1, :],
                                  ALU.subtract).then_inc(state_ready[c], 1)
                dve.tensor_tensor(new[:, 1, :], old[:, 1, :], scaled[c][:, 0, :],
                                  ALU.add).then_inc(state_ready[c], 1)
                dve.wait_ge(state_ready[c], m * 2 + 2)
                dve.tensor_scalar(minus_b[:], new[:, 1, :], -1.0, None,
                                  ALU.mult).then_inc(minus_b_ready, 1)

            walk_periods(dve, do)

        @block.tensor
        def _(pe):
            pe.wait_ge(f_hi, 13)
            pe.wait_ge(f_consts, 3)

            def do(n, turn, r):
                for kind, ahead, rest in period_steps(n):
                    m, slot = n + ahead, (r + ahead) % SLOTS
                    if kind == "turn":
                        c, = rest
                        pe.wait_ge(x0_ready, m * G + G)
                        at_least(pe, made_ready, (m - 1) * (2 * DC) + c + 2)
                        for t in range(G):
                            mm = nc.tensor.transpose(made_ps[c][:, t * P:(t + 1) * P],
                                                     x0[slot][:, t, c * P:(c + 1) * P], ident[:])
                        mm.then_inc(x0_turned, 1)
                    if kind == "product":
                        e, = rest
                        which, chunk = divmod(e, DC)
                        pe.wait_ge(x0T_ready, m * DC + DC)
                        if e == 0:
                            at_least(pe, made_ready, m * (2 * DC))
                        if e == 3:
                            pe.wait_ge(made_ready, m * (2 * DC) + 1)
                        cols = slice(chunk * P, (chunk + 1) * P)
                        ps = made_ps[(DC + e) % 3]
                        for k in range(DC):
                            hi, lo = w1_hi[which][:, k, cols], w1_lo[which][:, k, cols]
                            nc.tensor.matmul(ps[:], hi, x0T_hi[:, k, :], start=k == 0, stop=False)
                            nc.tensor.matmul(ps[:], hi, x0T_lo[:, k, :], start=False, stop=False)
                            mm = nc.tensor.matmul(ps[:], lo, x0T_hi[:, k, :], start=False,
                                                  stop=k == DC - 1)
                        mm.then_inc(made_done, 1)
                    if kind == "global" and r % 2 == 1:
                        s, = rest
                        batch = batch_of(turn, r, 0)
                        if s == 0:
                            pe.wait_ge(x0T_hi_ready, m * DC + DC)
                            at_least(pe, global_act, batch * 3)
                            for k in range(DC):
                                for half, of in enumerate(((slot - 1) % SLOTS, slot)):
                                    mm = nc.tensor.matmul(global_ps[:, 0:1], gw1_sb[:, k, :],
                                                          x0_sum[of][:, k:k + 1],
                                                          start=k + half == 0, stop=k + half == DC)
                        elif s == 1:
                            pe.wait_ge(global_act, batch * 3 + 1)
                            mm = nc.tensor.matmul(global_ps[0:H3, 1:2], gw2_sb[:], gh1[:],
                                                  start=True, stop=True)
                        else:
                            pe.wait_ge(global_act, batch * 3 + 2)
                            mm = nc.tensor.matmul(global_ps[:, 2:3],
                                                  gw3_sb[:].to_broadcast([H3, P]), gh2[:],
                                                  start=True, stop=True)
                        mm.then_inc(global_done, 1)
                    if kind == "spread":
                        c, = rest
                        a_b = state[c - 1][slot % 2]
                        if c == 1:
                            pe.wait_ge(coupling_ready[0], m + 1)
                        else:
                            pe.wait_ge(state_ready[c - 1], m * 2 + 2)
                            at_least(pe, parts_ready[c], m * c)
                        at_least(pe, h3_ready[c], m)
                        for which in range(2 if c == 2 else 1):
                            ps = spread_a_ps if c == 2 and which == 0 else cycle_ps[c]
                            part = 0 if ps is spread_a_ps else 1
                            for t in range(G):
                                mm = nc.tensor.transpose(ps[:, t * P:(t + 1) * P],
                                                         a_b[:, part, t:t + 1].to_broadcast([P, P]),
                                                         ident[:])
                        mm.then_inc(spread_done[c], 1)
                    if kind == "h2":
                        c, = rest
                        pe.wait_ge(h1_ready[c], m * DC + DC)
                        if c == 0:
                            at_least(pe, h3_ready[c], m)
                        for k in range(DC):
                            mm = nc.tensor.matmul(cycle_ps[c][:], w2_sb[:, k, :], h1[c][:, k, :],
                                                  start=k == 0, stop=k == DC - 1)
                        mm.then_inc(h2_done[c], 1)
                    if kind == "h3":
                        c, = rest
                        pe.wait_ge(h2_ready[c], m + 1)
                        ps = cycle_ps[c][:, 0:G * H3]
                        for part, b3 in enumerate((b3_hi, b3_lo)):
                            nc.tensor.matmul(ps.rearrange("p (t k) -> p t k", k=H3), ones_r[:],
                                             b3[:].unsqueeze(1).broadcast_to([1, G, H3]),
                                             start=part == 0, stop=False)
                        for t in range(G):
                            mm = nc.tensor.matmul(ps[:, t * H3:(t + 1) * H3],
                                                  h2[c][:, t * P:(t + 1) * P], w3_sb[:],
                                                  start=False, stop=t == G - 1)
                        mm.then_inc(h3_done[c], 1)

            walk_periods(pe, do)


def rope_tables():
    import numpy as np
    positions = np.arange(0, HS, 2, dtype=np.float32)
    theta = (np.float32(10000.0) ** (np.float32(-2.0) * positions / np.float32(HS))).astype(np.float32)
    angles = (np.arange(T, dtype=np.float32)[:, None] * theta[None, :]).astype(np.float64)
    scale = HS ** -0.25
    cos, sin = np.cos(angles) * scale, np.sin(angles) * scale
    return cos.astype(np.float32), np.concatenate([-sin, sin], axis=1).astype(np.float32)


WEIGHTS = ["cn_w1", "cn_b1", "cn_w2", "cn_b2", "cn_w3", "cn_b3", "cn_w4", "cn_b4", "gc_w1",
           "gc_b1", "gc_w2", "gc_b2", "gc_w3", "gc_b3", "adaptive_range"]


def kernel(**inputs):
    import numpy as np
    import concourse.bacc as bacc
    from concourse.bass_utils import run_bass_kernel_spmd

    def halves(w):
        return np.concatenate([w[0::2], w[1::2]], axis=0)

    wq, wk, wv = (np.asarray(inputs[f"L0_attn_W{n}"]) for n in "qkv")
    wqkv = np.concatenate([halves(wq[0]), halves(wq[1]), halves(wk), wv], axis=0).T
    cos_t, sin_t = rope_tables()
    arrays = {"x": np.ascontiguousarray(inputs["L0_attn_x"]), "wqkv": np.ascontiguousarray(wqkv),
              "wo": np.ascontiguousarray(np.asarray(inputs["L0_attn_Wo"]).T),
              "cos_t": cos_t, "sin_t": sin_t}
    arrays.update({n: np.ascontiguousarray(inputs[f"L0_ffn_{n}"]) for n in WEIGHTS})
    nc = bacc.Bacc("TRN2", target_bir_lowering=False, num_devices=1)
    ins = {name: nc.dram_tensor(name, a.shape, F32, kind="ExternalInput").ap()
           for name, a in arrays.items()}
    x2 = nc.dram_tensor("x2", (B, T, D), F32, kind="Internal").ap()
    out = nc.dram_tensor("out", (B, T, D), F32, kind="ExternalOutput").ap()
    attention_phase(nc, *(ins[n] for n in ("x", "wqkv", "wo", "cos_t", "sin_t")), x2)
    ffn_phase(nc, x2, ins, out)
    r = run_bass_kernel_spmd(nc, [arrays], core_ids=[0])
    return r.results[0]["out"]
```

```python
from contextlib import ExitStack

import concourse.bass as bass
from concourse import mybir

F32 = mybir.dt.float32
F32R = mybir.dt.float32r
BF16 = mybir.dt.bfloat16
ALU = mybir.AluOpType
ACT = mybir.ActivationFunctionType
AX_X = mybir.AxisListType.X

P = 128
B, T, D = 8, 1024, 256
HS, NH = 128, 2
TILES = T // P
G = 4
GROUPS = TILES // G
DC = D // P
EPS = 1e-5
MASKED = -1e30
HALF = HS // 2

UNITS = [(g, h) for g in range(GROUPS) for h in range(NH)]
STEPS = [G * (g + 1) for g, h in UNITS]
FIRST_STEP = [sum(STEPS[:u]) for u in range(len(UNITS))]
BATCH_STEPS = sum(STEPS)
BATCH_SCORES = len(UNITS) * G


def at_least(engine, semaphore, value):
    if isinstance(value, int) and value <= 0:
        return
    engine.wait_ge(semaphore, value)


def spread(*parts):
    keyed = [(start + (stop - start) * (n + 0.5) / len(part), which, n, step)
             for which, (part, start, stop) in enumerate(parts) for n, step in enumerate(part)]
    return [step for _, _, _, step in sorted(keyed, key=lambda x: x[:3])]


ACT_LATER = {"scores": 2.5, "turn_p": 0.5, "close": 0.5}
DVE_LATER = {"scores": 0.5, "turn_p": 1.6, "turn_x": 1.6, "turn_qk": 1.6, "close": 1.6, "output": 1.2,
             "project": 2.0}


def delayed(order, later):
    at = sorted(range(len(order)), key=lambda n: (n + later.get(order[n][0], 0), n))
    return [order[n] for n in at]


def projections(ahead, g):
    return ([("turn_x", ahead, g, c) for c in range(DC)]
            + [("project", ahead, g, t) for t in range(G)])


def rotated(ahead, g):
    return [("turn_qk", ahead, g, c) for c in range(NH + 1)]


LAG = 2


def attention_steps(ahead, u):
    steps = []
    for j in range(STEPS[u]):
        steps.append(("turn_p", ahead, u, j))
        if j >= LAG:
            steps.append(("attend", ahead, u, j - LAG))
    return steps


def attention_end(ahead, u):
    return [("attend", ahead, u, j) for j in range(STEPS[u] - LAG, STEPS[u])] + [("close", ahead, u)]


def outputs(ahead, g):
    return [("output", ahead, g, t) for t in range(G)]


def batch_order(first, last):
    def scores(u):
        return [("scores", 0, u, k) for k in range(G)]

    def following(steps):
        return [] if last else steps

    def preceding(steps):
        return [] if first else steps

    return spread(
        (scores(0), -0.05, 0.9),
        (preceding(attention_steps(-1, 3)), 0, 1),
        (projections(0, 1), 0, 1),
        (following([("norm", 1, 0)]), 1, 1),
        (scores(1), 0.95, 1.9),
        (preceding(attention_end(-1, 3)) + attention_steps(0, 0), 1, 2),
        (preceding(outputs(-1, 1)), 1.35, 1.8),
        (rotated(0, 1), 1.6, 1.95),
        (following([("scale", 1, 0)]), 1.9, 1.9),
        (scores(2), 1.95, 2.9),
        (attention_end(0, 0) + attention_steps(0, 1), 2, 3),
        (following(projections(1, 0)), 2, 3),
        (following([("norm", 1, 1)]), 3, 3),
        (scores(3), 2.95, 3.9),
        (attention_end(0, 1) + attention_steps(0, 2) + attention_end(0, 2), 3, 4),
        (outputs(0, 0), 3.25, 3.7),
        (following(rotated(1, 0)), 3.7, 4),
        (following([("scale", 1, 1)]), 3.9, 3.9))
    return order


PROLOGUE = [("norm", 0, 0), ("scale", 0, 0), ("norm", 0, 1)] + projections(0, 0) + [
    ("scale", 0, 1)] + rotated(0, 0)
FIRST_BATCH = batch_order(True, False)
MIDDLE_BATCH = batch_order(False, False)
LAST_BATCH = batch_order(False, True)
EPILOGUE = attention_steps(-1, 3) + attention_end(-1, 3) + outputs(-1, 1)


BANKS = 3


def banks_of(order):
    users = [step for step in order if step[0] in ("turn_x", "project", "turn_qk", "turn_p", "output")]
    return {step: n % BANKS for n, step in enumerate(users)}


def last_users(order):
    return {n: step for step, n in banks_of(order).items()}


assert last_users(FIRST_BATCH) == last_users(MIDDLE_BATCH)


def walk(engine, do, later={}):
    def run(order, b, half, parity):
        do(delayed(order, later), banks_of(order), b, half, parity)

    run(PROLOGUE, 0, 0, 0)
    run(FIRST_BATCH, 0, 0, 0)
    with engine.Fori(0, (B - 2) // 2) as pair:
        run(MIDDLE_BATCH, pair * 2 + 1, pair, 1)
        run(MIDDLE_BATCH, pair * 2 + 2, pair + 1, 0)
    run(LAST_BATCH, B - 1, (B - 1) // 2, (B - 1) % 2)
    run(EPILOGUE, B, B // 2, B % 2)


def attention_phase(nc, x, wqkv, wo, cos_t, sin_t, x2):
    x_view = x.rearrange("b (i p) f -> b p i f", p=P)
    x2_view = x2.rearrange("b (i p) f -> b p i f", p=P)
    with ExitStack() as ctx:
        def sb(name, shape, dt=F32):
            return ctx.enter_context(nc.sbuf_tensor(name, shape, dt))

        def psum(name, shape):
            return ctx.enter_context(nc.psum_tensor(name, shape, F32))

        def sem(name):
            return ctx.enter_context(nc.semaphore(name))

        ident = sb("ident", [P, P])
        ident_b = sb("ident_b", [P, P], BF16)
        mask_b = sb("mask_b", [P, P], BF16)
        minus_half = sb("minus_half", [P, 1])
        wqkv_f = sb("wqkv_f", [P, DC, 4 * HS])
        wqkv_hi = sb("wqkv_hi", [P, DC, 4 * HS], F32R)
        wqkv_lo = sb("wqkv_lo", [P, DC, 4 * HS], F32R)
        wo_f = sb("wo_f", [P, NH, D])
        wo_hi = sb("wo_hi", [P, NH, D], F32R)
        wo_lo = sb("wo_lo", [P, NH, D], F32R)
        cos_sb = sb("cos_sb", [P, TILES, HALF])
        sin_sb = sb("sin_sb", [P, TILES, HS])
        xt = [sb(f"xt{n}", [P, TILES, D]) for n in range(2)]
        stats = sb("stats", [P, G, 6])
        moments = [sb(f"moments{n}", [P, G, 2]) for n in range(GROUPS)]
        var_eps = [sb(f"var_eps{n}", [P, G]) for n in range(GROUPS)]
        rstd = [sb(f"rstd{n}", [P, G]) for n in range(GROUPS)]
        xn = [sb(f"xn{n}", [P, G, D]) for n in range(GROUPS)]
        xnT_hi = sb("xnT_hi", [P, DC, G * P], F32R)
        xnT_lo = sb("xnT_lo", [P, DC, G * P], F32R)
        qkv = [sb(f"qkv{t}", [P, 4 * HS]) for t in range(G)]
        rope_a = sb("rope_a", [P, 3 * HS])
        rope_b = sb("rope_b", [P, 3 * HS])
        rot = sb("rot", [P, G, 3 * HS])
        q_hi = [[sb(f"q_hi{g}{h}", [P, G * P], F32R) for h in range(NH)] for g in range(GROUPS)]
        q_lo = [[sb(f"q_lo{g}{h}", [P, G * P], F32R) for h in range(NH)] for g in range(GROUPS)]
        k_hi = [sb(f"k_hi{n}", [P, T], F32R) for n in range(2)]
        k_lo = [sb(f"k_lo{n}", [P, T], F32R) for n in range(2)]
        v_hi = [sb(f"v_hi{n}", [P, TILES, HS], F32R) for n in range(2)]
        v_lo = [sb(f"v_lo{n}", [P, TILES, HS], F32R) for n in range(2)]
        neg_max = sb("neg_max", [P, BATCH_SCORES])
        row_sum = [sb(f"row_sum{n}", [P, BATCH_SCORES]) for n in range(2)]
        inv_sum = sb("inv_sum", [P, NH * G])
        probs = [sb(f"probs{n}", [P, G, T]) for n in range(2)]
        PT_RING = 4
        pT_hi = [sb(f"pT_hi{n}", [P, G * P], F32R) for n in range(PT_RING)]
        pT_lo = [sb(f"pT_lo{n}", [P, G * P], F32R) for n in range(PT_RING)]
        oT_hi = [sb(f"oT_hi{h}", [P, G * P], F32R) for h in range(NH)]
        oT_lo = [sb(f"oT_lo{h}", [P, G * P], F32R) for h in range(NH)]
        x_plus = sb("x_plus", [P, D])

        scores_ps = [psum(f"scores_ps{n}", [P, T]) for n in range(2)]
        bank = [psum(f"bank{n}", [P, G * P]) for n in range(BANKS)]
        oT_ps = psum("oT_ps", [P, G * P])

        x_loaded = [[sem(f"x_loaded{n}{g}") for g in range(GROUPS)] for n in range(2)]
        w_loaded = sem("w_loaded")
        x2_stored = [[sem(f"x2_stored{n}{g}") for g in range(GROUPS)] for n in range(2)]
        zeroed = sem("zeroed")
        consts_ready = sem("consts_ready")
        w_hi_ready = sem("w_hi_ready")
        w_ready = sem("w_ready")
        moments_ready = sem("moments_ready")
        var_ready = sem("var_ready")
        rstd_ready = sem("rstd_ready")
        xn_ready = sem("xn_ready")
        x_turned = sem("x_turned")
        xT_hi_ready = sem("xT_hi_ready")
        xT_ready = sem("xT_ready")
        projected = sem("projected")
        qkv_ready = sem("qkv_ready")
        v_hi_ready = sem("v_hi_ready")
        v_ready = sem("v_ready")
        rope_products = sem("rope_products")
        rot_ready = sem("rot_ready")
        qk_turned = sem("qk_turned")
        qk_hi_ready = sem("qk_hi_ready")
        qk_ready = sem("qk_ready")
        scores_done = sem("scores_done")
        max_ready = sem("max_ready")
        probs_ready = sem("probs_ready")
        p_turned = sem("p_turned")
        pT_hi_ready = sem("pT_hi_ready")
        pT_ready = sem("pT_ready")
        attended = sem("attended")
        oT_hi_ready = sem("oT_hi_ready")
        oT_ready = sem("oT_ready")
        inv_ready = sem("inv_ready")
        output_done = sem("output_done")
        x_plus_ready = sem("x_plus_ready")
        x2_ready = sem("x2_ready")

        block = ctx.enter_context(nc.Block())

        @block.sync
        def _(sp):
            def tiles(g):
                return slice(G * g, G * (g + 1))

            sp.dma_start(xt[0][:, tiles(0), :], x_view[0, :, tiles(0), :]).then_inc(x_loaded[0][0], 16)
            for dst, src in ((wqkv_f, wqkv.rearrange("(c p) n -> p c n", p=P)),
                             (cos_sb, cos_t.rearrange("(i p) n -> p i n", p=P)),
                             (sin_sb, sin_t.rearrange("(i p) n -> p i n", p=P)),
                             (wo_f, wo.rearrange("(c p) n -> p c n", p=P))):
                sp.dma_start(dst[:], src).then_inc(w_loaded, 16)
            for n, g in ((0, 1), (1, 0), (1, 1)):
                sp.dma_start(xt[n][:, tiles(g), :], x_view[n, :, tiles(g), :]).then_inc(x_loaded[n][g], 16)

            def load_next(b, half, parity, g):
                if isinstance(b, int) and not 0 < b < B - 1:
                    return
                n = 1 - parity
                sp.wait_ge(x2_stored[n][g], (half + (parity - 1) // 2) * 16 + 16)
                sp.dma_start(xt[n][:, tiles(g), :],
                             x_view[b + 1, :, tiles(g), :]).then_inc(x_loaded[n][g], 16)

            def do(order, banks, b, half, parity):
                if order != PROLOGUE:
                    load_next(b, half, parity, 0)
                for kind, ahead, *rest in order:
                    if kind != "output" or rest[1] != G - 1:
                        continue
                    g, bb, n = rest[0], b + ahead, (parity + ahead) % 2
                    sp.wait_ge(x2_ready, bb * TILES + G * (g + 1))
                    sp.dma_start(x2_view[bb, :, tiles(g), :],
                                 xt[n][:, tiles(g), :]).then_inc(x2_stored[n][g], 16)
                    if g == 1:
                        load_next(b, half, parity, 1)

            walk(sp, do)
            for n in range(2):
                for g in range(GROUPS):
                    sp.wait_ge(x2_stored[n][g], 16 * B // 2)

        @block.gpsimd
        def _(pool):
            pool.memset(ident[:], 0.0).then_inc(zeroed, 1)
            pool.memset(ident_b[:], 0.0).then_inc(zeroed, 1)
            pool.memset(mask_b[:], 0.0).then_inc(zeroed, 1)
            pool.memset(minus_half[:], -0.5).then_inc(zeroed, 1)
            pool.wait_ge(zeroed, 4)
            for m in (ident, ident_b):
                pool.affine_select(out=m[:], in_=m[:], compare_op=ALU.not_equal, fill=1.0, base=0,
                                   pattern=[[-1, P]], channel_multiplier=1).then_inc(consts_ready, 1)
            pool.affine_select(out=mask_b[:], in_=mask_b[:], compare_op=ALU.is_ge, fill=MASKED,
                               base=0, pattern=[[-1, P]],
                               channel_multiplier=1).then_inc(consts_ready, 1)
            pool.wait_ge(w_loaded, 64)

            def do(order, banks, b, half, parity):
                for kind, ahead, *rest in order:
                    bb, n = b + ahead, (parity + ahead) % 2
                    if kind == "norm":
                        g, = rest
                        group = bb * GROUPS + g
                        pool.wait_ge(var_ready, group + 1)
                        pool.tensor_tensor(rstd[g][:], var_eps[g][:],
                                           minus_half[:].to_broadcast([P, G]),
                                           ALU.pow).then_inc(rstd_ready, 1)
                    if kind == "project":
                        g, t = rest
                        i = G * g + t
                        tile = bb * TILES + i
                        pool.wait_ge(qkv_ready, tile + 1)
                        v = qkv[t][:, 3 * HS:4 * HS]
                        at_least(pool, rot_ready, tile)
                        qk = qkv[t][:, 0:3 * HS].rearrange("p (c e d) -> p c e d", e=2, d=HALF)
                        cos = cos_sb[:, i, :].unsqueeze(1).broadcast_to([P, 2 * (NH + 1), HALF])
                        sin = sin_sb[:, i, :].unsqueeze(1).broadcast_to([P, NH + 1, HS])
                        pool.tensor_tensor(
                            rope_a[:].rearrange("p (c d) -> p c d", d=HALF),
                            qkv[t][:, 0:3 * HS].rearrange("p (c d) -> p c d", d=HALF),
                            cos, ALU.mult).then_inc(rope_products, 1)
                        pool.tensor_tensor(
                            rope_b[:].rearrange("p (c e d) -> p c e d", e=2, d=HALF),
                            qk[:, :, ::-1, :],
                            sin.rearrange("p c (e d) -> p c e d", e=2),
                            ALU.mult).then_inc(rope_products, 1)
                        pool.wait_ge(v_hi_ready, tile + 1)
                        pool.tensor_tensor(v_lo[n][:, i, :], v, v_hi[n][:, i, :].bitcast(F32),
                                           ALU.subtract).then_inc(v_ready, 1)
                        pool.wait_ge(rope_products, (tile + 1) * 2)
                        at_least(pool, qk_turned, (bb * GROUPS + g) * (NH + 1))
                        pool.tensor_tensor(rot[:, t, :], rope_a[:], rope_b[:],
                                           ALU.add).then_inc(rot_ready, 1)

            walk(pool, do)

        @block.scalar
        def _(act):
            def copy(out, in_):
                return nc.scalar.activation(out, in_, ACT.Copy)

            def do(order, banks, b, half, parity):
                for step in order:
                    kind, ahead, *rest = step
                    bb, n = b + ahead, (parity + ahead) % 2
                    ps = bank[banks[step]] if step in banks else None
                    if kind == "turn_x":
                        g, c = rest
                        group = bb * GROUPS + g
                        act.wait_ge(x_turned, group * DC + c + 1)
                        at_least(act, projected, group * G)
                        copy(xnT_hi[:, c, :], ps[:]).then_inc(xT_hi_ready, 1)
                    if kind == "project":
                        g, t = rest
                        tile = bb * TILES + G * g + t
                        act.wait_ge(projected, tile + 1)
                        at_least(act, rot_ready, tile - G + 1)
                        at_least(act, v_ready, tile - G + 1)
                        copy(qkv[t][:], ps[:]).then_inc(qkv_ready, 1)
                    if kind == "turn_qk":
                        g, c = rest
                        group = bb * GROUPS + g
                        act.wait_ge(qk_turned, group * (NH + 1) + c + 1)
                        at_least(act, scores_done,
                                 (bb - 1) * BATCH_SCORES + NH * G * (g + 1))
                        out = q_hi[g][c][:] if c < NH else k_hi[n][:, g * G * P:(g + 1) * G * P]
                        copy(out, ps[:]).then_inc(qk_hi_ready, 1)
                    if kind == "scores":
                        u, k = rest
                        g, h = UNITS[u]
                        keys = (G * g + k + 1) * P
                        s = bb * BATCH_SCORES + u * G + k
                        act.wait_ge(max_ready, s + 1)
                        if k == 0:
                            before = (u - 2) % len(UNITS)
                            at_least(act, p_turned, (bb - (u < 2)) * BATCH_STEPS
                                     + FIRST_STEP[before] + STEPS[before])
                        nc.scalar.activation(probs[u % 2][:, k, 0:keys], scores_ps[k % 2][:, 0:keys],
                                             ACT.Exp, bias=neg_max[:, u * G + k:u * G + k + 1],
                                             accum_out=row_sum[n][:, u * G + k:u * G + k + 1]
                                             ).then_inc(probs_ready, 1)
                    if kind == "turn_p":
                        u, j = rest
                        m = bb * BATCH_STEPS + FIRST_STEP[u] + j
                        skip = max(0, j - G * UNITS[u][0]) * P
                        r = (FIRST_STEP[u] + j) % PT_RING
                        act.wait_ge(p_turned, m + 1)
                        at_least(act, attended, m - PT_RING + 1)
                        copy(pT_hi[r][:, skip:], ps[:, skip:]).then_inc(pT_hi_ready, 1)
                    if kind == "close":
                        u, = rest
                        g, h = UNITS[u]
                        act.wait_ge(attended, bb * BATCH_STEPS + FIRST_STEP[u] + STEPS[u])
                        at_least(act, output_done, bb * TILES + G * g)
                        copy(oT_hi[h][:], oT_ps[:]).then_inc(oT_hi_ready, 1)

            walk(act, do, ACT_LATER)

        @block.vector
        def _(dve):
            dve.wait_ge(w_loaded, 64)
            for hi, f in ((wqkv_hi, wqkv_f), (wo_hi, wo_f)):
                dve.tensor_copy(hi[:], f[:]).then_inc(w_hi_ready, 1)
            dve.wait_ge(w_hi_ready, 2)
            for lo, f, hi in ((wqkv_lo, wqkv_f, wqkv_hi), (wo_lo, wo_f, wo_hi)):
                dve.tensor_tensor(lo[:], f[:], hi[:].bitcast(F32), ALU.subtract).then_inc(w_ready, 1)

            def low(out, whole, hi):
                return dve.tensor_tensor(out, whole, hi.bitcast(F32), ALU.subtract)

            def do(order, banks, b, half, parity):
                for step in order:
                    kind, ahead, *rest = step
                    bb, n = b + ahead, (parity + ahead) % 2
                    ps = bank[banks[step]] if step in banks else None
                    if kind == "norm":
                        g, = rest
                        group = bb * GROUPS + g
                        turn = half + (parity + ahead) // 2
                        dve.wait_ge(x_loaded[n][g], turn * 16 + 16)
                        at_least(dve, moments_ready, group * G)
                        at_least(dve, xn_ready, (group - GROUPS + 1) * G)
                        for t in range(G):
                            dve.bn_stats(stats[:, t, :], xt[n][:, G * g + t, :])
                        dve.drain()
                        for t in range(G):
                            dve.bn_aggr(moments[g][:, t, :], stats[:, t, :]).then_inc(moments_ready, 1)
                        dve.wait_ge(moments_ready, (group + 1) * G)
                        dve.tensor_scalar(var_eps[g][:], moments[g][:, :, 1], EPS, None,
                                          ALU.add).then_inc(var_ready, 1)
                    if kind == "scale":
                        g, = rest
                        group = bb * GROUPS + g
                        dve.wait_ge(rstd_ready, group + 1)
                        at_least(dve, x_turned, (group - GROUPS + 1) * DC)
                        for t in range(G):
                            dve.tensor_scalar(xn[g][:, t, :], xt[n][:, G * g + t, :],
                                              moments[g][:, t, 0:1], rstd[g][:, t:t + 1],
                                              ALU.subtract, ALU.mult).then_inc(xn_ready, 1)
                    if kind == "turn_x":
                        g, c = rest
                        dve.wait_ge(xT_hi_ready, (bb * GROUPS + g) * DC + c + 1)
                        low(xnT_lo[:, c, :], ps[:], xnT_hi[:, c, :]).then_inc(xT_ready, 1)
                    if kind == "project":
                        g, t = rest
                        i = G * g + t
                        dve.wait_ge(qkv_ready, bb * TILES + i + 1)
                        dve.tensor_copy(v_hi[n][:, i, :], qkv[t][:, 3 * HS:]).then_inc(v_hi_ready, 1)
                    if kind == "turn_qk":
                        g, c = rest
                        dve.wait_ge(qk_hi_ready, (bb * GROUPS + g) * (NH + 1) + c + 1)
                        cols = slice(g * G * P, (g + 1) * G * P)
                        lo, hi = ((q_lo[g][c][:], q_hi[g][c][:]) if c < NH
                                  else (k_lo[n][:, cols], k_hi[n][:, cols]))
                        low(lo, ps[:], hi).then_inc(qk_ready, 1)
                    if kind == "scores":
                        u, k = rest
                        keys = (G * UNITS[u][0] + k + 1) * P
                        dve.wait_ge(scores_done, bb * BATCH_SCORES + u * G + k + 1)
                        dve.tensor_reduce(neg_max[:, u * G + k:u * G + k + 1],
                                          scores_ps[k % 2][:, 0:keys], AX_X, ALU.max,
                                          negate=True).then_inc(max_ready, 1)
                    if kind == "turn_p":
                        u, j = rest
                        m = bb * BATCH_STEPS + FIRST_STEP[u] + j
                        skip = max(0, j - G * UNITS[u][0]) * P
                        r = (FIRST_STEP[u] + j) % PT_RING
                        dve.wait_ge(pT_hi_ready, m + 1)
                        low(pT_lo[r][:, skip:], ps[:, skip:],
                            pT_hi[r][:, skip:]).then_inc(pT_ready, 1)
                    if kind == "close":
                        u, = rest
                        h = UNITS[u][1]
                        dve.wait_ge(oT_hi_ready, bb * len(UNITS) + u + 1)
                        low(oT_lo[h][:], oT_ps[:], oT_hi[h][:]).then_inc(oT_ready, 1)
                    if kind == "output":
                        g, t = rest
                        i = G * g + t
                        tile = bb * TILES + i
                        if t == 0:
                            dve.wait_ge(probs_ready, bb * BATCH_SCORES + NH * G * (g + 1))
                            at_least(dve, x2_ready, tile)
                            dve.reciprocal(inv_sum[:], row_sum[n][:, NH * G * g:NH * G * (g + 1)]
                                           ).then_inc(inv_ready, 1)
                            dve.wait_ge(inv_ready, bb * GROUPS + g + 1)
                        dve.wait_ge(output_done, tile + 1)
                        at_least(dve, x2_ready, tile)
                        dve.scalar_tensor_tensor(out=x_plus[:], in0=ps[:, 0:D],
                                                 scalar=inv_sum[:, t:t + 1], in1=xt[n][:, i, :],
                                                 op0=ALU.mult, op1=ALU.add).then_inc(x_plus_ready, 1)
                        dve.wait_ge(x_plus_ready, tile + 1)
                        dve.scalar_tensor_tensor(out=xt[n][:, i, :], in0=ps[:, D:2 * D],
                                                 scalar=inv_sum[:, G + t:G + t + 1], in1=x_plus[:],
                                                 op0=ALU.mult, op1=ALU.add).then_inc(x2_ready, 1)

            walk(dve, do, DVE_LATER)

        @block.tensor
        def _(pe):
            def split_product(out, stationary, moving, first=True, last=True):
                nc.tensor.matmul(out, stationary[0], moving[0], start=first, stop=False)
                nc.tensor.matmul(out, stationary[0], moving[1], start=False, stop=False)
                return nc.tensor.matmul(out, stationary[1], moving[0], start=False, stop=last)

            pe.wait_ge(consts_ready, 3)
            pe.wait_ge(w_ready, 2)
            def reader_of(b, kind, ahead, *rest):
                bb = b + ahead
                if kind == "turn_x":
                    return xT_ready, (bb * GROUPS + rest[0]) * DC + rest[1] + 1
                if kind == "project":
                    return qkv_ready, bb * TILES + G * rest[0] + rest[1] + 1
                if kind == "turn_qk":
                    return qk_ready, (bb * GROUPS + rest[0]) * (NH + 1) + rest[1] + 1
                if kind == "turn_p":
                    return pT_ready, bb * BATCH_STEPS + FIRST_STEP[rest[0]] + rest[1] + 1
                return x2_ready, bb * TILES + G * rest[0] + rest[1] + 1

            user = [None] * BANKS

            def take(before):
                if before is not None:
                    pe.wait_ge(*reader_of(before[0], *before[1]))

            def do(order, banks, b, half, parity):
                if order in (MIDDLE_BATCH, LAST_BATCH):
                    for n, step in last_users(MIDDLE_BATCH).items():
                        user[n] = b - 1, step
                for step in order:
                    kind, ahead, *rest = step
                    bb, n = b + ahead, (parity + ahead) % 2
                    if step in banks:
                        ps = bank[banks[step]]
                        before, user[banks[step]] = user[banks[step]], (b, step)
                    if kind == "turn_x":
                        g, c = rest
                        group = bb * GROUPS + g
                        pe.wait_ge(xn_ready, (group + 1) * G)
                        take(before)
                        for t in range(G):
                            mm = nc.tensor.transpose(ps[:, t * P:(t + 1) * P],
                                                     xn[g][:, t, c * P:(c + 1) * P], ident[:])
                        mm.then_inc(x_turned, 1)
                    if kind == "project":
                        g, t = rest
                        tile = bb * TILES + G * g + t
                        pe.wait_ge(xT_ready, (bb * GROUPS + g + 1) * DC)
                        take(before)
                        for c in range(DC):
                            cols = slice(t * P, (t + 1) * P)
                            mm = split_product(ps[:], (xnT_hi[:, c, cols], xnT_lo[:, c, cols]),
                                               (wqkv_hi[:, c, :], wqkv_lo[:, c, :]),
                                               c == 0, c == DC - 1)
                        mm.then_inc(projected, 1)
                    if kind == "turn_qk":
                        g, c = rest
                        group = bb * GROUPS + g
                        pe.wait_ge(rot_ready, (group + 1) * G)
                        take(before)
                        for t in range(G):
                            mm = nc.tensor.transpose(ps[:, t * P:(t + 1) * P],
                                                     rot[:, t, c * HS:(c + 1) * HS], ident[:])
                        mm.then_inc(qk_turned, 1)
                    if kind == "scores":
                        u, k = rest
                        g, h = UNITS[u]
                        keys = (G * g + k + 1) * P
                        s = bb * BATCH_SCORES + u * G + k
                        pe.wait_ge(qk_ready, (bb * GROUPS + g + 1) * (NH + 1))
                        at_least(pe, probs_ready, s - 1)
                        tile = slice(k * P, (k + 1) * P)
                        ps = scores_ps[k % 2]
                        for at in range(0, keys, G * P):
                            cols = slice(at, min(at + G * P, keys))
                            mm = split_product(ps[:, cols], (q_hi[g][h][:, tile], q_lo[g][h][:, tile]),
                                               (k_hi[n][:, cols], k_lo[n][:, cols]),
                                               last=cols.stop < keys)
                        mm = nc.tensor.matmul(ps[:, keys - P:keys], ident_b[:], mask_b[:],
                                              start=False, stop=True)
                        mm.then_inc(scores_done, 1)
                    if kind == "attend":
                        u, j = rest
                        attend(bb, n, u, j)
                    if kind == "turn_p":
                        take(before)
                        turn_p(ps, bb, *rest)
                    if kind == "output":
                        g, t = rest
                        pe.wait_ge(oT_ready, bb * len(UNITS) + NH * (g + 1))
                        take(before)
                        for h in range(NH):
                            cols = slice(t * P, (t + 1) * P)
                            mm = split_product(ps[:, h * D:(h + 1) * D],
                                               (oT_hi[h][:, cols], oT_lo[h][:, cols]),
                                               (wo_hi[:, h, :], wo_lo[:, h, :]))
                        mm.then_inc(output_done, 1)

            def turn_p(ps, bb, u, j):
                m = bb * BATCH_STEPS + FIRST_STEP[u] + j
                g = UNITS[u][0]
                pe.wait_ge(probs_ready, bb * BATCH_SCORES + (u + 1) * G)
                for k in range(max(0, j - G * g), G):
                    mm = nc.tensor.transpose(ps[:, k * P:(k + 1) * P],
                                             probs[u % 2][:, k, j * P:(j + 1) * P], ident[:])
                mm.then_inc(p_turned, 1)

            def attend(bb, n, u, j):
                m = bb * BATCH_STEPS + FIRST_STEP[u] + j
                skip = max(0, j - G * UNITS[u][0]) * P
                r = (FIRST_STEP[u] + j) % PT_RING
                pe.wait_ge(pT_ready, m + 1)
                if j == 0:
                    at_least(pe, oT_ready, bb * len(UNITS) + u)
                    pe.wait_ge(v_ready, bb * TILES + STEPS[u])
                split_product(oT_ps[:, skip:], (v_hi[n][:, j, :], v_lo[n][:, j, :]),
                              (pT_hi[r][:, skip:], pT_lo[r][:, skip:]),
                              j == 0, j == STEPS[u] - 1).then_inc(attended, 1)

            walk(pe, do)


FFN_CYCLES = 3
H2, H3 = D // 2, D // 4
BLOCK = D // 4
NGROUPS = B * GROUPS
STAGES = 1 + FFN_CYCLES
SLOTS = 4

PERIODS = {
    "tensor": [
        ("global", 0, 0), ("h3", -3, 2), ("global", 0, 1), ("global", 0, 2), ("product", 0, 0),
        ("spread", -1, 1), ("product", 0, 1), ("spread", -2, 2), ("product", 0, 2),
        ("product", 0, 3), ("h2", 0, 0), ("h2", -1, 1), ("h3", 0, 0), ("h2", -2, 2), ("turn", 1, 0),
        ("turn", 1, 1), ("h3", -1, 1),
    ],
    "scalar": [
        ("h3", -2, 1), ("global", 0, 0), ("global", 0, 1), ("h3", -3, 2), ("global", 0, 2),
        ("squash", -1, 0), ("squash", -2, 1), ("product", 0, 0), ("squash", -3, 2),
        ("product", 0, 1), ("gelu1", 0, 0), ("gelu1", -1, 1), ("h2", 0, 0), ("gelu1", -2, 2),
        ("product", 0, 2), ("product", 0, 3), ("h3", 0, 0), ("h2", -1, 1), ("h2", -2, 2),
        ("turn", 1, 0), ("turn", 1, 1),
    ],
    "vector": [
        ("stats", 1), ("turn", 0, 0), ("turn", 0, 1), ("dot", -1, 0), ("dot", -2, 1),
        ("global", 0, 2), ("squash", -1, 0), ("dot", -3, 2), ("squash", -2, 1), ("mix", -1, 1),
        ("squash", -3, 2), ("mix", -2, 2), ("final", -3, 0), ("final", -3, 1), ("final", -3, 2),
        ("final", -3, 3), ("scale", 1),
    ],
    "gpsimd": [
        ("mix", -2, 1), ("mix", -3, 2), ("dot", -1, 0), ("dot", -2, 1), ("dot", -3, 2),
        ("stats", 1),
    ],
}
AHEAD = max(step[1] for steps in PERIODS.values() for step in steps)
BEHIND = -min(step[1] for steps in PERIODS.values() for step in steps)


def period_steps(engine_name, n, r):
    for kind, ahead, *rest in PERIODS[engine_name]:
        if isinstance(n, int) and not 0 <= n + ahead < NGROUPS:
            continue
        if kind == "global" and (r + ahead) % GROUPS != GROUPS - 1:
            continue
        yield kind, ahead, rest


def walk_periods(engine, do):
    for n in range(-AHEAD, SLOTS):
        do(n, n // SLOTS, n % SLOTS)
    with engine.Fori(1, NGROUPS // SLOTS - 1) as turn:
        for r in range(SLOTS):
            do(turn * SLOTS + r, turn, r)
    for n in range(NGROUPS - SLOTS, NGROUPS + BEHIND):
        do(n, n // SLOTS, n % SLOTS)


def batch_of(turn, r, ahead):
    return (turn + (r + ahead) // SLOTS) * (SLOTS // GROUPS) + (r + ahead) % SLOTS // GROUPS


def ffn_phase(nc, x2, w, out):
    x2_view = x2.rearrange("b (i p) f -> b p i f", p=P)
    out_view = out.rearrange("b (g i p) f -> (b g) p i f", p=P, g=GROUPS)
    with ExitStack() as ctx:
        def sb(name, shape, dt=F32):
            return ctx.enter_context(nc.sbuf_tensor(name, shape, dt))

        def psum(name, shape):
            return ctx.enter_context(nc.psum_tensor(name, shape, F32))

        def sem(name):
            return ctx.enter_context(nc.semaphore(name))

        def cycle_sems(name):
            return [sem(f"{name}{c}") for c in range(FFN_CYCLES)]

        ident = sb("f_ident", [P, P])
        minus_half = sb("f_minus_half", [P, 1])
        sign = sb("sign", [P, 2])
        ones = sb("ones", [1, P])
        ones_r = sb("ones_r", [1, P], F32R)
        w1_f = sb("w1_f", [P, DC, D])
        w1_hi = [sb(f"w1_hi{n}", [P, DC, D], F32R) for n in range(2)]
        w1_lo = [sb(f"w1_lo{n}", [P, DC, D], F32R) for n in range(2)]
        w2_sb = sb("w2_sb", [P, DC, H2])
        w3_sb = sb("w3_sb", [P, H3])
        w4_sb = sb("w4_sb", [P, H3])
        b1_sb = sb("b1_sb", [P, DC])
        b2_sb = sb("b2_sb", [P, 1])
        b3_f = sb("b3_f", [1, H3])
        b3_hi = sb("b3_hi", [1, H3], F32R)
        b3_lo = sb("b3_lo", [1, H3], F32R)
        b4_f = sb("b4_f", [P, 1])
        b4_half = sb("b4_half", [P, 1])
        gw1_sb = sb("gw1_sb", [P, DC, H2])
        gw2_sb = sb("gw2_sb", [P, H3])
        gw3_sb = sb("gw3_sb", [H3, 1])
        gb1_sb = sb("gb1_sb", [P, 1])
        gb2_sb = sb("gb2_sb", [H3, 1])
        gb3_f = sb("gb3_f", [P, 1])
        gb3_half = sb("gb3_half", [P, 1])
        range_f = sb("range_f", [P, 1])
        range_token = sb("range_token", [P, 1])
        range_global = sb("range_global", [P, 1])

        x_all = sb("x_all", [P, B * TILES, D])
        stats = sb("f_stats", [P, G, 6])
        moments = [sb(f"f_moments{n}", [P, G, 2]) for n in range(SLOTS)]
        var_eps = [sb(f"f_var_eps{n}", [P, G]) for n in range(SLOTS)]
        rstd = [sb(f"f_rstd{n}", [P, G]) for n in range(SLOTS)]
        x0 = [sb(f"x0_{n}", [P, G, D]) for n in range(SLOTS)]
        x0T_hi = sb("x0T_hi", [P, DC, G * P], F32R)
        x0T_lo = sb("x0T_lo", [P, DC, G * P], F32R)
        x0_sum = [sb(f"x0_sum{n}", [P, DC]) for n in range(SLOTS)]
        made = [sb(f"made{n}", [P, 2 * DC, G * P]) for n in range(SLOTS)]
        part_a = sb("part_a", [P, DC, G * P])
        part_b = [None] + [sb(f"part_b{c}", [P, DC, G * P]) for c in range(1, FFN_CYCLES)]
        mixed_sb = [None] + [sb(f"mixed{c}", [P, DC, G * P]) for c in range(1, FFN_CYCLES)]
        h1 = [sb(f"h1_{c}", [P, DC, G * P]) for c in range(FFN_CYCLES)]
        h2 = [sb(f"h2_{c}", [P, G * P]) for c in range(FFN_CYCLES)]
        h3 = [sb(f"h3_{c}", [P, G, H3]) for c in range(FFN_CYCLES)]
        h3_w4 = [sb(f"h3_w4_{c}", [P, G, H3]) for c in range(FFN_CYCLES)]
        logit = [sb(f"logit{c}", [P, G]) for c in range(FFN_CYCLES)]
        token_tanh = [sb(f"token_tanh{c}", [P, G]) for c in range(FFN_CYCLES)]
        coupling = [sb(f"coupling{c}", [P, G]) for c in range(FFN_CYCLES)]
        scaled = [sb(f"scaled{c}", [P, 2, G]) for c in range(FFN_CYCLES)]
        state = [[sb(f"state{c}_{n}", [P, 2, G]) for n in range(2)] for c in range(FFN_CYCLES)]
        minus_b = sb("minus_b", [P, G])
        gh1 = sb("gh1", [P, 1])
        gh2 = sb("gh2", [H3, 1])
        global_tanh = sb("global_tanh", [P, 1])
        base_coupling = [sb(f"base_coupling{n}", [P, 1]) for n in range(2)]
        y_part = sb("y_part", [P, D])

        made_ps = [psum(f"made_ps{n}", [P, G * P]) for n in range(3)]
        cycle_ps = [psum(f"cycle_ps{c}", [P, G * P]) for c in range(FFN_CYCLES)]
        spread_a_ps = psum("spread_a_ps", [P, G * P])
        global_ps = psum("global_ps", [P, G * P])

        f_loaded = sem("f_loaded")
        x2_loaded = [sem(f"x2_loaded{n}") for n in range(2)]
        f_zeroed = sem("f_zeroed")
        f_consts = sem("f_consts")
        f_hi = sem("f_hi")
        moments_ready = sem("f_moments_ready")
        var_ready = sem("f_var_ready")
        rstd_ready = sem("f_rstd_ready")
        x0_ready = sem("x0_ready")
        x0_turned = sem("x0_turned")
        x0T_hi_ready = sem("x0T_hi_ready")
        x0T_ready = sem("x0T_ready")
        made_done = sem("made_done")
        made_ready = sem("made_ready")
        global_done = sem("global_done")
        global_act = sem("global_act")
        base_ready = sem("base_ready")
        spread_done = cycle_sems("spread_done")
        parts_ready = cycle_sems("parts_ready")
        mix_ready = cycle_sems("mix_ready")
        h1_ready = cycle_sems("h1_ready")
        h2_done = cycle_sems("h2_done")
        h2_ready = cycle_sems("h2_ready")
        h3_done = cycle_sems("h3_done")
        h3_ready = cycle_sems("h3_ready")
        h3_w4_ready = cycle_sems("h3_w4_ready")
        logit_ready = cycle_sems("logit_ready")
        tanh_ready = cycle_sems("tanh_ready")
        coupling_ready = cycle_sems("coupling_ready")
        scaled_ready = cycle_sems("scaled_ready")
        state_ready = cycle_sems("state_ready")
        minus_b_ready = sem("minus_b_ready")
        y_part_ready = sem("y_part_ready")
        y_ready = sem("y_ready")
        y_stored = sem("y_stored")

        block = ctx.enter_context(nc.Block())

        loads = [
            (w1_f, w["cn_w1"].rearrange("(c p) n -> p c n", p=P)),
            (w2_sb, w["cn_w2"].rearrange("(c p) n -> p c n", p=P)),
            (w3_sb, w["cn_w3"]),
            (w4_sb, w["cn_w4"].rearrange("k n -> n k").partition_broadcast(P)),
            (b1_sb, w["cn_b1"].rearrange("(c p) -> p c", p=P)),
            (b2_sb, w["cn_b2"].rearrange("(p a) -> p a", a=1)),
            (b3_f, w["cn_b3"].rearrange("(a n) -> a n", a=1)),
            (b4_f, w["cn_b4"].rearrange("(a n) -> a n", a=1).partition_broadcast(P)),
            (gw1_sb, w["gc_w1"].rearrange("(c p) n -> p c n", p=P)),
            (gw2_sb, w["gc_w2"]),
            (gw3_sb, w["gc_w3"]),
            (gb1_sb, w["gc_b1"].rearrange("(p a) -> p a", a=1)),
            (gb2_sb, w["gc_b2"].rearrange("(p a) -> p a", a=1)),
            (gb3_f, w["gc_b3"].rearrange("(a n) -> a n", a=1).partition_broadcast(P)),
            (range_f, w["adaptive_range"].rearrange("(a n) -> a n", a=1).partition_broadcast(P)),
        ]

        @block.sync
        def _(sp):
            sp.dma_start(x_all[:, 0:TILES, :], x2_view[0]).then_inc(x2_loaded[0], 16)
            with nc.allow_non_contiguous_dma(reason="small vectors"):
                for dst, src in loads:
                    sp.dma_start(dst[:], src).then_inc(f_loaded, 16)
            for b in range(1, B):
                at_least(sp, x2_loaded[b % 2], 16 * (b // 2))
                sp.dma_start(x_all[:, b * TILES:(b + 1) * TILES, :],
                             x2_view[b]).then_inc(x2_loaded[b % 2], 16)
            with sp.Fori(0, NGROUPS) as m:
                sp.wait_ge(y_ready, m * (2 * G) + 2 * G)
                sp.dma_start(out_view[m], x_all[:, bass.ds(m * G, G), :]).then_inc(y_stored, 16)
            sp.wait_ge(y_stored, 16 * NGROUPS)

        @block.gpsimd
        def _(pool):
            pool.memset(ident[:], 0.0).then_inc(f_zeroed, 1)
            pool.memset(minus_half[:], -0.5).then_inc(f_zeroed, 1)
            pool.memset(ones[:], 1.0).then_inc(f_zeroed, 1)
            pool.memset(sign[:, 0:1], -1.0).then_inc(f_zeroed, 1)
            pool.memset(sign[:, 1:2], 1.0).then_inc(f_zeroed, 1)
            pool.wait_ge(f_zeroed, 5)
            pool.affine_select(out=ident[:], in_=ident[:], compare_op=ALU.not_equal, fill=1.0,
                               base=0, pattern=[[-1, P]], channel_multiplier=1).then_inc(f_consts, 1)
            for s in range(2):
                pool.affine_select(out=sign[:, s:s + 1], in_=sign[:, s:s + 1], compare_op=ALU.is_gt,
                                   fill=1.0 - 2.0 * s, base=BLOCK, pattern=[[0, 1]],
                                   channel_multiplier=-1).then_inc(f_consts, 1)
            pool.wait_ge(f_loaded, 16 * len(loads))

            def do(n, turn, r):
                for kind, ahead, rest in period_steps("gpsimd", n, r):
                    m, slot = n + ahead, (r + ahead) % SLOTS
                    if kind == "stats":
                        pool.wait_ge(var_ready, m + 1)
                        pool.tensor_tensor(rstd[slot][:], var_eps[slot][:],
                                           minus_half[:].to_broadcast([P, G]),
                                           ALU.pow).then_inc(rstd_ready, 1)
                    if kind == "mix":
                        c, = rest
                        pool.wait_ge(parts_ready[c], (m + 1) * c)
                        at_least(pool, h1_ready[c], m * DC)
                        other = made[slot][:, 0:DC, :] if c == 1 else part_a[:]
                        pool.tensor_tensor(mixed_sb[c][:], part_b[c][:], other,
                                           ALU.add).then_inc(mix_ready[c], 1)
                    if kind == "dot":
                        c, = rest
                        pool.wait_ge(h3_ready[c], m + 1)
                        at_least(pool, logit_ready[c], m)
                        pool.tensor_tensor(h3_w4[c][:], h3[c][:],
                                           w4_sb[:].unsqueeze(1).broadcast_to([P, G, H3]),
                                           ALU.mult).then_inc(h3_w4_ready[c], 1)

            walk_periods(pool, do)

        @block.scalar
        def _(act):
            act.wait_ge(f_loaded, 16 * len(loads))
            act.wait_ge(f_hi, 13)

            def do(n, turn, r):
                for kind, ahead, rest in period_steps("scalar", n, r):
                    m, slot = n + ahead, (r + ahead) % SLOTS
                    if kind == "turn":
                        c, = rest
                        act.wait_ge(x0_turned, m * DC + c + 1)
                        at_least(act, made_done, m * (2 * DC))
                        nc.scalar.activation(x0T_hi[:, c, :], made_ps[c][:], ACT.Copy,
                                             accum_out=x0_sum[slot][:, c:c + 1]
                                             ).then_inc(x0T_hi_ready, 1)
                    if kind == "product":
                        e, = rest
                        act.wait_ge(made_done, m * (2 * DC) + e + 1)
                        at_least(act, mix_ready[FFN_CYCLES - 1], m - SLOTS + 1)
                        nc.scalar.activation(made[slot][:, e, :], made_ps[(DC + e) % 3][:],
                                             ACT.Copy).then_inc(made_ready, 1)
                    if kind == "global":
                        s, = rest
                        batch = batch_of(turn, r, ahead)
                        act.wait_ge(global_done, batch * 3 + s + 1)
                        if s == 0:
                            nc.scalar.activation(gh1[:], global_ps[:, 0:1], ACT.Gelu,
                                                 bias=gb1_sb[:], scale=1.0 / T).then_inc(global_act, 1)
                        elif s == 1:
                            nc.scalar.activation(gh2[:], global_ps[0:H3, 1:2], ACT.Gelu,
                                                 bias=gb2_sb[:]).then_inc(global_act, 1)
                        else:
                            at_least(act, base_ready, batch)
                            nc.scalar.activation(global_tanh[:], global_ps[:, 2:3], ACT.Tanh,
                                                 bias=gb3_half[:], scale=0.5).then_inc(global_act, 1)
                    if kind == "gelu1":
                        c, = rest
                        if c == 0:
                            act.wait_ge(made_ready, m * (2 * DC) + DC)
                        else:
                            act.wait_ge(mix_ready[c], m + 1)
                        at_least(act, h2_done[c], m)
                        for k in range(DC):
                            src = made[slot][:, k, :] if c == 0 else mixed_sb[c][:, k, :]
                            nc.scalar.activation(h1[c][:, k, :], src, ACT.Gelu,
                                                 bias=b1_sb[:, k:k + 1]).then_inc(h1_ready[c], 1)
                    if kind == "h2":
                        c, = rest
                        act.wait_ge(h2_done[c], m + 1)
                        at_least(act, h3_done[c], m)
                        nc.scalar.activation(h2[c][:], cycle_ps[c][:], ACT.Gelu,
                                             bias=b2_sb[:]).then_inc(h2_ready[c], 1)
                    if kind == "h3":
                        c, = rest
                        act.wait_ge(h3_done[c], m + 1)
                        at_least(act, h3_w4_ready[c], m)
                        nc.scalar.activation(h3[c][:].rearrange("p t k -> p (t k)"),
                                             cycle_ps[c][:, 0:G * H3],
                                             ACT.Gelu).then_inc(h3_ready[c], 1)
                    if kind == "squash":
                        c, = rest
                        act.wait_ge(logit_ready[c], m + 1)
                        at_least(act, coupling_ready[c], m)
                        nc.scalar.activation(token_tanh[c][:], logit[c][:], ACT.Tanh,
                                             bias=b4_half[:], scale=0.5).then_inc(tanh_ready[c], 1)

            walk_periods(act, do)

        @block.vector
        def _(dve):
            dve.wait_ge(f_loaded, 16 * len(loads))
            dve.wait_ge(f_consts, 3)
            dve.tensor_copy(w1_hi[0][:], w1_f[:]).then_inc(f_hi, 1)
            dve.tensor_copy(b3_hi[:], b3_f[:]).then_inc(f_hi, 1)
            dve.tensor_copy(ones_r[:], ones[:]).then_inc(f_hi, 1)
            dve.wait_ge(f_hi, 3)
            dve.tensor_tensor(w1_lo[0][:], w1_f[:], w1_hi[0][:].bitcast(F32),
                              ALU.subtract).then_inc(f_hi, 1)
            dve.tensor_tensor(b3_lo[:], b3_f[:], b3_hi[:].bitcast(F32),
                              ALU.subtract).then_inc(f_hi, 1)
            dve.wait_ge(f_hi, 5)
            for dst, src in ((w1_hi[1], w1_hi[0]), (w1_lo[1], w1_lo[0])):
                for k in range(DC):
                    dve.tensor_scalar(dst[:, k, :], src[:, DC - 1 - k, :].bitcast(F32),
                                      sign[:, k:k + 1], None, ALU.mult).then_inc(f_hi, 1)
            for dst, src, by in ((b4_half, b4_f, 0.5), (gb3_half, gb3_f, 0.5),
                                 (range_token, range_f, 0.3), (range_global, range_f, 0.7)):
                dve.tensor_scalar(dst[:], src[:], by, None, ALU.mult).then_inc(f_hi, 1)

            dve.wait_ge(f_hi, 13)

            def do(n, turn, r):
                for kind, ahead, rest in period_steps("vector", n, r):
                    m, slot = n + ahead, (r + ahead) % SLOTS
                    if kind == "stats":
                        batch_parity = slot // 2
                        dve.wait_ge(x2_loaded[batch_parity], (turn + (r + ahead) // SLOTS) * 16 + 16)
                        at_least(dve, moments_ready, m * G)
                        for t in range(G):
                            dve.bn_stats(stats[:, t, :], x_tile(m, t))
                        dve.drain()
                        for t in range(G):
                            dve.bn_aggr(moments[slot][:, t, :], stats[:, t, :]).then_inc(moments_ready, 1)
                        dve.wait_ge(moments_ready, m * G + G)
                        dve.tensor_scalar(var_eps[slot][:], moments[slot][:, :, 1], EPS, None,
                                          ALU.add).then_inc(var_ready, 1)
                    if kind == "scale":
                        dve.wait_ge(rstd_ready, m + 1)
                        at_least(dve, x0_turned, (m - SLOTS + 1) * DC)
                        at_least(dve, y_ready, (m - SLOTS + 1) * (2 * G))
                        for t in range(G):
                            dve.tensor_scalar(x0[slot][:, t, :], x_tile(m, t),
                                              moments[slot][:, t, 0:1], rstd[slot][:, t:t + 1],
                                              ALU.subtract, ALU.mult).then_inc(x0_ready, 1)
                    if kind == "turn":
                        c, = rest
                        dve.wait_ge(x0T_hi_ready, m * DC + c + 1)
                        dve.tensor_tensor(x0T_lo[:, c, :], made_ps[c][:], x0T_hi[:, c, :].bitcast(F32),
                                          ALU.subtract).then_inc(x0T_ready, 1)
                    if kind == "global" and rest[0] == 2:
                        batch = batch_of(turn, r, ahead)
                        dve.wait_ge(global_act, batch * 3 + 3)
                        dve.tensor_scalar(base_coupling[slot // 2][:], global_tanh[:],
                                          range_global[:], 0.1, ALU.mult,
                                          ALU.add).then_inc(base_ready, 1)
                    if kind == "mix":
                        c, = rest
                        dve.wait_ge(spread_done[c], m + 1)
                        at_least(dve, mix_ready[c], m)
                        if c == FFN_CYCLES - 1:
                            dve.tensor_tensor(part_a[:],
                                              spread_a_ps[:].unsqueeze(1).broadcast_to([P, DC, G * P]),
                                              made[slot][:, 0:DC, :], ALU.mult).then_inc(parts_ready[c], 1)
                        dve.tensor_tensor(part_b[c][:],
                                          cycle_ps[c][:].unsqueeze(1).broadcast_to([P, DC, G * P]),
                                          made[slot][:, DC:, :], ALU.mult).then_inc(parts_ready[c], 1)
                    if kind == "dot":
                        c, = rest
                        dve.wait_ge(h3_w4_ready[c], m + 1)
                        at_least(dve, tanh_ready[c], m)
                        dve.tensor_reduce(logit[c][:], h3_w4[c][:], AX_X, ALU.add).then_inc(logit_ready[c], 1)
                    if kind == "squash":
                        c, = rest
                        if c == 0:
                            dve.wait_ge(base_ready, batch_of(turn, r, ahead) + 1)
                        update_state(c, m, slot)
                    if kind == "final":
                        t, = rest
                        a_b = state[FFN_CYCLES - 1][slot % 2]
                        if t == 0:
                            dve.wait_ge(minus_b_ready, m + 1)
                        at_least(dve, y_ready, (m * G + t) * 2)
                        dve.scalar_tensor_tensor(out=y_part[:], in0=x0[slot][:, t, :],
                                                 scalar=a_b[:, 0, t:t + 1], in1=x_tile(m, t),
                                                 op0=ALU.mult, op1=ALU.add).then_inc(y_part_ready, 1)
                        dve.wait_ge(y_part_ready, m * G + t + 1)
                        y = x_tile(m, t).rearrange("p (k d) -> p k d", d=BLOCK)
                        y_in = y_part[:].rearrange("p (k d) -> p k d", d=BLOCK)
                        source = x0[slot][:, t, :].rearrange("p (k d) -> p k d", d=BLOCK)
                        dve.scalar_tensor_tensor(out=y[:, 0:4:3, :], in0=source[:, 2:0:-1, :],
                                                 scalar=a_b[:, 1, t:t + 1], in1=y_in[:, 0:4:3, :],
                                                 op0=ALU.mult, op1=ALU.add).then_inc(y_ready, 1)
                        dve.scalar_tensor_tensor(out=y[:, 1:3, :], in0=source[:, 3::-3, :],
                                                 scalar=minus_b[:, t:t + 1], in1=y_in[:, 1:3, :],
                                                 op0=ALU.mult, op1=ALU.add).then_inc(y_ready, 1)

            def x_tile(m, t):
                if isinstance(m, int):
                    return x_all[:, m * G + t, :]
                return x_all[:, bass.ds(m * G + t, 1), :].rearrange("p a f -> p (a f)")

            def update_state(c, m, slot):
                new = state[c][slot % 2]
                old = state[c - 1][slot % 2]
                dve.wait_ge(tanh_ready[c], m + 1)
                if c == 0:
                    at_least(dve, spread_done[1], m - 1)
                    at_least(dve, coupling_ready[0], m)
                    dve.tensor_scalar(new[:, 1, :], token_tanh[c][:], range_token[:],
                                      base_coupling[slot // 2][:], ALU.mult,
                                      ALU.add).then_inc(coupling_ready[0], 1)
                    return
                at_least(dve, state_ready[c], m * 2)
                dve.tensor_scalar(coupling[c][:], token_tanh[c][:], range_token[:],
                                  base_coupling[slot // 2][:], ALU.mult,
                                  ALU.add).then_inc(coupling_ready[c], 1)
                dve.wait_ge(coupling_ready[c], m + 1)
                if c == 1:
                    dve.wait_ge(coupling_ready[0], m + 1)
                    dve.tensor_tensor(scaled[c][:, 0, :], old[:, 1, :], coupling[c][:],
                                      ALU.mult).then_inc(scaled_ready[c], 1)
                    dve.wait_ge(scaled_ready[c], m + 1)
                    at_least(dve, spread_done[2], m - 1)
                    dve.tensor_tensor(new[:, 1, :], old[:, 1, :], coupling[c][:],
                                      ALU.add).then_inc(state_ready[c], 1)
                    dve.tensor_scalar(new[:, 0, :], scaled[c][:, 0, :], -1.0, 1.0, ALU.mult,
                                      ALU.add).then_inc(state_ready[c], 1)
                    return
                dve.wait_ge(state_ready[1], m * 2 + 2)
                dve.tensor_tensor(scaled[c][:], old[:],
                                  coupling[c][:].unsqueeze(1).broadcast_to([P, 2, G]),
                                  ALU.mult).then_inc(scaled_ready[c], 1)
                dve.wait_ge(scaled_ready[c], m + 1)
                at_least(dve, y_ready, m * (2 * G))
                dve.tensor_tensor(new[:, 0, :], old[:, 0, :], scaled[c][:, 1, :],
                                  ALU.subtract).then_inc(state_ready[c], 1)
                dve.tensor_tensor(new[:, 1, :], old[:, 1, :], scaled[c][:, 0, :],
                                  ALU.add).then_inc(state_ready[c], 1)
                dve.wait_ge(state_ready[c], m * 2 + 2)
                dve.tensor_scalar(minus_b[:], new[:, 1, :], -1.0, None,
                                  ALU.mult).then_inc(minus_b_ready, 1)

            walk_periods(dve, do)

        @block.tensor
        def _(pe):
            pe.wait_ge(f_hi, 13)
            pe.wait_ge(f_consts, 3)

            def do(n, turn, r):
                for kind, ahead, rest in period_steps("tensor", n, r):
                    m, slot = n + ahead, (r + ahead) % SLOTS
                    if kind == "turn":
                        c, = rest
                        pe.wait_ge(x0_ready, m * G + G)
                        at_least(pe, made_ready, (m - 1) * (2 * DC) + c + 2)
                        for t in range(G):
                            mm = nc.tensor.transpose(made_ps[c][:, t * P:(t + 1) * P],
                                                     x0[slot][:, t, c * P:(c + 1) * P], ident[:])
                        mm.then_inc(x0_turned, 1)
                    if kind == "product":
                        e, = rest
                        which, chunk = divmod(e, DC)
                        pe.wait_ge(x0T_ready, m * DC + DC)
                        if e == 0:
                            at_least(pe, made_ready, m * (2 * DC))
                        if e == 3:
                            pe.wait_ge(made_ready, m * (2 * DC) + 1)
                        cols = slice(chunk * P, (chunk + 1) * P)
                        ps = made_ps[(DC + e) % 3]
                        for k in range(DC):
                            hi, lo = w1_hi[which][:, k, cols], w1_lo[which][:, k, cols]
                            nc.tensor.matmul(ps[:], hi, x0T_hi[:, k, :], start=k == 0, stop=False)
                            nc.tensor.matmul(ps[:], hi, x0T_lo[:, k, :], start=False, stop=False)
                            mm = nc.tensor.matmul(ps[:], lo, x0T_hi[:, k, :], start=False,
                                                  stop=k == DC - 1)
                        mm.then_inc(made_done, 1)
                    if kind == "global":
                        s, = rest
                        batch = batch_of(turn, r, ahead)
                        if s == 0:
                            pe.wait_ge(x0T_hi_ready, m * DC + DC)
                            at_least(pe, global_act, batch * 3)
                            for k in range(DC):
                                for half, of in enumerate(((slot - 1) % SLOTS, slot)):
                                    mm = nc.tensor.matmul(global_ps[:, 0:1], gw1_sb[:, k, :],
                                                          x0_sum[of][:, k:k + 1],
                                                          start=k + half == 0, stop=k + half == DC)
                        elif s == 1:
                            pe.wait_ge(global_act, batch * 3 + 1)
                            mm = nc.tensor.matmul(global_ps[0:H3, 1:2], gw2_sb[:], gh1[:],
                                                  start=True, stop=True)
                        else:
                            pe.wait_ge(global_act, batch * 3 + 2)
                            mm = nc.tensor.matmul(global_ps[:, 2:3],
                                                  gw3_sb[:].to_broadcast([H3, P]), gh2[:],
                                                  start=True, stop=True)
                        mm.then_inc(global_done, 1)
                    if kind == "spread":
                        c, = rest
                        a_b = state[c - 1][slot % 2]
                        if c == 1:
                            pe.wait_ge(coupling_ready[0], m + 1)
                        else:
                            pe.wait_ge(state_ready[c - 1], m * 2 + 2)
                            at_least(pe, parts_ready[c], m * c)
                        at_least(pe, h3_ready[c], m)
                        for which in range(2 if c == 2 else 1):
                            ps = spread_a_ps if c == 2 and which == 0 else cycle_ps[c]
                            part = 0 if ps is spread_a_ps else 1
                            for t in range(G):
                                mm = nc.tensor.transpose(ps[:, t * P:(t + 1) * P],
                                                         a_b[:, part, t:t + 1].to_broadcast([P, P]),
                                                         ident[:])
                        mm.then_inc(spread_done[c], 1)
                    if kind == "h2":
                        c, = rest
                        pe.wait_ge(h1_ready[c], m * DC + DC)
                        if c == 0:
                            at_least(pe, h3_ready[c], m)
                        for k in range(DC):
                            mm = nc.tensor.matmul(cycle_ps[c][:], w2_sb[:, k, :], h1[c][:, k, :],
                                                  start=k == 0, stop=k == DC - 1)
                        mm.then_inc(h2_done[c], 1)
                    if kind == "h3":
                        c, = rest
                        pe.wait_ge(h2_ready[c], m + 1)
                        ps = cycle_ps[c][:, 0:G * H3]
                        for part, b3 in enumerate((b3_hi, b3_lo)):
                            nc.tensor.matmul(ps.rearrange("p (t k) -> p t k", k=H3), ones_r[:],
                                             b3[:].unsqueeze(1).broadcast_to([1, G, H3]),
                                             start=part == 0, stop=False)
                        for t in range(G):
                            mm = nc.tensor.matmul(ps[:, t * H3:(t + 1) * H3],
                                                  h2[c][:, t * P:(t + 1) * P], w3_sb[:],
                                                  start=False, stop=t == G - 1)
                        mm.then_inc(h3_done[c], 1)

            walk_periods(pe, do)


def rope_tables():
    import numpy as np
    positions = np.arange(0, HS, 2, dtype=np.float32)
    theta = (np.float32(10000.0) ** (np.float32(-2.0) * positions / np.float32(HS))).astype(np.float32)
    angles = (np.arange(T, dtype=np.float32)[:, None] * theta[None, :]).astype(np.float64)
    scale = HS ** -0.25
    cos, sin = np.cos(angles) * scale, np.sin(angles) * scale
    return cos.astype(np.float32), np.concatenate([-sin, sin], axis=1).astype(np.float32)


WEIGHTS = ["cn_w1", "cn_b1", "cn_w2", "cn_b2", "cn_w3", "cn_b3", "cn_w4", "cn_b4", "gc_w1",
           "gc_b1", "gc_w2", "gc_b2", "gc_w3", "gc_b3", "adaptive_range"]


def kernel(**inputs):
    import numpy as np
    import concourse.bacc as bacc
    from concourse.bass_utils import run_bass_kernel_spmd

    def halves(w):
        return np.concatenate([w[0::2], w[1::2]], axis=0)

    wq, wk, wv = (np.asarray(inputs[f"L0_attn_W{n}"]) for n in "qkv")
    wqkv = np.concatenate([halves(wq[0]), halves(wq[1]), halves(wk), wv], axis=0).T
    cos_t, sin_t = rope_tables()
    arrays = {"x": np.ascontiguousarray(inputs["L0_attn_x"]), "wqkv": np.ascontiguousarray(wqkv),
              "wo": np.ascontiguousarray(np.asarray(inputs["L0_attn_Wo"]).T),
              "cos_t": cos_t, "sin_t": sin_t}
    arrays.update({n: np.ascontiguousarray(inputs[f"L0_ffn_{n}"]) for n in WEIGHTS})
    nc = bacc.Bacc("TRN2", target_bir_lowering=False, num_devices=1)
    ins = {name: nc.dram_tensor(name, a.shape, F32, kind="ExternalInput").ap()
           for name, a in arrays.items()}
    x2 = nc.dram_tensor("x2", (B, T, D), F32, kind="Internal").ap()
    out = nc.dram_tensor("out", (B, T, D), F32, kind="ExternalOutput").ap()
    attention_phase(nc, *(ins[n] for n in ("x", "wqkv", "wo", "cos_t", "sin_t")), x2)
    ffn_phase(nc, x2, ins, out)
    r = run_bass_kernel_spmd(nc, [arrays], core_ids=[0])
    return r.results[0]["out"]
```

```python
from contextlib import ExitStack

import concourse.bass as bass
from concourse import mybir

F32 = mybir.dt.float32
F32R = mybir.dt.float32r
BF16 = mybir.dt.bfloat16
ALU = mybir.AluOpType
ACT = mybir.ActivationFunctionType
AX_X = mybir.AxisListType.X

P = 128
B, T, D = 8, 1024, 256
HS, NH = 128, 2
TILES = T // P
G = 4
GROUPS = TILES // G
DC = D // P
EPS = 1e-5
MASKED = -1e30
HALF = HS // 2
FFN_CYCLES = 3
H2, H3 = D // 2, D // 4
BLOCK = D // 4
BIAS_ROWS = 33
SLOTS = 4
IN_PLACE = 2

UNITS = [(g, h) for g in range(GROUPS) for h in range(NH)]
STEPS = [G * (g + 1) for g, h in UNITS]
FIRST_STEP = [sum(STEPS[:u]) for u in range(len(UNITS))]
BATCH_STEPS = sum(STEPS)
BATCH_SCORES = len(UNITS) * G


def at_least(engine, semaphore, value):
    if isinstance(value, int) and value <= 0:
        return
    engine.wait_ge(semaphore, value)


BATCH_PERIODS = {
    "tensor": [
        ("turn_p", -1, 3, 2), ("scores", 0, 0, 2), ("scores", 0, 0, 3), ("turn_p", -1, 3, 3),
        ("attend", -1, 3, 0), ("turn_p", -1, 3, 4), ("attend", -1, 3, 1), ("turn_p", -1, 3, 5),
        ("attend", -1, 3, 2), ("turn_p", -1, 3, 6), ("attend", -1, 3, 3), ("project", 0, 1, 2),
        ("turn_p", -1, 3, 7), ("attend", -1, 3, 4), ("scores", 0, 1, 0), ("turn_p", 0, 0, 0),
        ("attend", -1, 3, 5), ("attend", -1, 3, 6), ("attend", -1, 3, 7), ("turn_p", 0, 0, 1),
        ("project", 0, 1, 3), ("scores", 0, 1, 1), ("turn_p", 0, 0, 2), ("turn_p", 0, 0, 3),
        ("scores", 0, 1, 2), ("output", -1, 1, 0), ("output", -1, 1, 1), ("attend", 0, 0, 0),
        ("output", -1, 1, 2), ("scores", 0, 1, 3), ("turn_qk", 0, 1, 0), ("turn_qk", 0, 1, 1),
        ("attend", 0, 0, 1), ("turn_qk", 0, 1, 2), ("attend", 0, 0, 2), ("attend", 0, 0, 3),
        ("output", -1, 1, 3), ("turn_x", 1, 0, 0), ("turn_x", 1, 0, 1), ("scores", 0, 2, 0),
        ("scores", 0, 2, 1), ("turn_p", 0, 1, 0), ("turn_p", 0, 1, 1), ("project", 1, 0, 0),
        ("scores", 0, 2, 2), ("scores", 0, 2, 3), ("attend", 0, 1, 0), ("project", 1, 0, 1),
        ("turn_p", 0, 1, 2), ("project", 1, 0, 2), ("turn_p", 0, 1, 3), ("attend", 0, 1, 1),
        ("scores", 0, 3, 0), ("attend", 0, 1, 2), ("attend", 0, 1, 3), ("project", 1, 0, 3),
        ("turn_p", 0, 2, 0), ("turn_p", 0, 2, 1), ("turn_p", 0, 2, 2), ("scores", 0, 3, 1),
        ("turn_p", 0, 2, 3), ("attend", 0, 2, 0), ("output", 0, 0, 0), ("turn_p", 0, 2, 4),
        ("attend", 0, 2, 1), ("scores", 0, 3, 2), ("output", 0, 0, 1), ("output", 0, 0, 2),
        ("turn_p", 0, 2, 5), ("scores", 0, 3, 3), ("turn_p", 0, 2, 6), ("attend", 0, 2, 2),
        ("attend", 0, 2, 3), ("turn_p", 0, 2, 7), ("output", 0, 0, 3), ("turn_qk", 1, 0, 0),
        ("turn_qk", 1, 0, 1), ("attend", 0, 2, 4), ("turn_qk", 1, 0, 2), ("attend", 0, 2, 5),
        ("turn_x", 1, 1, 0), ("turn_x", 1, 1, 1), ("attend", 0, 2, 6), ("turn_p", 0, 3, 0),
        ("attend", 0, 2, 7), ("scores", 1, 0, 0), ("scores", 1, 0, 1), ("turn_p", 0, 3, 1),
        ("project", 1, 1, 0), ("project", 1, 1, 1),
    ],
    "scalar": [
        ("scores", 0, 0, 1), ("project", 0, 1, 1), ("turn_p", -1, 3, 1), ("turn_p", -1, 3, 2),
        ("turn_p", -1, 3, 3), ("turn_p", -1, 3, 4), ("turn_p", -1, 3, 5), ("scores", 0, 0, 2),
        ("turn_p", -1, 3, 6), ("scores", 0, 0, 3), ("turn_p", -1, 3, 7), ("project", 0, 1, 2),
        ("turn_p", 0, 0, 0), ("scores", 0, 1, 0), ("turn_p", 0, 0, 1), ("close", -1, 3),
        ("project", 0, 1, 3), ("turn_p", 0, 0, 2), ("turn_p", 0, 0, 3), ("scores", 0, 1, 1),
        ("scores", 0, 1, 2), ("turn_qk", 0, 1, 0), ("turn_qk", 0, 1, 1), ("turn_qk", 0, 1, 2),
        ("scores", 0, 1, 3), ("turn_x", 1, 0, 0), ("turn_x", 1, 0, 1), ("close", 0, 0),
        ("scores", 0, 2, 0), ("turn_p", 0, 1, 0), ("scores", 0, 2, 1), ("turn_p", 0, 1, 1),
        ("scores", 0, 2, 2), ("project", 1, 0, 0), ("project", 1, 0, 1), ("turn_p", 0, 1, 2),
        ("turn_p", 0, 1, 3), ("project", 1, 0, 2), ("scores", 0, 2, 3), ("close", 0, 1),
        ("project", 1, 0, 3), ("turn_p", 0, 2, 0), ("turn_p", 0, 2, 1), ("turn_p", 0, 2, 2),
        ("turn_p", 0, 2, 3), ("scores", 0, 3, 0), ("scores", 0, 3, 1), ("turn_p", 0, 2, 4),
        ("turn_p", 0, 2, 5), ("scores", 0, 3, 2), ("turn_p", 0, 2, 6), ("turn_p", 0, 2, 7),
        ("scores", 0, 3, 3), ("turn_qk", 1, 0, 0), ("turn_qk", 1, 0, 1), ("turn_qk", 1, 0, 2),
        ("turn_x", 1, 1, 0), ("turn_x", 1, 1, 1), ("turn_p", 0, 3, 0), ("close", 0, 2),
        ("scores", 1, 0, 0), ("project", 1, 1, 0),
    ],
    "vector": [
        ("scores", 0, 0, 0), ("turn_p", -1, 3, 0), ("scores", 0, 0, 1), ("norm", 1, 0),
        ("close", -1, 2), ("project", 0, 1, 0), ("turn_p", -1, 3, 1), ("turn_p", -1, 3, 2),
        ("project", 0, 1, 1), ("turn_p", -1, 3, 3), ("scores", 0, 0, 2), ("turn_p", -1, 3, 4),
        ("scores", 0, 0, 3), ("turn_p", -1, 3, 5), ("turn_p", -1, 3, 6), ("turn_p", -1, 3, 7),
        ("scores", 0, 1, 0), ("project", 0, 1, 2), ("scale", 1, 0), ("turn_p", 0, 0, 0),
        ("turn_p", 0, 0, 1), ("close", -1, 3), ("scores", 0, 1, 1), ("project", 0, 1, 3),
        ("turn_p", 0, 0, 2), ("turn_p", 0, 0, 3), ("scores", 0, 1, 2), ("output", -1, 1, 0),
        ("output", -1, 1, 1), ("output", -1, 1, 2), ("scores", 0, 1, 3), ("turn_qk", 0, 1, 0),
        ("turn_qk", 0, 1, 1), ("turn_qk", 0, 1, 2), ("output", -1, 1, 3), ("turn_x", 1, 0, 0),
        ("turn_x", 1, 0, 1), ("scores", 0, 2, 0), ("scores", 0, 2, 1), ("close", 0, 0),
        ("turn_p", 0, 1, 0), ("scores", 0, 2, 2), ("turn_p", 0, 1, 1), ("norm", 1, 1),
        ("scores", 0, 2, 3), ("project", 1, 0, 0), ("project", 1, 0, 1), ("turn_p", 0, 1, 2),
        ("turn_p", 0, 1, 3), ("project", 1, 0, 2), ("scores", 0, 3, 0), ("scale", 1, 1),
        ("close", 0, 1), ("project", 1, 0, 3), ("turn_p", 0, 2, 0), ("turn_p", 0, 2, 1),
        ("turn_p", 0, 2, 2), ("scores", 0, 3, 1), ("turn_p", 0, 2, 3), ("output", 0, 0, 0),
        ("turn_p", 0, 2, 4), ("scores", 0, 3, 2), ("output", 0, 0, 1), ("output", 0, 0, 2),
        ("turn_p", 0, 2, 5), ("scores", 0, 3, 3), ("turn_p", 0, 2, 6), ("turn_p", 0, 2, 7),
        ("output", 0, 0, 3), ("turn_qk", 1, 0, 0), ("turn_qk", 1, 0, 1), ("turn_qk", 1, 0, 2),
        ("turn_x", 1, 1, 0), ("turn_x", 1, 1, 1),
    ],
    "gpsimd": [
        ("project", -1, 1, 1), ("norm", 0, 0), ("project", -1, 1, 2), ("project", -1, 1, 3),
        ("norm", 0, 1), ("project", 0, 0, 0), ("project", 0, 0, 1), ("project", 0, 0, 2),
        ("project", 0, 0, 3), ("project", 0, 1, 0),
    ],
}


BANKS = 3
BANK_USERS = ("turn_x", "project", "turn_qk", "turn_p", "output")
USES = [step for step in BATCH_PERIODS["tensor"] if step[0] in BANK_USERS]
BANK_OF = {(kind, *rest): n % BANKS for n, (kind, ahead, *rest) in enumerate(USES)}
LAST_USERS = {BANK_OF[(kind, *rest)]: (kind, ahead, *rest) for kind, ahead, *rest in USES}
assert all(ahead >= 0 for kind, ahead, *rest in LAST_USERS.values())


def batch_steps(engine_name, b):
    for kind, ahead, *rest in BATCH_PERIODS[engine_name]:
        if isinstance(b, int) and not 0 <= b + ahead < B:
            continue
        yield kind, ahead, rest


def walk_batches(engine, do):
    for b in (-1, 0):
        do(b, b // 2, b % 2)
    with engine.Fori(0, (B - 2) // 2) as pair:
        do(pair * 2 + 1, pair, 1)
        do(pair * 2 + 2, pair + 1, 0)
    for b in (B - 1, B):
        do(b, b // 2, b % 2)


class SharedTensors:

    def __init__(self, nc, ctx):
        def sb(name, shape, dt=F32):
            return ctx.enter_context(nc.sbuf_tensor(name, shape, dt))

        self.x_all = sb("x_all", [P, B * TILES, D])
        self.ident = sb("ident", [P, P])
        self.minus_half = sb("minus_half", [P, 1])
        self.sign = sb("sign", [P, 2])
        self.ones = sb("ones", [BIAS_ROWS, P])
        self.ones_r = sb("ones_r", [BIAS_ROWS, P], F32R)
        self.w1_hi = [sb(f"w1_hi{n}", [P, DC, D], F32R) for n in range(2)]
        self.w1_lo = [sb(f"w1_lo{n}", [P, DC, D], F32R) for n in range(2)]
        self.w2_sb = sb("w2_sb", [P, DC, H2])
        self.w3_sb = sb("w3_sb", [P, H3])
        self.w4_sb = sb("w4_sb", [P, H3])
        self.b1_sb = sb("b1_sb", [P, DC])
        self.b2_sb = sb("b2_sb", [P, 1])
        self.b3_f = sb("b3_f", [BIAS_ROWS, H3])
        self.b3_parts = sb("b3_parts", [BIAS_ROWS, H3], F32R)
        self.b4_f = sb("b4_f", [P, 1])
        self.b4_half = sb("b4_half", [P, 1])
        self.gw1_sb = sb("gw1_sb", [P, DC, H2])
        self.gw2_sb = sb("gw2_sb", [P, H3])
        self.gw3_sb = sb("gw3_sb", [H3, 1])
        self.gb1_sb = sb("gb1_sb", [P, 1])
        self.gb2_sb = sb("gb2_sb", [H3, 1])
        self.gb3_f = sb("gb3_f", [P, 1])
        self.gb3_half = sb("gb3_half", [P, 1])
        self.range_f = sb("range_f", [P, 1])
        self.range_token = sb("range_token", [P, 1])
        self.range_global = sb("range_global", [P, 1])
        self.stats = sb("f_stats", [P, G, 6])
        self.moments = [sb(f"f_moments{n}", [P, G, 2]) for n in range(SLOTS)]
        self.var_eps = [sb(f"f_var_eps{n}", [P, G]) for n in range(SLOTS)]
        self.rstd = [sb(f"f_rstd{n}", [P, G]) for n in range(SLOTS)]
        self.first_x0 = sb("x0_0", [P, G, D])
        self.moments_ready = ctx.enter_context(nc.semaphore("f_moments_ready"))
        self.var_ready = ctx.enter_context(nc.semaphore("f_var_ready"))
        self.rstd_ready = ctx.enter_context(nc.semaphore("f_rstd_ready"))
        self.x0_ready = ctx.enter_context(nc.semaphore("x0_ready"))


def ffn_moments(dve, f, m, slot, x_tiles):
    at_least(dve, f.moments_ready, m * G)
    for t in range(G):
        dve.bn_stats(f.stats[:, t, :], x_tiles[t])
    dve.drain()
    for t in range(G):
        dve.bn_aggr(f.moments[slot][:, t, :], f.stats[:, t, :]).then_inc(f.moments_ready, 1)
    dve.wait_ge(f.moments_ready, m * G + G)
    dve.tensor_scalar(f.var_eps[slot][:], f.moments[slot][:, :, 1], EPS, None,
                      ALU.add).then_inc(f.var_ready, 1)


def ffn_rstd(pool, f, m, slot):
    pool.wait_ge(f.var_ready, m + 1)
    pool.tensor_tensor(f.rstd[slot][:], f.var_eps[slot][:], f.minus_half[:].to_broadcast([P, G]),
                       ALU.pow).then_inc(f.rstd_ready, 1)


def ffn_scale(dve, f, m, slot, x0, x_tiles):
    dve.wait_ge(f.rstd_ready, m + 1)
    for t in range(G):
        dve.tensor_scalar(x0[:, t, :], x_tiles[t], f.moments[slot][:, t, 0:1],
                          f.rstd[slot][:, t:t + 1], ALU.subtract, ALU.mult).then_inc(f.x0_ready, 1)


def ffn_weight_loads(f, w):
    return [
        (f.w2_sb, w["cn_w2"].rearrange("(c p) n -> p c n", p=P)),
        (f.w3_sb, w["cn_w3"]),
        (f.w4_sb, w["cn_w4"].rearrange("k n -> n k").partition_broadcast(P)),
        (f.b1_sb, w["cn_b1"].rearrange("(c p) -> p c", p=P)),
        (f.b2_sb, w["cn_b2"].rearrange("(p a) -> p a", a=1)),
        (f.b3_f[0:1, :], w["cn_b3"].rearrange("(a n) -> a n", a=1)),
        (f.b3_f[BIAS_ROWS - 1:, :], w["cn_b3"].rearrange("(a n) -> a n", a=1)),
        (f.b4_f, w["cn_b4"].rearrange("(a n) -> a n", a=1).partition_broadcast(P)),
        (f.gw1_sb, w["gc_w1"].rearrange("(c p) n -> p c n", p=P)),
        (f.gw2_sb, w["gc_w2"]),
        (f.gw3_sb, w["gc_w3"]),
        (f.gb1_sb, w["gc_b1"].rearrange("(p a) -> p a", a=1)),
        (f.gb2_sb, w["gc_b2"].rearrange("(p a) -> p a", a=1)),
        (f.gb3_f, w["gc_b3"].rearrange("(a n) -> a n", a=1).partition_broadcast(P)),
        (f.range_f, w["adaptive_range"].rearrange("(a n) -> a n", a=1).partition_broadcast(P)),
    ]


def attention_phase(nc, f, x, wqkv, wo, cos_t, sin_t, w, x2):
    x_view = x.rearrange("b (i p) f -> b p i f", p=P)
    x2_view = x2.rearrange("b (i p) f -> b p i f", p=P)
    with ExitStack() as ctx:
        def sb(name, shape, dt=F32):
            return ctx.enter_context(nc.sbuf_tensor(name, shape, dt))

        def psum(name, shape):
            return ctx.enter_context(nc.psum_tensor(name, shape, F32))

        def sem(name):
            return ctx.enter_context(nc.semaphore(name))

        x_columns = f.x_all[:].rearrange("p t d -> p (t d)")
        pieces = iter(range(IN_PLACE * TILES * D, B * TILES * D, G * P))

        def room(count):
            start = [next(pieces) for _ in range(count)][0]
            return x_columns[:, start:start + count * G * P]

        probs = [room(TILES).rearrange("p (t k) -> p t k", k=T) for n in range(2)]
        xn = [room(DC).rearrange("p (t d) -> p t d", d=D) for n in range(GROUPS)]
        qkv = [room(1) for t in range(G)]
        wqkv_f = probs[1][:, 0, :].rearrange("p (c n) -> p c n", c=DC)
        wo_f = probs[1][:, 1, 0:NH * D].rearrange("p (c n) -> p c n", c=NH)
        w1_f = probs[1][:, 2, 0:DC * D].rearrange("p (c n) -> p c n", c=DC)
        ident, minus_half = f.ident, f.minus_half
        ident_b = sb("ident_b", [P, P], BF16)
        mask_b = sb("mask_b", [P, P], BF16)
        wqkv_hi = sb("wqkv_hi", [P, DC, 4 * HS], F32R)
        wqkv_lo = sb("wqkv_lo", [P, DC, 4 * HS], F32R)
        wo_hi = sb("wo_hi", [P, NH, D], F32R)
        wo_lo = sb("wo_lo", [P, NH, D], F32R)
        cos_sb = sb("cos_sb", [P, TILES, HALF])
        sin_sb = sb("sin_sb", [P, TILES, HS])
        xt = [f.x_all[:, n * TILES:(n + 1) * TILES, :] for n in range(2)]
        stats = sb("stats", [P, G, 6])
        moments = [sb(f"moments{n}", [P, G, 2]) for n in range(GROUPS)]
        var_eps = [sb(f"var_eps{n}", [P, G]) for n in range(GROUPS)]
        rstd = [sb(f"rstd{n}", [P, G]) for n in range(GROUPS)]
        xnT_hi = sb("xnT_hi", [P, DC, G * P], F32R)
        xnT_lo = sb("xnT_lo", [P, DC, G * P], F32R)
        rope_a = sb("rope_a", [P, 3 * HS])
        rope_b = sb("rope_b", [P, 3 * HS])
        rot = sb("rot", [P, G, 3 * HS])
        q_hi = [[sb(f"q_hi{g}{h}", [P, G * P], F32R) for h in range(NH)] for g in range(GROUPS)]
        q_lo = [[sb(f"q_lo{g}{h}", [P, G * P], F32R) for h in range(NH)] for g in range(GROUPS)]
        k_hi = [sb(f"k_hi{n}", [P, T], F32R) for n in range(2)]
        k_lo = [sb(f"k_lo{n}", [P, T], F32R) for n in range(2)]
        v_hi = [sb(f"v_hi{n}", [P, TILES, HS], F32R) for n in range(2)]
        v_lo = [sb(f"v_lo{n}", [P, TILES, HS], F32R) for n in range(2)]
        neg_max = sb("neg_max", [P, BATCH_SCORES])
        row_sum = [sb(f"row_sum{n}", [P, BATCH_SCORES]) for n in range(2)]
        inv_sum = sb("inv_sum", [P, NH * G])
        PT_RING = 4
        pT_hi = [sb(f"pT_hi{n}", [P, G * P], F32R) for n in range(PT_RING)]
        pT_lo = [sb(f"pT_lo{n}", [P, G * P], F32R) for n in range(PT_RING)]
        oT_hi = [sb(f"oT_hi{h}", [P, G * P], F32R) for h in range(NH)]
        oT_lo = [sb(f"oT_lo{h}", [P, G * P], F32R) for h in range(NH)]
        x_plus = sb("x_plus", [P, D])

        scores_ps = [psum(f"scores_ps{n}", [P, T]) for n in range(2)]
        bank = [psum(f"bank{n}", [P, G * P]) for n in range(BANKS)]
        oT_ps = psum("oT_ps", [P, G * P])

        x_loaded = [[sem(f"x_loaded{n}{g}") for g in range(GROUPS)] for n in range(2)]
        wqkv_loaded = sem("wqkv_loaded")
        wo_loaded = sem("wo_loaded")
        tables_loaded = sem("tables_loaded")
        f_loaded = sem("f_loaded")
        f_consts = sem("f_consts")
        f_prepared = sem("f_prepared")
        x2_stored = [[sem(f"x2_stored{n}{g}") for g in range(GROUPS)] for n in range(2)]
        zeroed = sem("zeroed")
        consts_ready = sem("consts_ready")
        wqkv_hi_ready = sem("wqkv_hi_ready")
        wqkv_ready = sem("wqkv_ready")
        wo_hi_ready = sem("wo_hi_ready")
        wo_ready = sem("wo_ready")
        moments_ready = sem("moments_ready")
        var_ready = sem("var_ready")
        rstd_ready = sem("rstd_ready")
        xn_ready = sem("xn_ready")
        x_turned = sem("x_turned")
        xT_hi_ready = sem("xT_hi_ready")
        xT_ready = sem("xT_ready")
        projected = sem("projected")
        qkv_ready = sem("qkv_ready")
        v_hi_ready = sem("v_hi_ready")
        v_ready = sem("v_ready")
        rope_products = sem("rope_products")
        first_cos_ready = sem("first_cos_ready")
        rot_ready = sem("rot_ready")
        qk_turned = sem("qk_turned")
        qk_hi_ready = sem("qk_hi_ready")
        qk_ready = sem("qk_ready")
        scores_done = sem("scores_done")
        max_ready = sem("max_ready")
        probs_ready = sem("probs_ready")
        p_turned = sem("p_turned")
        pT_hi_ready = sem("pT_hi_ready")
        pT_ready = sem("pT_ready")
        attended = sem("attended")
        oT_hi_ready = sem("oT_hi_ready")
        oT_ready = sem("oT_ready")
        inv_ready = sem("inv_ready")
        output_done = sem("output_done")
        x_plus_ready = sem("x_plus_ready")
        x2_ready = sem("x2_ready")

        ffn_loads = [(w1_f, w["cn_w1"].rearrange("(c p) n -> p c n", p=P))] + ffn_weight_loads(f, w)

        block = ctx.enter_context(nc.Block())

        def rope_cos(engine, i, t, ready):
            cos = cos_sb[:, i, :].unsqueeze(1).broadcast_to([P, 2 * (NH + 1), HALF])
            engine.tensor_tensor(rope_a[:].rearrange("p (c d) -> p c d", d=HALF),
                                 qkv[t][:, 0:3 * HS].rearrange("p (c d) -> p c d", d=HALF),
                                 cos, ALU.mult).then_inc(ready, 1)

        def split_v(engine, n, i, t):
            engine.tensor_tensor(v_lo[n][:, i, :], qkv[t][:, 3 * HS:4 * HS],
                                 v_hi[n][:, i, :].bitcast(F32), ALU.subtract).then_inc(v_ready, 1)

        @block.sync
        def _(sp):
            def tiles(g):
                return slice(G * g, G * (g + 1))

            sp.dma_start(xt[0][:, tiles(0), :], x_view[0, :, tiles(0), :]).then_inc(x_loaded[0][0], 16)
            sp.dma_start(wqkv_f[:], wqkv.rearrange("(c p) n -> p c n", p=P)).then_inc(wqkv_loaded, 16)
            for dst, src in ((cos_sb, cos_t), (sin_sb, sin_t)):
                sp.dma_start(dst[:], src.rearrange("(i p) n -> p i n", p=P)).then_inc(tables_loaded, 16)
            sp.dma_start(xt[0][:, tiles(1), :], x_view[0, :, tiles(1), :]).then_inc(x_loaded[0][1], 16)
            sp.dma_start(wo_f[:], wo.rearrange("(c p) n -> p c n", p=P)).then_inc(wo_loaded, 16)
            for n, g in ((1, 0), (1, 1)):
                sp.dma_start(xt[n][:, tiles(g), :], x_view[n, :, tiles(g), :]).then_inc(x_loaded[n][g], 16)

            sp.wait_ge(zeroed, 8)
            with nc.allow_non_contiguous_dma(reason="small vectors"):
                for dst, src in ffn_loads:
                    sp.dma_start(dst[:], src).then_inc(f_loaded, 16)

            def store_and_load(b, turn, n):
                for g in range(GROUPS):
                    sp.wait_ge(x2_ready, b * TILES + G * (g + 1))
                    sp.dma_start(x2_view[b, :, tiles(g), :],
                                 xt[n][:, tiles(g), :]).then_inc(x2_stored[n][g], 16)
                    sp.wait_ge(x2_stored[n][g], turn * 16 + 16)
                    sp.dma_start(xt[n][:, tiles(g), :],
                                 x_view[b + 2, :, tiles(g), :]).then_inc(x_loaded[n][g], 16)

            with sp.Fori(0, B // 2 - 1) as pair:
                for n in range(2):
                    store_and_load(pair * 2 + n, pair, n)
            for n in range(2):
                for g in range(GROUPS):
                    sp.wait_ge(x2_stored[n][g], 16 * (B // 2 - 1))

        @block.gpsimd
        def _(pool):
            pool.memset(ident[:], 0.0).then_inc(zeroed, 1)
            pool.memset(ident_b[:], 0.0).then_inc(zeroed, 1)
            pool.memset(mask_b[:], 0.0).then_inc(zeroed, 1)
            pool.memset(minus_half[:], -0.5).then_inc(zeroed, 1)
            pool.memset(f.ones[:], 1.0).then_inc(zeroed, 1)
            pool.memset(f.sign[:, 0:1], -1.0).then_inc(zeroed, 1)
            pool.memset(f.sign[:, 1:2], 1.0).then_inc(zeroed, 1)
            pool.memset(f.b3_f[:], 0.0).then_inc(zeroed, 1)
            pool.wait_ge(zeroed, 8)
            for m in (ident, ident_b):
                pool.affine_select(out=m[:], in_=m[:], compare_op=ALU.not_equal, fill=1.0, base=0,
                                   pattern=[[-1, P]], channel_multiplier=1).then_inc(consts_ready, 1)
            pool.affine_select(out=mask_b[:], in_=mask_b[:], compare_op=ALU.is_ge, fill=MASKED,
                               base=0, pattern=[[-1, P]],
                               channel_multiplier=1).then_inc(consts_ready, 1)
            for s in range(2):
                pool.affine_select(out=f.sign[:, s:s + 1], in_=f.sign[:, s:s + 1],
                                   compare_op=ALU.is_gt, fill=1.0 - 2.0 * s, base=BLOCK,
                                   pattern=[[0, 1]], channel_multiplier=-1).then_inc(f_consts, 1)

            def do(b, half, parity):
                for kind, ahead, rest in batch_steps("gpsimd", b):
                    bb, n = b + ahead, (parity + ahead) % 2
                    if kind == "norm":
                        g, = rest
                        group = bb * GROUPS + g
                        pool.wait_ge(var_ready, group + 1)
                        pool.tensor_tensor(rstd[g][:], var_eps[g][:],
                                           minus_half[:].to_broadcast([P, G]),
                                           ALU.pow).then_inc(rstd_ready, 1)
                    if kind == "project":
                        g, t = rest
                        i = G * g + t
                        tile = bb * TILES + i
                        if isinstance(b, int) and b < 0 and g == t == 0:
                            pool.wait_ge(tables_loaded, 32)
                        pool.wait_ge(qkv_ready, tile + 1)
                        at_least(pool, rot_ready, tile)
                        first = isinstance(bb, int) and bb == g == 0
                        if not first:
                            rope_cos(pool, i, t, rope_products)
                        qk = qkv[t][:, 0:3 * HS].rearrange("p (c e d) -> p c e d", e=2, d=HALF)
                        sin = sin_sb[:, i, :].unsqueeze(1).broadcast_to([P, NH + 1, HS])
                        pool.tensor_tensor(
                            rope_b[:].rearrange("p (c e d) -> p c e d", e=2, d=HALF),
                            qk[:, :, ::-1, :],
                            sin.rearrange("p c (e d) -> p c e d", e=2),
                            ALU.mult).then_inc(rope_products, 2 if first else 1)
                        if not first:
                            pool.wait_ge(v_hi_ready, tile + 1)
                            split_v(pool, n, i, t)
                        pool.wait_ge(rope_products, (tile + 1) * 2)
                        if first:
                            pool.wait_ge(first_cos_ready, tile + 1)
                        at_least(pool, qk_turned, (bb * GROUPS + g) * (NH + 1))
                        pool.tensor_tensor(rot[:, t, :], rope_a[:], rope_b[:],
                                           ALU.add).then_inc(rot_ready, 1)

            walk_batches(pool, do)
            ffn_rstd(pool, f, 0, 0)

        @block.scalar
        def _(act):
            def copy(out, in_):
                return nc.scalar.activation(out, in_, ACT.Copy)

            act.wait_ge(wqkv_loaded, 16)
            copy(wqkv_hi[:], wqkv_f[:]).then_inc(wqkv_hi_ready, 1)

            def do(b, half, parity):
                for kind, ahead, rest in batch_steps("scalar", b):
                    bb, n = b + ahead, (parity + ahead) % 2
                    ps = bank[BANK_OF[(kind, *rest)]] if kind in BANK_USERS else None
                    if kind == "turn_x":
                        g, c = rest
                        group = bb * GROUPS + g
                        act.wait_ge(x_turned, group * DC + c + 1)
                        at_least(act, projected, group * G)
                        copy(xnT_hi[:, c, :], ps[:]).then_inc(xT_hi_ready, 1)
                    if kind == "project":
                        g, t = rest
                        tile = bb * TILES + G * g + t
                        act.wait_ge(projected, tile + 1)
                        at_least(act, rot_ready, tile - G + 1)
                        at_least(act, v_ready, tile - G + 1)
                        copy(qkv[t][:], ps[:]).then_inc(qkv_ready, 1)
                    if kind == "turn_qk":
                        g, c = rest
                        if isinstance(b, int) and b < 0 and g == c == 0:
                            act.wait_ge(wo_loaded, 16)
                            copy(wo_hi[:], wo_f[:]).then_inc(wo_hi_ready, 1)
                        group = bb * GROUPS + g
                        act.wait_ge(qk_turned, group * (NH + 1) + c + 1)
                        at_least(act, scores_done,
                                 (bb - 1) * BATCH_SCORES + NH * G * (g + 1))
                        out = q_hi[g][c][:] if c < NH else k_hi[n][:, g * G * P:(g + 1) * G * P]
                        copy(out, ps[:]).then_inc(qk_hi_ready, 1)
                    if kind == "scores":
                        u, k = rest
                        g, h = UNITS[u]
                        keys = (G * g + k + 1) * P
                        s = bb * BATCH_SCORES + u * G + k
                        act.wait_ge(max_ready, s + 1)
                        if k == 0:
                            before = (u - 2) % len(UNITS)
                            at_least(act, p_turned, (bb - (u < 2)) * BATCH_STEPS
                                     + FIRST_STEP[before] + STEPS[before])
                        nc.scalar.activation(probs[u % 2][:, k, 0:keys], scores_ps[k % 2][:, 0:keys],
                                             ACT.Exp, bias=neg_max[:, u * G + k:u * G + k + 1],
                                             accum_out=row_sum[n][:, u * G + k:u * G + k + 1]
                                             ).then_inc(probs_ready, 1)
                    if kind == "turn_p":
                        u, j = rest
                        m = bb * BATCH_STEPS + FIRST_STEP[u] + j
                        skip = max(0, j - G * UNITS[u][0]) * P
                        r = (FIRST_STEP[u] + j) % PT_RING
                        act.wait_ge(p_turned, m + 1)
                        at_least(act, attended, m - PT_RING + 1)
                        copy(pT_hi[r][:, skip:], ps[:, skip:]).then_inc(pT_hi_ready, 1)
                    if kind == "close":
                        u, = rest
                        g, h = UNITS[u]
                        act.wait_ge(attended, bb * BATCH_STEPS + FIRST_STEP[u] + STEPS[u])
                        at_least(act, output_done, bb * TILES + G * g)
                        copy(oT_hi[h][:], oT_ps[:]).then_inc(oT_hi_ready, 1)

            walk_batches(act, do)

        @block.vector
        def _(dve):
            def low(out, whole, hi):
                return dve.tensor_tensor(out, whole, hi.bitcast(F32), ALU.subtract)

            first_tiles = [f.x_all[:, t, :] for t in range(G)]

            def prepare_output_and_ffn_weights():
                dve.wait_ge(wo_hi_ready, 1)
                low(wo_lo[:], wo_f[:], wo_hi[:]).then_inc(wo_ready, 1)
                dve.wait_ge(f_loaded, 16 * len(ffn_loads))
                dve.wait_ge(f_consts, 2)
                dve.wait_ge(consts_ready, 3)
                dve.tensor_copy(f.w1_hi[0][:], w1_f[:]).then_inc(f_prepared, 1)
                dve.tensor_copy(f.b3_parts[:], f.b3_f[:]).then_inc(f_prepared, 1)
                dve.tensor_copy(f.ones_r[:], f.ones[:]).then_inc(f_prepared, 1)
                dve.wait_ge(f_prepared, 3)
                dve.tensor_tensor(f.w1_lo[0][:], w1_f[:], f.w1_hi[0][:].bitcast(F32),
                                  ALU.subtract).then_inc(f_prepared, 1)
                last_row = f.b3_parts[BIAS_ROWS - 1:, :]
                dve.tensor_tensor(last_row, f.b3_f[BIAS_ROWS - 1:, :], last_row.bitcast(F32),
                                  ALU.subtract).then_inc(f_prepared, 1)
                dve.wait_ge(f_prepared, 5)
                for dst, src in ((f.w1_hi[1], f.w1_hi[0]), (f.w1_lo[1], f.w1_lo[0])):
                    for k in range(DC):
                        dve.tensor_scalar(dst[:, k, :], src[:, DC - 1 - k, :].bitcast(F32),
                                          f.sign[:, k:k + 1], None, ALU.mult).then_inc(f_prepared, 1)
                for dst, src, by in ((f.b4_half, f.b4_f, 0.5), (f.gb3_half, f.gb3_f, 0.5),
                                     (f.range_token, f.range_f, 0.3), (f.range_global, f.range_f, 0.7)):
                    dve.tensor_scalar(dst[:], src[:], by, None, ALU.mult).then_inc(f_prepared, 1)

                dve.wait_ge(f_prepared, 13)

            def do(b, half, parity):
                if isinstance(b, int) and b == B - 1:
                    dve.wait_ge(x2_ready, (B - IN_PLACE) * TILES + G)
                    ffn_moments(dve, f, 0, 0, first_tiles)
                for kind, ahead, rest in batch_steps("vector", b):
                    bb, n = b + ahead, (parity + ahead) % 2
                    ps = bank[BANK_OF[(kind, *rest)]] if kind in BANK_USERS else None
                    if kind == "norm":
                        g, = rest
                        group = bb * GROUPS + g
                        turn = half + (parity + ahead) // 2
                        dve.wait_ge(x_loaded[n][g], turn * 16 + 16)
                        at_least(dve, moments_ready, group * G)
                        at_least(dve, xn_ready, (group - GROUPS + 1) * G)
                        for t in range(G):
                            dve.bn_stats(stats[:, t, :], xt[n][:, G * g + t, :])
                        dve.drain()
                        for t in range(G):
                            dve.bn_aggr(moments[g][:, t, :], stats[:, t, :]).then_inc(moments_ready, 1)
                        dve.wait_ge(moments_ready, (group + 1) * G)
                        dve.tensor_scalar(var_eps[g][:], moments[g][:, :, 1], EPS, None,
                                          ALU.add).then_inc(var_ready, 1)
                    if kind == "scale":
                        g, = rest
                        group = bb * GROUPS + g
                        dve.wait_ge(rstd_ready, group + 1)
                        at_least(dve, x_turned, (group - GROUPS + 1) * DC)
                        for t in range(G):
                            dve.tensor_scalar(xn[g][:, t, :], xt[n][:, G * g + t, :],
                                              moments[g][:, t, 0:1], rstd[g][:, t:t + 1],
                                              ALU.subtract, ALU.mult).then_inc(xn_ready, 1)
                    if kind == "turn_x":
                        g, c = rest
                        if isinstance(b, int) and b < 0 and g == c == 0:
                            dve.wait_ge(wqkv_hi_ready, 1)
                            low(wqkv_lo[:], wqkv_f[:], wqkv_hi[:]).then_inc(wqkv_ready, 1)
                        dve.wait_ge(xT_hi_ready, (bb * GROUPS + g) * DC + c + 1)
                        low(xnT_lo[:, c, :], ps[:], xnT_hi[:, c, :]).then_inc(xT_ready, 1)
                    if kind == "project":
                        g, t = rest
                        i = G * g + t
                        dve.wait_ge(qkv_ready, bb * TILES + i + 1)
                        dve.tensor_copy(v_hi[n][:, i, :], qkv[t][:, 3 * HS:]).then_inc(v_hi_ready, 1)
                        if isinstance(bb, int) and bb == g == 0:
                            if i == 0:
                                dve.wait_ge(tables_loaded, 32)
                            at_least(dve, rot_ready, i)
                            rope_cos(dve, i, t, first_cos_ready)
                            dve.wait_ge(v_hi_ready, i + 1)
                            split_v(dve, n, i, t)
                    if kind == "turn_qk":
                        g, c = rest
                        if isinstance(b, int) and b < 0 and g == c == 0:
                            prepare_output_and_ffn_weights()
                        dve.wait_ge(qk_hi_ready, (bb * GROUPS + g) * (NH + 1) + c + 1)
                        cols = slice(g * G * P, (g + 1) * G * P)
                        lo, hi = ((q_lo[g][c][:], q_hi[g][c][:]) if c < NH
                                  else (k_lo[n][:, cols], k_hi[n][:, cols]))
                        low(lo, ps[:], hi).then_inc(qk_ready, 1)
                    if kind == "scores":
                        u, k = rest
                        keys = (G * UNITS[u][0] + k + 1) * P
                        dve.wait_ge(scores_done, bb * BATCH_SCORES + u * G + k + 1)
                        dve.tensor_reduce(neg_max[:, u * G + k:u * G + k + 1],
                                          scores_ps[k % 2][:, 0:keys], AX_X, ALU.max,
                                          negate=True).then_inc(max_ready, 1)
                    if kind == "turn_p":
                        u, j = rest
                        if isinstance(b, int) and b == B and j == G:
                            ffn_scale(dve, f, 0, 0, f.first_x0, first_tiles)
                        m = bb * BATCH_STEPS + FIRST_STEP[u] + j
                        skip = max(0, j - G * UNITS[u][0]) * P
                        r = (FIRST_STEP[u] + j) % PT_RING
                        dve.wait_ge(pT_hi_ready, m + 1)
                        low(pT_lo[r][:, skip:], ps[:, skip:],
                            pT_hi[r][:, skip:]).then_inc(pT_ready, 1)
                    if kind == "close":
                        u, = rest
                        h = UNITS[u][1]
                        dve.wait_ge(oT_hi_ready, bb * len(UNITS) + u + 1)
                        low(oT_lo[h][:], oT_ps[:], oT_hi[h][:]).then_inc(oT_ready, 1)
                    if kind == "output":
                        g, t = rest
                        i = G * g + t
                        tile = bb * TILES + i
                        if t == 0:
                            dve.wait_ge(probs_ready, bb * BATCH_SCORES + NH * G * (g + 1))
                            at_least(dve, x2_ready, tile)
                            dve.reciprocal(inv_sum[:], row_sum[n][:, NH * G * g:NH * G * (g + 1)]
                                           ).then_inc(inv_ready, 1)
                            dve.wait_ge(inv_ready, bb * GROUPS + g + 1)
                        dve.wait_ge(output_done, tile + 1)
                        at_least(dve, x2_ready, tile)
                        dve.scalar_tensor_tensor(out=x_plus[:], in0=ps[:, 0:D],
                                                 scalar=inv_sum[:, t:t + 1], in1=xt[n][:, i, :],
                                                 op0=ALU.mult, op1=ALU.add).then_inc(x_plus_ready, 1)
                        dve.wait_ge(x_plus_ready, tile + 1)
                        dve.scalar_tensor_tensor(out=xt[n][:, i, :], in0=ps[:, D:2 * D],
                                                 scalar=inv_sum[:, G + t:G + t + 1], in1=x_plus[:],
                                                 op0=ALU.mult, op1=ALU.add).then_inc(x2_ready, 1)

            walk_batches(dve, do)

        @block.tensor
        def _(pe):
            def split_product(out, stationary, moving, first=True, last=True):
                nc.tensor.matmul(out, stationary[0], moving[0], start=first, stop=False)
                nc.tensor.matmul(out, stationary[0], moving[1], start=False, stop=False)
                return nc.tensor.matmul(out, stationary[1], moving[0], start=False, stop=last)

            pe.wait_ge(consts_ready, 3)

            def reader_of(b, kind, ahead, *rest):
                bb = b + ahead
                if kind == "turn_x":
                    return xT_ready, (bb * GROUPS + rest[0]) * DC + rest[1] + 1
                if kind == "project":
                    return qkv_ready, bb * TILES + G * rest[0] + rest[1] + 1
                if kind == "turn_qk":
                    return qk_ready, (bb * GROUPS + rest[0]) * (NH + 1) + rest[1] + 1
                if kind == "turn_p":
                    return pT_ready, bb * BATCH_STEPS + FIRST_STEP[rest[0]] + rest[1] + 1
                return x2_ready, bb * TILES + G * rest[0] + rest[1] + 1

            user = [None] * BANKS

            def take(before):
                if before is not None:
                    pe.wait_ge(*reader_of(before[0], *before[1]))

            def do(b, half, parity):
                if not isinstance(b, int) or b == B - 1:
                    for n, step in LAST_USERS.items():
                        user[n] = b - 1, step
                for kind, ahead, rest in batch_steps("tensor", b):
                    bb, n = b + ahead, (parity + ahead) % 2
                    if kind in BANK_USERS:
                        n_bank = BANK_OF[(kind, *rest)]
                        ps = bank[n_bank]
                        before, user[n_bank] = user[n_bank], (b, (kind, ahead, *rest))
                    if kind == "turn_x":
                        g, c = rest
                        group = bb * GROUPS + g
                        pe.wait_ge(xn_ready, (group + 1) * G)
                        take(before)
                        for t in range(G):
                            mm = nc.tensor.transpose(ps[:, t * P:(t + 1) * P],
                                                     xn[g][:, t, c * P:(c + 1) * P], ident[:])
                        mm.then_inc(x_turned, 1)
                    if kind == "project":
                        g, t = rest
                        tile = bb * TILES + G * g + t
                        if isinstance(b, int) and b < 0 and g == t == 0:
                            pe.wait_ge(wqkv_ready, 1)
                        pe.wait_ge(xT_ready, (bb * GROUPS + g + 1) * DC)
                        take(before)
                        for c in range(DC):
                            cols = slice(t * P, (t + 1) * P)
                            mm = split_product(ps[:], (xnT_hi[:, c, cols], xnT_lo[:, c, cols]),
                                               (wqkv_hi[:, c, :], wqkv_lo[:, c, :]),
                                               c == 0, c == DC - 1)
                        mm.then_inc(projected, 1)
                    if kind == "turn_qk":
                        g, c = rest
                        group = bb * GROUPS + g
                        pe.wait_ge(rot_ready, (group + 1) * G)
                        take(before)
                        for t in range(G):
                            mm = nc.tensor.transpose(ps[:, t * P:(t + 1) * P],
                                                     rot[:, t, c * HS:(c + 1) * HS], ident[:])
                        mm.then_inc(qk_turned, 1)
                    if kind == "scores":
                        u, k = rest
                        g, h = UNITS[u]
                        keys = (G * g + k + 1) * P
                        s = bb * BATCH_SCORES + u * G + k
                        pe.wait_ge(qk_ready, (bb * GROUPS + g + 1) * (NH + 1))
                        at_least(pe, probs_ready, s - 1)
                        tile = slice(k * P, (k + 1) * P)
                        ps = scores_ps[k % 2]
                        for at in range(0, keys, G * P):
                            cols = slice(at, min(at + G * P, keys))
                            mm = split_product(ps[:, cols], (q_hi[g][h][:, tile], q_lo[g][h][:, tile]),
                                               (k_hi[n][:, cols], k_lo[n][:, cols]),
                                               last=cols.stop < keys)
                        mm = nc.tensor.matmul(ps[:, keys - P:keys], ident_b[:], mask_b[:],
                                              start=False, stop=True)
                        mm.then_inc(scores_done, 1)
                    if kind == "attend":
                        u, j = rest
                        attend(bb, n, u, j)
                    if kind == "turn_p":
                        take(before)
                        turn_p(ps, bb, *rest)
                    if kind == "output":
                        g, t = rest
                        if isinstance(bb, int) and bb == 0 and g == 0 and t == 0:
                            pe.wait_ge(wo_ready, 1)
                        pe.wait_ge(oT_ready, bb * len(UNITS) + NH * (g + 1))
                        take(before)
                        for h in range(NH):
                            cols = slice(t * P, (t + 1) * P)
                            mm = split_product(ps[:, h * D:(h + 1) * D],
                                               (oT_hi[h][:, cols], oT_lo[h][:, cols]),
                                               (wo_hi[:, h, :], wo_lo[:, h, :]))
                        mm.then_inc(output_done, 1)

            def turn_p(ps, bb, u, j):
                m = bb * BATCH_STEPS + FIRST_STEP[u] + j
                g = UNITS[u][0]
                pe.wait_ge(probs_ready, bb * BATCH_SCORES + (u + 1) * G)
                for k in range(max(0, j - G * g), G):
                    mm = nc.tensor.transpose(ps[:, k * P:(k + 1) * P],
                                             probs[u % 2][:, k, j * P:(j + 1) * P], ident[:])
                mm.then_inc(p_turned, 1)

            def attend(bb, n, u, j):
                m = bb * BATCH_STEPS + FIRST_STEP[u] + j
                skip = max(0, j - G * UNITS[u][0]) * P
                r = (FIRST_STEP[u] + j) % PT_RING
                pe.wait_ge(pT_ready, m + 1)
                if j == 0:
                    at_least(pe, oT_ready, bb * len(UNITS) + u)
                    pe.wait_ge(v_ready, bb * TILES + STEPS[u])
                split_product(oT_ps[:, skip:], (v_hi[n][:, j, :], v_lo[n][:, j, :]),
                              (pT_hi[r][:, skip:], pT_lo[r][:, skip:]),
                              j == 0, j == STEPS[u] - 1).then_inc(attended, 1)

            walk_batches(pe, do)


NGROUPS = B * GROUPS

PERIODS = {
    "tensor": [
        ("product", -1, 0), ("global", -1, 2), ("product", -1, 1), ("spread", -2, 1),
        ("spread", -3, 2), ("product", -1, 2), ("h2", -1, 0), ("product", -1, 3), ("h3", -1, 0),
        ("h2", -2, 1), ("h2", -3, 2), ("turn", 0, 0), ("turn", 0, 1), ("h3", -2, 1),
        ("global", 0, 0), ("h3", -3, 2), ("global", 0, 1),
    ],
    "scalar": [
        ("product", -1, 3), ("h3", -1, 0), ("h2", -2, 1), ("h2", -3, 2), ("turn", 0, 0),
        ("turn", 0, 1), ("global", 0, 0), ("h3", -2, 1), ("h3", -3, 2), ("global", 0, 1),
        ("squash", -2, 1), ("squash", -1, 0), ("global", 0, 2), ("squash", -3, 2),
        ("product", 0, 0), ("product", 0, 1), ("gelu1", 0, 0), ("h2", 0, 0), ("gelu1", -1, 1),
        ("product", 0, 2), ("gelu1", -2, 2),
    ],
    "vector": [
        ("scale", 0), ("stats", 1), ("turn", 0, 0), ("turn", 0, 1), ("dot", -2, 1), ("dot", -1, 0),
        ("dot", -3, 2), ("squash", -2, 1), ("global", 0, 2), ("squash", -1, 0), ("squash", -3, 2),
        ("mix", -1, 1), ("mix", -2, 2), ("final", -3, 0), ("final", -3, 1), ("final", -3, 2),
        ("final", -3, 3),
    ],
    "gpsimd": [
        ("dot", -1, 0), ("stats", 1), ("dot", -2, 1), ("dot", -3, 2), ("mix", -1, 1),
        ("mix", -2, 2),
    ],
}
AHEAD = max(step[1] for steps in PERIODS.values() for step in steps)
BEHIND = -min(step[1] for steps in PERIODS.values() for step in steps)


def period_steps(engine_name, n, r):
    for kind, ahead, *rest in PERIODS[engine_name]:
        if isinstance(n, int) and not 0 <= n + ahead < NGROUPS:
            continue
        if kind in ("stats", "scale") and isinstance(n, int) and n + ahead == 0:
            continue
        if kind == "global" and (r + ahead) % GROUPS != GROUPS - 1:
            continue
        yield kind, ahead, rest


def walk_periods(engine, do):
    for n in range(-AHEAD, SLOTS):
        do(n, n // SLOTS, n % SLOTS)
    with engine.Fori(1, NGROUPS // SLOTS - 1) as turn:
        for r in range(SLOTS):
            do(turn * SLOTS + r, turn, r)
    for n in range(NGROUPS - SLOTS, NGROUPS + BEHIND):
        do(n, n // SLOTS, n % SLOTS)


def batch_of(turn, r, ahead):
    return (turn + (r + ahead) // SLOTS) * (SLOTS // GROUPS) + (r + ahead) % SLOTS // GROUPS


def ffn_phase(nc, f, x2, out):
    x2_view = x2.rearrange("b (i p) f -> b p i f", p=P)
    out_view = out.rearrange("b (g i p) f -> (b g) p i f", p=P, g=GROUPS)
    x_all = f.x_all
    with ExitStack() as ctx:
        def sb(name, shape, dt=F32):
            return ctx.enter_context(nc.sbuf_tensor(name, shape, dt))

        def psum(name, shape):
            return ctx.enter_context(nc.psum_tensor(name, shape, F32))

        def sem(name):
            return ctx.enter_context(nc.semaphore(name))

        def cycle_sems(name):
            return [sem(f"{name}{c}") for c in range(FFN_CYCLES)]

        x0 = [f.first_x0] + [sb(f"x0_{n}", [P, G, D]) for n in range(1, SLOTS)]
        x0T_hi = sb("x0T_hi", [P, DC, G * P], F32R)
        x0T_lo = sb("x0T_lo", [P, DC, G * P], F32R)
        x0_sum = [sb(f"x0_sum{n}", [P, DC]) for n in range(SLOTS)]
        made = [sb(f"made{n}", [P, 2 * DC, G * P]) for n in range(SLOTS)]
        part_a = sb("part_a", [P, DC, G * P])
        part_b = [None] + [sb(f"part_b{c}", [P, DC, G * P]) for c in range(1, FFN_CYCLES)]
        mixed_sb = [None] + [sb(f"mixed{c}", [P, DC, G * P]) for c in range(1, FFN_CYCLES)]
        h1 = [sb(f"h1_{c}", [P, DC, G * P]) for c in range(FFN_CYCLES)]
        h2 = [sb(f"h2_{c}", [P, G * P]) for c in range(FFN_CYCLES)]
        h3 = [sb(f"h3_{c}", [P, G, H3]) for c in range(FFN_CYCLES)]
        h3_w4 = [sb(f"h3_w4_{c}", [P, G, H3]) for c in range(FFN_CYCLES)]
        logit = [sb(f"logit{c}", [P, G]) for c in range(FFN_CYCLES)]
        token_tanh = [sb(f"token_tanh{c}", [P, G]) for c in range(FFN_CYCLES)]
        coupling = [sb(f"coupling{c}", [P, G]) for c in range(FFN_CYCLES)]
        scaled = [sb(f"scaled{c}", [P, 2, G]) for c in range(FFN_CYCLES)]
        state = [[sb(f"state{c}_{n}", [P, 2, G]) for n in range(2)] for c in range(FFN_CYCLES)]
        minus_b = sb("minus_b", [P, G])
        gh1 = sb("gh1", [P, 1])
        gh2 = sb("gh2", [H3, 1])
        global_tanh = sb("global_tanh", [P, 1])
        base_coupling = [sb(f"base_coupling{n}", [P, 1]) for n in range(2)]
        y_part = sb("y_part", [P, D])

        made_ps = [psum(f"made_ps{n}", [P, G * P]) for n in range(3)]
        cycle_ps = [psum(f"cycle_ps{c}", [P, G * P]) for c in range(FFN_CYCLES)]
        spread_a_ps = psum("spread_a_ps", [P, G * P])
        global_ps = psum("global_ps", [P, G * P])

        x2_loaded = [sem(f"x2_loaded{n}") for n in range(2)]
        x0_turned = sem("x0_turned")
        x0T_hi_ready = sem("x0T_hi_ready")
        x0T_ready = sem("x0T_ready")
        made_done = sem("made_done")
        made_ready = sem("made_ready")
        global_done = sem("global_done")
        global_act = sem("global_act")
        base_ready = sem("base_ready")
        spread_done = cycle_sems("spread_done")
        parts_ready = cycle_sems("parts_ready")
        mix_ready = cycle_sems("mix_ready")
        h1_ready = cycle_sems("h1_ready")
        h2_done = cycle_sems("h2_done")
        h2_ready = cycle_sems("h2_ready")
        h3_done = cycle_sems("h3_done")
        h3_ready = cycle_sems("h3_ready")
        h3_w4_ready = cycle_sems("h3_w4_ready")
        logit_ready = cycle_sems("logit_ready")
        tanh_ready = cycle_sems("tanh_ready")
        coupling_ready = cycle_sems("coupling_ready")
        scaled_ready = cycle_sems("scaled_ready")
        state_ready = cycle_sems("state_ready")
        minus_b_ready = sem("minus_b_ready")
        y_part_ready = sem("y_part_ready")
        y_ready = sem("y_ready")
        y_stored = sem("y_stored")

        block = ctx.enter_context(nc.Block())

        @block.sync
        def _(sp):
            for n in range(IN_PLACE, B):
                at_least(sp, x2_loaded[n % 2], 16 * (n // 2 - 1))
                sp.dma_start(x_all[:, n * TILES:(n + 1) * TILES, :],
                             x2_view[n - IN_PLACE]).then_inc(x2_loaded[n % 2], 16)

            def store(m, to):
                sp.wait_ge(y_ready, m * (2 * G) + 2 * G)
                sp.dma_start(out_view[to], x_all[:, rows(m), :]).then_inc(y_stored, 16)

            def rows(m):
                return slice(m * G, m * G + G) if isinstance(m, int) else bass.ds(m * G, G)

            first = IN_PLACE * GROUPS
            for m in range(first):
                store(m, NGROUPS - first + m)
            with sp.Fori(0, NGROUPS - first) as to:
                store(to + first, to)
            sp.wait_ge(y_stored, 16 * NGROUPS)

        @block.gpsimd
        def _(pool):
            def do(n, turn, r):
                for kind, ahead, rest in period_steps("gpsimd", n, r):
                    m, slot = n + ahead, (r + ahead) % SLOTS
                    if kind == "stats":
                        ffn_rstd(pool, f, m, slot)
                    if kind == "mix":
                        c, = rest
                        pool.wait_ge(parts_ready[c], (m + 1) * c)
                        at_least(pool, h1_ready[c], m * DC)
                        other = made[slot][:, 0:DC, :] if c == 1 else part_a[:]
                        pool.tensor_tensor(mixed_sb[c][:], part_b[c][:], other,
                                           ALU.add).then_inc(mix_ready[c], 1)
                    if kind == "dot":
                        c, = rest
                        pool.wait_ge(h3_ready[c], m + 1)
                        at_least(pool, logit_ready[c], m)
                        pool.tensor_tensor(h3_w4[c][:], h3[c][:],
                                           f.w4_sb[:].unsqueeze(1).broadcast_to([P, G, H3]),
                                           ALU.mult).then_inc(h3_w4_ready[c], 1)

            walk_periods(pool, do)

        @block.scalar
        def _(act):
            def do(n, turn, r):
                for kind, ahead, rest in period_steps("scalar", n, r):
                    m, slot = n + ahead, (r + ahead) % SLOTS
                    if kind == "turn":
                        c, = rest
                        act.wait_ge(x0_turned, m * DC + c + 1)
                        at_least(act, made_done, m * (2 * DC))
                        nc.scalar.activation(x0T_hi[:, c, :], made_ps[c][:], ACT.Copy,
                                             accum_out=x0_sum[slot][:, c:c + 1]
                                             ).then_inc(x0T_hi_ready, 1)
                    if kind == "product":
                        e, = rest
                        act.wait_ge(made_done, m * (2 * DC) + e + 1)
                        at_least(act, mix_ready[FFN_CYCLES - 1], m - SLOTS + 1)
                        nc.scalar.activation(made[slot][:, e, :], made_ps[(DC + e) % 3][:],
                                             ACT.Copy).then_inc(made_ready, 1)
                    if kind == "global":
                        s, = rest
                        batch = batch_of(turn, r, ahead)
                        act.wait_ge(global_done, batch * 3 + s + 1)
                        if s == 0:
                            nc.scalar.activation(gh1[:], global_ps[:, 0:1], ACT.Gelu,
                                                 bias=f.gb1_sb[:], scale=1.0 / T).then_inc(global_act, 1)
                        elif s == 1:
                            nc.scalar.activation(gh2[:], global_ps[0:H3, 1:2], ACT.Gelu,
                                                 bias=f.gb2_sb[:]).then_inc(global_act, 1)
                        else:
                            at_least(act, base_ready, batch)
                            nc.scalar.activation(global_tanh[:], global_ps[:, 2:3], ACT.Tanh,
                                                 bias=f.gb3_half[:], scale=0.5).then_inc(global_act, 1)
                    if kind == "gelu1":
                        c, = rest
                        if c == 0:
                            act.wait_ge(made_ready, m * (2 * DC) + DC)
                        else:
                            act.wait_ge(mix_ready[c], m + 1)
                        at_least(act, h2_done[c], m)
                        for k in range(DC):
                            src = made[slot][:, k, :] if c == 0 else mixed_sb[c][:, k, :]
                            nc.scalar.activation(h1[c][:, k, :], src, ACT.Gelu,
                                                 bias=f.b1_sb[:, k:k + 1]).then_inc(h1_ready[c], 1)
                    if kind == "h2":
                        c, = rest
                        act.wait_ge(h2_done[c], m + 1)
                        at_least(act, h3_done[c], m)
                        nc.scalar.activation(h2[c][:], cycle_ps[c][:], ACT.Gelu,
                                             bias=f.b2_sb[:]).then_inc(h2_ready[c], 1)
                    if kind == "h3":
                        c, = rest
                        act.wait_ge(h3_done[c], m + 1)
                        at_least(act, h3_w4_ready[c], m)
                        nc.scalar.activation(h3[c][:].rearrange("p t k -> p (t k)"),
                                             cycle_ps[c][:, 0:G * H3],
                                             ACT.Gelu).then_inc(h3_ready[c], 1)
                    if kind == "squash":
                        c, = rest
                        act.wait_ge(logit_ready[c], m + 1)
                        at_least(act, coupling_ready[c], m)
                        nc.scalar.activation(token_tanh[c][:], logit[c][:], ACT.Tanh,
                                             bias=f.b4_half[:], scale=0.5).then_inc(tanh_ready[c], 1)

            walk_periods(act, do)

        @block.vector
        def _(dve):
            def do(n, turn, r):
                for kind, ahead, rest in period_steps("vector", n, r):
                    m, slot = n + ahead, (r + ahead) % SLOTS
                    if kind == "stats":
                        batch_parity = slot // 2
                        at_least(dve, x2_loaded[batch_parity], (turn + (r + ahead) // SLOTS) * 16)
                        ffn_moments(dve, f, m, slot, [x_tile(m, t) for t in range(G)])
                    if kind == "scale":
                        at_least(dve, x0_turned, (m - SLOTS + 1) * DC)
                        at_least(dve, y_ready, (m - SLOTS + 1) * (2 * G))
                        ffn_scale(dve, f, m, slot, x0[slot], [x_tile(m, t) for t in range(G)])
                    if kind == "turn":
                        c, = rest
                        dve.wait_ge(x0T_hi_ready, m * DC + c + 1)
                        dve.tensor_tensor(x0T_lo[:, c, :], made_ps[c][:], x0T_hi[:, c, :].bitcast(F32),
                                          ALU.subtract).then_inc(x0T_ready, 1)
                    if kind == "global" and rest[0] == 2:
                        batch = batch_of(turn, r, ahead)
                        dve.wait_ge(global_act, batch * 3 + 3)
                        dve.tensor_scalar(base_coupling[slot // 2][:], global_tanh[:],
                                          f.range_global[:], 0.1, ALU.mult,
                                          ALU.add).then_inc(base_ready, 1)
                    if kind == "mix":
                        c, = rest
                        dve.wait_ge(spread_done[c], m + 1)
                        at_least(dve, mix_ready[c], m)
                        if c == FFN_CYCLES - 1:
                            dve.tensor_tensor(part_a[:],
                                              spread_a_ps[:].unsqueeze(1).broadcast_to([P, DC, G * P]),
                                              made[slot][:, 0:DC, :], ALU.mult).then_inc(parts_ready[c], 1)
                        dve.tensor_tensor(part_b[c][:],
                                          cycle_ps[c][:].unsqueeze(1).broadcast_to([P, DC, G * P]),
                                          made[slot][:, DC:, :], ALU.mult).then_inc(parts_ready[c], 1)
                    if kind == "dot":
                        c, = rest
                        dve.wait_ge(h3_w4_ready[c], m + 1)
                        at_least(dve, tanh_ready[c], m)
                        dve.tensor_reduce(logit[c][:], h3_w4[c][:], AX_X, ALU.add).then_inc(logit_ready[c], 1)
                    if kind == "squash":
                        c, = rest
                        if c == 0:
                            dve.wait_ge(base_ready, batch_of(turn, r, ahead) + 1)
                        update_state(c, m, slot)
                    if kind == "final":
                        t, = rest
                        a_b = state[FFN_CYCLES - 1][slot % 2]
                        if t == 0:
                            dve.wait_ge(minus_b_ready, m + 1)
                        at_least(dve, y_ready, (m * G + t) * 2)
                        dve.scalar_tensor_tensor(out=y_part[:], in0=x0[slot][:, t, :],
                                                 scalar=a_b[:, 0, t:t + 1], in1=x_tile(m, t),
                                                 op0=ALU.mult, op1=ALU.add).then_inc(y_part_ready, 1)
                        dve.wait_ge(y_part_ready, m * G + t + 1)
                        y = x_tile(m, t).rearrange("p (k d) -> p k d", d=BLOCK)
                        y_in = y_part[:].rearrange("p (k d) -> p k d", d=BLOCK)
                        source = x0[slot][:, t, :].rearrange("p (k d) -> p k d", d=BLOCK)
                        dve.scalar_tensor_tensor(out=y[:, 0:4:3, :], in0=source[:, 2:0:-1, :],
                                                 scalar=a_b[:, 1, t:t + 1], in1=y_in[:, 0:4:3, :],
                                                 op0=ALU.mult, op1=ALU.add).then_inc(y_ready, 1)
                        dve.scalar_tensor_tensor(out=y[:, 1:3, :], in0=source[:, 3::-3, :],
                                                 scalar=minus_b[:, t:t + 1], in1=y_in[:, 1:3, :],
                                                 op0=ALU.mult, op1=ALU.add).then_inc(y_ready, 1)

            def x_tile(m, t):
                if isinstance(m, int):
                    return x_all[:, m * G + t, :]
                return x_all[:, bass.ds(m * G + t, 1), :].rearrange("p a f -> p (a f)")

            def update_state(c, m, slot):
                new = state[c][slot % 2]
                old = state[c - 1][slot % 2]
                dve.wait_ge(tanh_ready[c], m + 1)
                if c == 0:
                    at_least(dve, spread_done[1], m - 1)
                    at_least(dve, coupling_ready[0], m)
                    dve.tensor_scalar(new[:, 1, :], token_tanh[c][:], f.range_token[:],
                                      base_coupling[slot // 2][:], ALU.mult,
                                      ALU.add).then_inc(coupling_ready[0], 1)
                    return
                at_least(dve, state_ready[c], m * 2)
                dve.tensor_scalar(coupling[c][:], token_tanh[c][:], f.range_token[:],
                                  base_coupling[slot // 2][:], ALU.mult,
                                  ALU.add).then_inc(coupling_ready[c], 1)
                dve.wait_ge(coupling_ready[c], m + 1)
                if c == 1:
                    dve.wait_ge(coupling_ready[0], m + 1)
                    dve.tensor_tensor(scaled[c][:, 0, :], old[:, 1, :], coupling[c][:],
                                      ALU.mult).then_inc(scaled_ready[c], 1)
                    dve.wait_ge(scaled_ready[c], m + 1)
                    at_least(dve, spread_done[2], m - 1)
                    dve.tensor_tensor(new[:, 1, :], old[:, 1, :], coupling[c][:],
                                      ALU.add).then_inc(state_ready[c], 1)
                    dve.tensor_scalar(new[:, 0, :], scaled[c][:, 0, :], -1.0, 1.0, ALU.mult,
                                      ALU.add).then_inc(state_ready[c], 1)
                    return
                dve.wait_ge(state_ready[1], m * 2 + 2)
                dve.tensor_tensor(scaled[c][:], old[:],
                                  coupling[c][:].unsqueeze(1).broadcast_to([P, 2, G]),
                                  ALU.mult).then_inc(scaled_ready[c], 1)
                dve.wait_ge(scaled_ready[c], m + 1)
                at_least(dve, y_ready, m * (2 * G))
                dve.tensor_tensor(new[:, 0, :], old[:, 0, :], scaled[c][:, 1, :],
                                  ALU.subtract).then_inc(state_ready[c], 1)
                dve.tensor_tensor(new[:, 1, :], old[:, 1, :], scaled[c][:, 0, :],
                                  ALU.add).then_inc(state_ready[c], 1)
                dve.wait_ge(state_ready[c], m * 2 + 2)
                dve.tensor_scalar(minus_b[:], new[:, 1, :], -1.0, None,
                                  ALU.mult).then_inc(minus_b_ready, 1)

            walk_periods(dve, do)

        @block.tensor
        def _(pe):
            def do(n, turn, r):
                for kind, ahead, rest in period_steps("tensor", n, r):
                    m, slot = n + ahead, (r + ahead) % SLOTS
                    if kind == "turn":
                        c, = rest
                        pe.wait_ge(f.x0_ready, m * G + G)
                        at_least(pe, made_ready, (m - 1) * (2 * DC) + c + 2)
                        for t in range(G):
                            mm = nc.tensor.transpose(made_ps[c][:, t * P:(t + 1) * P],
                                                     x0[slot][:, t, c * P:(c + 1) * P], f.ident[:])
                        mm.then_inc(x0_turned, 1)
                    if kind == "product":
                        e, = rest
                        which, chunk = divmod(e, DC)
                        pe.wait_ge(x0T_ready, m * DC + DC)
                        if e == 0:
                            at_least(pe, made_ready, m * (2 * DC))
                        if e == 3:
                            pe.wait_ge(made_ready, m * (2 * DC) + 1)
                        cols = slice(chunk * P, (chunk + 1) * P)
                        ps = made_ps[(DC + e) % 3]
                        for k in range(DC):
                            hi, lo = f.w1_hi[which][:, k, cols], f.w1_lo[which][:, k, cols]
                            nc.tensor.matmul(ps[:], hi, x0T_hi[:, k, :], start=k == 0, stop=False)
                            nc.tensor.matmul(ps[:], hi, x0T_lo[:, k, :], start=False, stop=False)
                            mm = nc.tensor.matmul(ps[:], lo, x0T_hi[:, k, :], start=False,
                                                  stop=k == DC - 1)
                        mm.then_inc(made_done, 1)
                    if kind == "global":
                        s, = rest
                        batch = batch_of(turn, r, ahead)
                        if s == 0:
                            pe.wait_ge(x0T_hi_ready, m * DC + DC)
                            at_least(pe, global_act, batch * 3)
                            for k in range(DC):
                                for half, of in enumerate(((slot - 1) % SLOTS, slot)):
                                    mm = nc.tensor.matmul(global_ps[:, 0:1], f.gw1_sb[:, k, :],
                                                          x0_sum[of][:, k:k + 1],
                                                          start=k + half == 0, stop=k + half == DC)
                        elif s == 1:
                            pe.wait_ge(global_act, batch * 3 + 1)
                            mm = nc.tensor.matmul(global_ps[0:H3, 1:2], f.gw2_sb[:], gh1[:],
                                                  start=True, stop=True)
                        else:
                            pe.wait_ge(global_act, batch * 3 + 2)
                            mm = nc.tensor.matmul(global_ps[:, 2:3],
                                                  f.gw3_sb[:].to_broadcast([H3, P]), gh2[:],
                                                  start=True, stop=True)
                        mm.then_inc(global_done, 1)
                    if kind == "spread":
                        c, = rest
                        a_b = state[c - 1][slot % 2]
                        if c == 1:
                            pe.wait_ge(coupling_ready[0], m + 1)
                        else:
                            pe.wait_ge(state_ready[c - 1], m * 2 + 2)
                            at_least(pe, parts_ready[c], m * c)
                        at_least(pe, h3_ready[c], m)
                        for which in range(2 if c == 2 else 1):
                            ps = spread_a_ps if c == 2 and which == 0 else cycle_ps[c]
                            part = 0 if ps is spread_a_ps else 1
                            for t in range(G):
                                mm = nc.tensor.transpose(ps[:, t * P:(t + 1) * P],
                                                         a_b[:, part, t:t + 1].to_broadcast([P, P]),
                                                         f.ident[:])
                        mm.then_inc(spread_done[c], 1)
                    if kind == "h2":
                        c, = rest
                        pe.wait_ge(h1_ready[c], m * DC + DC)
                        if c == 0:
                            at_least(pe, h3_ready[c], m)
                        for k in range(DC):
                            mm = nc.tensor.matmul(cycle_ps[c][:], f.w2_sb[:, k, :], h1[c][:, k, :],
                                                  start=k == 0, stop=k == DC - 1)
                        mm.then_inc(h2_done[c], 1)
                    if kind == "h3":
                        c, = rest
                        pe.wait_ge(h2_ready[c], m + 1)
                        ps = cycle_ps[c][:, 0:G * H3]
                        nc.tensor.matmul(ps.rearrange("p (t k) -> p t k", k=H3), f.ones_r[:],
                                         f.b3_parts[:].unsqueeze(1).broadcast_to([BIAS_ROWS, G, H3]),
                                         start=True, stop=False)
                        for t in range(G):
                            mm = nc.tensor.matmul(ps[:, t * H3:(t + 1) * H3],
                                                  h2[c][:, t * P:(t + 1) * P], f.w3_sb[:],
                                                  start=False, stop=t == G - 1)
                        mm.then_inc(h3_done[c], 1)

            walk_periods(pe, do)


def rope_tables():
    import numpy as np
    positions = np.arange(0, HS, 2, dtype=np.float32)
    theta = (np.float32(10000.0) ** (np.float32(-2.0) * positions / np.float32(HS))).astype(np.float32)
    angles = (np.arange(T, dtype=np.float32)[:, None] * theta[None, :]).astype(np.float64)
    scale = HS ** -0.25
    cos, sin = np.cos(angles) * scale, np.sin(angles) * scale
    return cos.astype(np.float32), np.concatenate([-sin, sin], axis=1).astype(np.float32)


WEIGHTS = ["cn_w1", "cn_b1", "cn_w2", "cn_b2", "cn_w3", "cn_b3", "cn_w4", "cn_b4", "gc_w1",
           "gc_b1", "gc_w2", "gc_b2", "gc_w3", "gc_b3", "adaptive_range"]


def kernel(**inputs):
    import numpy as np
    import concourse.bacc as bacc
    from concourse.bass_utils import run_bass_kernel_spmd

    def halves(w):
        return np.concatenate([w[0::2], w[1::2]], axis=0)

    wq, wk, wv = (np.asarray(inputs[f"L0_attn_W{n}"]) for n in "qkv")
    wqkv = np.concatenate([halves(wq[0]), halves(wq[1]), halves(wk), wv], axis=0).T
    cos_t, sin_t = rope_tables()
    arrays = {"x": np.ascontiguousarray(inputs["L0_attn_x"]), "wqkv": np.ascontiguousarray(wqkv),
              "wo": np.ascontiguousarray(np.asarray(inputs["L0_attn_Wo"]).T),
              "cos_t": cos_t, "sin_t": sin_t}
    arrays.update({n: np.ascontiguousarray(inputs[f"L0_ffn_{n}"]) for n in WEIGHTS})
    nc = bacc.Bacc("TRN2", target_bir_lowering=False, num_devices=1)
    ins = {name: nc.dram_tensor(name, a.shape, F32, kind="ExternalInput").ap()
           for name, a in arrays.items()}
    x2 = nc.dram_tensor("x2", (B - IN_PLACE, T, D), F32, kind="Internal").ap()
    out = nc.dram_tensor("out", (B, T, D), F32, kind="ExternalOutput").ap()
    weights = {n: ins[n] for n in WEIGHTS}
    with ExitStack() as ctx:
        f = SharedTensors(nc, ctx)
        attention_phase(nc, f, *(ins[n] for n in ("x", "wqkv", "wo", "cos_t", "sin_t")), weights, x2)
        ffn_phase(nc, f, x2, out)
    r = run_bass_kernel_spmd(nc, [arrays], core_ids=[0])
    return r.results[0]["out"]
```
